# Optimizing a Trainium2 kernel written in Bass

```python
import numpy as np
import jax
import jax.numpy as jnp

def _softmax(x, axis=-1):
    return jax.nn.softmax(x, axis=axis)

def _gelu(x):
    return jax.nn.gelu(x, approximate=True)

def _silu(x):
    return jax.nn.silu(x)

def _sigmoid(x):
    return jax.nn.sigmoid(x)

def _layernorm(x, axis=-1, eps=1e-05):
    m = jnp.mean(x, axis=axis, keepdims=True)
    v = jnp.var(x, axis=axis, keepdims=True)
    return (x - m) / jnp.sqrt(v + eps)

def _scatter_add(tgt, idx, src, axis=0):
    return tgt.at[idx].add(src)

def _segment_sum(src, seg, n):
    return jax.ops.segment_sum(src, seg, n)
kernel_name = 'mk_vit_tower_d2_tok_img768_r4_ec25e6'

def setup_inputs(seed: int=0):
    np.random.seed(seed)
    _w = jnp.asarray

    def _rec_inputs():
        import jax
        import jax.numpy as jnp
        _rk = jax.random.key(seed)
        x = -0.00016672 + 0.999947 * jax.random.normal(jax.random.fold_in(_rk, 1), (16, 3, 96, 96), jnp.float32)
        return x
    x = _rec_inputs()

    def _L0_tok_setup():
        import jax, jax.numpy as jnp
        import numpy as np
        B, C, H, Wd = (64, 3, 96, 96)
        PH = PW = 16
        NH, NW = (H // PH, Wd // PW)
        NP = NH * NW
        PD = C * PH * PW
        ED = 192
        EPS = 1e-05

        def layernorm(x, g, b):
            mu = jnp.mean(x, axis=-1, keepdims=True)
            var = jnp.mean(jnp.square(x - mu), axis=-1, keepdims=True)
            return (x - mu) * jax.lax.rsqrt(var + EPS) * g + b
        key = jax.random.key(seed)
        ks = jax.random.split(key, 6)
        return {'x': jax.random.normal(ks[0], (B, C, H, Wd), dtype=jnp.float32), 'ln1_g': jnp.ones((PD,), jnp.float32), 'ln1_b': jnp.zeros((PD,), jnp.float32), 'W': jax.random.normal(ks[1], (PD, ED), dtype=jnp.float32) * 0.02, 'b': jnp.zeros((ED,), jnp.float32), 'ln2_g': jnp.ones((ED,), jnp.float32), 'ln2_b': jnp.zeros((ED,), jnp.float32), 'cls_token': jax.random.normal(ks[2], (ED,), dtype=jnp.float32), 'pos_embed': jax.random.normal(ks[3], (1, NP + 1, ED), dtype=jnp.float32) * 0.02}
    _L0_tok_all = _L0_tok_setup()
    _L0_tok_in = {k: v for k, v in _L0_tok_all.items() if k in ('ln1_g', 'ln1_b', 'W', 'b', 'ln2_g', 'ln2_b', 'cls_token', 'pos_embed')}
    del _L0_tok_all

    def _L0_attn_setup():
        import jax, jax.numpy as jnp
        import numpy as np
        B, N, E, H = (2, 512, 192, 12)
        D = E // H
        G = 16
        LN_EPS = 1e-05

        def _layernorm(x, w, b):
            mu = jnp.mean(x, axis=-1, keepdims=True)
            var = jnp.mean(jnp.square(x - mu), axis=-1, keepdims=True)
            return (x - mu) * jax.lax.rsqrt(var + LN_EPS) * w + b
        key = jax.random.key(seed)
        ks = jax.random.split(key, 8)
        s = E ** (-0.5)
        x = jax.random.normal(ks[0], (B, N, E), jnp.float32)
        log_slope = -2.0 ** (-8.0 * (jnp.arange(H, dtype=jnp.float32) + 1.0) / H)
        Wq = jax.random.normal(ks[1], (E, E), jnp.float32) * s
        Wk = jax.random.normal(ks[2], (E, E), jnp.float32) * s
        Wv = jax.random.normal(ks[3], (E, E), jnp.float32) * s
        Wo = jax.random.normal(ks[4], (E, E), jnp.float32) * s
        Wg1 = jax.random.normal(ks[5], (E, G), jnp.float32) * s
        Wg2 = jax.random.normal(ks[6], (G, E), jnp.float32) * G ** (-0.5)
        ln_w = jnp.ones((E,), jnp.float32)
        ln_b = jnp.zeros((E,), jnp.float32)
        return {'x': x, 'log_slope': log_slope, 'Wq': Wq, 'Wk': Wk, 'Wv': Wv, 'Wo': Wo, 'Wg1': Wg1, 'Wg2': Wg2, 'ln_w': ln_w, 'ln_b': ln_b}
    _L0_attn_all = _L0_attn_setup()
    _L0_attn_in = {k: v for k, v in _L0_attn_all.items() if k in ('log_slope', 'Wq', 'Wk', 'Wv', 'Wo', 'Wg1', 'Wg2', 'ln_w', 'ln_b')}
    del _L0_attn_all

    def _L0_ffn_setup():
        import jax, jax.numpy as jnp
        import numpy as np
        HID = 192
        NQ = 12
        NKV = 3
        HD = 64
        REP = NQ // NKV
        E = 16
        TOPK = 2
        FF = 384
        EPS = 1e-06
        THETA = 10000.0

        def rms_norm(x, w):
            return x / jnp.sqrt(jnp.mean(x * x, axis=-1, keepdims=True) + EPS) * w

        def rope_tables(seq_len):
            inv = 1.0 / THETA ** (jnp.arange(0, HD, 2, dtype=jnp.float32) / HD)
            f = jnp.arange(seq_len, dtype=jnp.float32)[:, None] * inv[None, :]
            return (jnp.cos(f), jnp.sin(f))

        def apply_rope(t, cos, sin):
            B, S, H, _ = t.shape
            tr = t.reshape(B, S, H, HD // 2, 2)
            c = cos[None, :, None, :]
            s = sin[None, :, None, :]
            r0 = tr[..., 0] * c - tr[..., 1] * s
            r1 = tr[..., 0] * s + tr[..., 1] * c
            return jnp.stack([r0, r1], axis=-1).reshape(B, S, H, HD)

        def attention(x, w_qkv, w_out):
            B, S, _ = x.shape
            qkv = x @ w_qkv
            q, k, v = jnp.split(qkv, [NQ * HD, (NQ + NKV) * HD], axis=-1)
            q = q.reshape(B, S, NQ, HD)
            k = k.reshape(B, S, NKV, HD)
            v = v.reshape(B, S, NKV, HD)
            cos, sin = rope_tables(S)
            q = apply_rope(q, cos, sin)
            k = apply_rope(k, cos, sin)
            k = jnp.repeat(k, REP, axis=2)
            v = jnp.repeat(v, REP, axis=2)
            q = q.transpose(0, 2, 1, 3)
            k = k.transpose(0, 2, 1, 3)
            v = v.transpose(0, 2, 1, 3)
            scores = jnp.einsum('bhqd,bhkd->bhqk', q, k) / jnp.sqrt(jnp.float32(HD))
            causal = jnp.tril(jnp.ones((S, S), dtype=bool))
            scores = jnp.where(causal[None, None], scores, jnp.finfo(scores.dtype).min)
            attn = jax.nn.softmax(scores, axis=-1)
            out = jnp.einsum('bhqk,bhkd->bhqd', attn, v)
            out = out.transpose(0, 2, 1, 3).reshape(B, S, NQ * HD)
            return out @ w_out

        def moe_ffn(x2d, w_router, w_gate_up, w_down):
            logits = x2d @ w_router
            probs = jax.nn.softmax(logits, axis=-1)
            vals, idx = jax.lax.top_k(probs, TOPK)
            vals = vals / jnp.sum(vals, axis=-1, keepdims=True)
            combine = jnp.sum(jax.nn.one_hot(idx, E, dtype=x2d.dtype) * vals[..., None], axis=1)
            out = jnp.zeros_like(x2d)
            for e in range(E):
                gu = x2d @ w_gate_up[e]
                gate, up = jnp.split(gu, 2, axis=-1)
                h = jax.nn.silu(gate) * up
                out = out + combine[:, e:e + 1] * (h @ w_down[e])
            return out
        key = jax.random.key(seed)
        ks = jax.random.split(key, 6)
        B, S = (1, 512)
        return {'x': jax.random.normal(ks[0], (B, S, HID), dtype=jnp.float32), 'norm1_w': jnp.ones((HID,), dtype=jnp.float32), 'w_qkv': jax.random.normal(ks[1], (HID, (NQ + 2 * NKV) * HD), dtype=jnp.float32) * 0.02, 'w_out': jax.random.normal(ks[2], (NQ * HD, HID), dtype=jnp.float32) * 0.02, 'norm2_w': jnp.ones((HID,), dtype=jnp.float32), 'w_router': jax.random.normal(ks[3], (HID, E), dtype=jnp.float32) * 0.02, 'w_gate_up': jax.random.normal(ks[4], (E, HID, 2 * FF), dtype=jnp.float32) * 0.02, 'w_down': jax.random.normal(ks[5], (E, FF, HID), dtype=jnp.float32) * 0.02}
    _L0_ffn_all = _L0_ffn_setup()
    _L0_ffn_in = {k: v for k, v in _L0_ffn_all.items() if k in ('norm1_w', 'w_qkv', 'w_out', 'norm2_w', 'w_router', 'w_gate_up', 'w_down')}
    del _L0_ffn_all

    def _L1_attn_setup():
        import jax, jax.numpy as jnp
        import numpy as np
        EPS = 1e-05
        NUM_HEADS = 12

        def rmsnorm(x, g):
            var = jnp.mean(x * x, axis=-1, keepdims=True)
            return x * jax.lax.rsqrt(var + EPS) * g

        def activation_quant(x):
            scale = 127.0 / jnp.clip(jnp.max(jnp.abs(x), axis=-1, keepdims=True), EPS, None)
            return jnp.clip(jnp.round(x * scale), -128, 127) / scale

        def weight_quant(w):
            scale = 1.0 / jnp.clip(jnp.mean(jnp.abs(w)), EPS, None)
            return jnp.clip(jnp.round(w * scale), -1, 1) / scale

        def bitlinear(x, w, g):
            xn = rmsnorm(x, g)
            xq = xn + jax.lax.stop_gradient(activation_quant(xn) - xn)
            wq = w + jax.lax.stop_gradient(weight_quant(w) - w)
            return jnp.einsum('bnc,oc->bno', xq, wq)
        key = jax.random.key(seed)
        k1, k2, k3 = jax.random.split(key, 3)
        B, N, C = (2, 512, 192)
        return {'x': jax.random.normal(k1, (B, N, C), dtype=jnp.float32), 'w_qkv': jax.random.normal(k2, (3 * C, C), dtype=jnp.float32) * 0.02, 'g_qkv': jnp.ones((C,), dtype=jnp.float32), 'w_proj': jax.random.normal(k3, (C, C), dtype=jnp.float32) * 0.02, 'g_proj': jnp.ones((C,), dtype=jnp.float32)}
    _L1_attn_all = _L1_attn_setup()
    _L1_attn_in = {k: v for k, v in _L1_attn_all.items() if k in ('w_qkv', 'g_qkv', 'w_proj', 'g_proj')}
    del _L1_attn_all

    def _L1_ffn_setup():
        import jax, jax.numpy as jnp
        import numpy as np
        from jax import lax
        DIM = 192
        INTER = 128
        E = 8
        G = 4
        TOPK_G = 2
        TOPK = 2
        ROUTE_SCALE = 1.0

        def _gate(x2, gate_weight, gate_bias):
            T = x2.shape[0]
            scores = jax.nn.sigmoid(x2 @ gate_weight.T)
            s = scores + gate_bias
            sv = s.reshape(T, G, E // G)
            top2, _ = lax.top_k(sv, 2)
            group_scores = top2.sum(-1)
            _, gidx = lax.top_k(group_scores, TOPK_G)
            gmask = jnp.zeros((T, G), bool).at[jnp.arange(T)[:, None], gidx].set(True)
            masked = jnp.where(gmask[:, :, None], sv, -jnp.inf).reshape(T, E)
            _, idx = lax.top_k(masked, TOPK)
            w = jnp.take_along_axis(scores, idx, axis=1)
            w = w / (w.sum(-1, keepdims=True) + 1e-06) * ROUTE_SCALE
            return (w, idx)
        key = jax.random.key(seed)
        ks = jax.random.split(key, 9)
        s = 1.0 / np.sqrt(DIM)
        si = 1.0 / np.sqrt(INTER)
        return {'x': jax.random.normal(ks[0], (4, 1024, DIM), jnp.float32), 'gate_weight': jax.random.uniform(ks[1], (E, DIM), jnp.float32, -s, s), 'gate_bias': jnp.zeros((E,), jnp.float32), 'w1': jax.random.uniform(ks[2], (E, INTER, DIM), jnp.float32, -s, s), 'w2': jax.random.uniform(ks[3], (E, DIM, INTER), jnp.float32, -si, si), 'w3': jax.random.uniform(ks[4], (E, INTER, DIM), jnp.float32, -s, s), 'sw1': jax.random.uniform(ks[5], (INTER, DIM), jnp.float32, -s, s), 'sw2': jax.random.uniform(ks[6], (DIM, INTER), jnp.float32, -si, si), 'sw3': jax.random.uniform(ks[7], (INTER, DIM), jnp.float32, -s, s)}
    _L1_ffn_all = _L1_ffn_setup()
    _L1_ffn_in = {k: v for k, v in _L1_ffn_all.items() if k in ('gate_weight', 'gate_bias', 'w1', 'w2', 'w3', 'sw1', 'sw2', 'sw3')}
    del _L1_ffn_all
    return {'x': x, 'L0_tok_ln1_g': _L0_tok_in['ln1_g'], 'L0_tok_ln1_b': _L0_tok_in['ln1_b'], 'L0_tok_W': _L0_tok_in['W'], 'L0_tok_b': _L0_tok_in['b'], 'L0_tok_ln2_g': _L0_tok_in['ln2_g'], 'L0_tok_ln2_b': _L0_tok_in['ln2_b'], 'L0_tok_cls_token': _L0_tok_in['cls_token'], 'L0_tok_pos_embed': _L0_tok_in['pos_embed'], 'L0_attn_log_slope': _L0_attn_in['log_slope'], 'L0_attn_Wq': _L0_attn_in['Wq'], 'L0_attn_Wk': _L0_attn_in['Wk'], 'L0_attn_Wv': _L0_attn_in['Wv'], 'L0_attn_Wo': _L0_attn_in['Wo'], 'L0_attn_Wg1': _L0_attn_in['Wg1'], 'L0_attn_Wg2': _L0_attn_in['Wg2'], 'L0_attn_ln_w': _L0_attn_in['ln_w'], 'L0_attn_ln_b': _L0_attn_in['ln_b'], 'L0_ffn_norm1_w': _L0_ffn_in['norm1_w'], 'L0_ffn_w_qkv': _L0_ffn_in['w_qkv'], 'L0_ffn_w_out': _L0_ffn_in['w_out'], 'L0_ffn_norm2_w': _L0_ffn_in['norm2_w'], 'L0_ffn_w_router': _L0_ffn_in['w_router'], 'L0_ffn_w_gate_up': _L0_ffn_in['w_gate_up'], 'L0_ffn_w_down': _L0_ffn_in['w_down'], 'L1_attn_w_qkv': _L1_attn_in['w_qkv'], 'L1_attn_g_qkv': _L1_attn_in['g_qkv'], 'L1_attn_w_proj': _L1_attn_in['w_proj'], 'L1_attn_g_proj': _L1_attn_in['g_proj'], 'L1_ffn_gate_weight': _L1_ffn_in['gate_weight'], 'L1_ffn_gate_bias': _L1_ffn_in['gate_bias'], 'L1_ffn_w1': _L1_ffn_in['w1'], 'L1_ffn_w2': _L1_ffn_in['w2'], 'L1_ffn_w3': _L1_ffn_in['w3'], 'L1_ffn_sw1': _L1_ffn_in['sw1'], 'L1_ffn_sw2': _L1_ffn_in['sw2'], 'L1_ffn_sw3': _L1_ffn_in['sw3']}

def reference(x, L0_tok_ln1_g, L0_tok_ln1_b, L0_tok_W, L0_tok_b, L0_tok_ln2_g, L0_tok_ln2_b, L0_tok_cls_token, L0_tok_pos_embed, L0_attn_log_slope, L0_attn_Wq, L0_attn_Wk, L0_attn_Wv, L0_attn_Wo, L0_attn_Wg1, L0_attn_Wg2, L0_attn_ln_w, L0_attn_ln_b, L0_ffn_norm1_w, L0_ffn_w_qkv, L0_ffn_w_out, L0_ffn_norm2_w, L0_ffn_w_router, L0_ffn_w_gate_up, L0_ffn_w_down, L1_attn_w_qkv, L1_attn_g_qkv, L1_attn_w_proj, L1_attn_g_proj, L1_ffn_gate_weight, L1_ffn_gate_bias, L1_ffn_w1, L1_ffn_w2, L1_ffn_w3, L1_ffn_sw1, L1_ffn_sw2, L1_ffn_sw3):
    import jax
    import jax.numpy as jnp

    def _L0_tok_ref(x, ln1_g, ln1_b, W, b, ln2_g, ln2_b, cls_token, pos_embed):
        import jax, jax.numpy as jnp
        import numpy as np
        B, C, H, Wd = (64, 3, 96, 96)
        PH = PW = 16
        NH, NW = (H // PH, Wd // PW)
        NP = NH * NW
        PD = C * PH * PW
        ED = 192
        EPS = 1e-05

        def layernorm(x, g, b):
            mu = jnp.mean(x, axis=-1, keepdims=True)
            var = jnp.mean(jnp.square(x - mu), axis=-1, keepdims=True)
            return (x - mu) * jax.lax.rsqrt(var + EPS) * g + b
        bsz = x.shape[0]
        p = x.reshape(bsz, C, NH, PH, NW, PW)
        p = p.transpose(0, 2, 4, 3, 5, 1).reshape(bsz, NP, PD)
        out = layernorm(p, ln1_g, ln1_b)
        out = jnp.einsum('bnp,pe->bne', out, W) + b
        out = layernorm(out, ln2_g, ln2_b)
        cls = jnp.broadcast_to(cls_token, (bsz, 1, ED))
        out = jnp.concatenate([cls, out], axis=1)
        out = out + pos_embed
        return out

    def _L0_attn_ref(x, log_slope, Wq, Wk, Wv, Wo, Wg1, Wg2, ln_w, ln_b):
        import jax, jax.numpy as jnp
        import numpy as np
        B, N, E, H = (2, 512, 192, 12)
        D = E // H
        G = 16
        LN_EPS = 1e-05

        def _layernorm(x, w, b):
            mu = jnp.mean(x, axis=-1, keepdims=True)
            var = jnp.mean(jnp.square(x - mu), axis=-1, keepdims=True)
            return (x - mu) * jax.lax.rsqrt(var + LN_EPS) * w + b
        b, n, e = x.shape
        h = log_slope.shape[0]
        d = e // h
        silu = jax.nn.silu
        q = silu(x @ Wq).reshape(b, n, h, d).transpose(0, 2, 1, 3)
        k = silu(x @ Wk).reshape(b, n, h, d).transpose(0, 2, 1, 3)
        v = silu(x @ Wv).reshape(b, n, h, d).transpose(0, 2, 1, 3)
        idx = jnp.arange(n, dtype=jnp.float32)
        diff = idx[:, None] - idx[None, :]
        keep = diff >= 0
        decay = jnp.where(keep, jnp.exp(log_slope[:, None, None] * jnp.maximum(diff, 0.0)), 0.0)
        energy = jnp.einsum('bhnd,bhmd->bhnm', q, k) * decay
        out = jnp.einsum('bhnm,bhmd->bhnd', energy, v)
        out = out.transpose(0, 2, 1, 3).reshape(b, n, e)
        gate = jax.nn.sigmoid(x @ Wg1 @ Wg2)
        out = out * gate
        out = out @ Wo
        out = _layernorm(out, ln_w, ln_b)
        return out

    def _L0_ffn_ref(x, norm1_w, w_qkv, w_out, norm2_w, w_router, w_gate_up, w_down):
        import jax, jax.numpy as jnp
        import numpy as np
        HID = 192
        NQ = 12
        NKV = 3
        HD = 64
        REP = NQ // NKV
        E = 16
        TOPK = 2
        FF = 384
        EPS = 1e-06
        THETA = 10000.0

        def rms_norm(x, w):
            return x / jnp.sqrt(jnp.mean(x * x, axis=-1, keepdims=True) + EPS) * w

        def rope_tables(seq_len):
            inv = 1.0 / THETA ** (jnp.arange(0, HD, 2, dtype=jnp.float32) / HD)
            f = jnp.arange(seq_len, dtype=jnp.float32)[:, None] * inv[None, :]
            return (jnp.cos(f), jnp.sin(f))

        def apply_rope(t, cos, sin):
            B, S, H, _ = t.shape
            tr = t.reshape(B, S, H, HD // 2, 2)
            c = cos[None, :, None, :]
            s = sin[None, :, None, :]
            r0 = tr[..., 0] * c - tr[..., 1] * s
            r1 = tr[..., 0] * s + tr[..., 1] * c
            return jnp.stack([r0, r1], axis=-1).reshape(B, S, H, HD)

        def attention(x, w_qkv, w_out):
            B, S, _ = x.shape
            qkv = x @ w_qkv
            q, k, v = jnp.split(qkv, [NQ * HD, (NQ + NKV) * HD], axis=-1)
            q = q.reshape(B, S, NQ, HD)
            k = k.reshape(B, S, NKV, HD)
            v = v.reshape(B, S, NKV, HD)
            cos, sin = rope_tables(S)
            q = apply_rope(q, cos, sin)
            k = apply_rope(k, cos, sin)
            k = jnp.repeat(k, REP, axis=2)
            v = jnp.repeat(v, REP, axis=2)
            q = q.transpose(0, 2, 1, 3)
            k = k.transpose(0, 2, 1, 3)
            v = v.transpose(0, 2, 1, 3)
            scores = jnp.einsum('bhqd,bhkd->bhqk', q, k) / jnp.sqrt(jnp.float32(HD))
            causal = jnp.tril(jnp.ones((S, S), dtype=bool))
            scores = jnp.where(causal[None, None], scores, jnp.finfo(scores.dtype).min)
            attn = jax.nn.softmax(scores, axis=-1)
            out = jnp.einsum('bhqk,bhkd->bhqd', attn, v)
            out = out.transpose(0, 2, 1, 3).reshape(B, S, NQ * HD)
            return out @ w_out

        def moe_ffn(x2d, w_router, w_gate_up, w_down):
            logits = x2d @ w_router
            probs = jax.nn.softmax(logits, axis=-1)
            vals, idx = jax.lax.top_k(probs, TOPK)
            vals = vals / jnp.sum(vals, axis=-1, keepdims=True)
            combine = jnp.sum(jax.nn.one_hot(idx, E, dtype=x2d.dtype) * vals[..., None], axis=1)
            out = jnp.zeros_like(x2d)
            for e in range(E):
                gu = x2d @ w_gate_up[e]
                gate, up = jnp.split(gu, 2, axis=-1)
                h = jax.nn.silu(gate) * up
                out = out + combine[:, e:e + 1] * (h @ w_down[e])
            return out
        B, S, _ = x.shape
        h = x + attention(rms_norm(x, norm1_w), w_qkv, w_out)
        moe_in = rms_norm(h, norm2_w).reshape(B * S, HID)
        out = h + moe_ffn(moe_in, w_router, w_gate_up, w_down).reshape(B, S, HID)
        return out

    def _L1_attn_ref(x, w_qkv, g_qkv, w_proj, g_proj):
        import jax, jax.numpy as jnp
        import numpy as np
        EPS = 1e-05
        NUM_HEADS = 12

        def rmsnorm(x, g):
            var = jnp.mean(x * x, axis=-1, keepdims=True)
            return x * jax.lax.rsqrt(var + EPS) * g

        def activation_quant(x):
            scale = 127.0 / jnp.clip(jnp.max(jnp.abs(x), axis=-1, keepdims=True), EPS, None)
            return jnp.clip(jnp.round(x * scale), -128, 127) / scale

        def weight_quant(w):
            scale = 1.0 / jnp.clip(jnp.mean(jnp.abs(w)), EPS, None)
            return jnp.clip(jnp.round(w * scale), -1, 1) / scale

        def bitlinear(x, w, g):
            xn = rmsnorm(x, g)
            xq = xn + jax.lax.stop_gradient(activation_quant(xn) - xn)
            wq = w + jax.lax.stop_gradient(weight_quant(w) - w)
            return jnp.einsum('bnc,oc->bno', xq, wq)
        B, N, C = x.shape
        H = NUM_HEADS
        D = C // H
        scale = D ** (-0.5)
        qkv = bitlinear(x, w_qkv, g_qkv)
        qkv = qkv.reshape(B, N, 3, H, D)
        q = qkv[:, :, 0].transpose(0, 2, 1, 3)
        k = qkv[:, :, 1].transpose(0, 2, 1, 3)
        v = qkv[:, :, 2].transpose(0, 2, 1, 3)
        attn = jnp.einsum('bhnd,bhmd->bhnm', q, k) * scale
        attn = jax.nn.softmax(attn, axis=-1)
        out = jnp.einsum('bhnm,bhmd->bhnd', attn, v)
        out = out.transpose(0, 2, 1, 3).reshape(B, N, C)
        return bitlinear(out, w_proj, g_proj)

    def _L1_ffn_ref(x, gate_weight, gate_bias, w1, w2, w3, sw1, sw2, sw3):
        import jax, jax.numpy as jnp
        import numpy as np
        from jax import lax
        DIM = 192
        INTER = 128
        E = 8
        G = 4
        TOPK_G = 2
        TOPK = 2
        ROUTE_SCALE = 1.0

        def _gate(x2, gate_weight, gate_bias):
            T = x2.shape[0]
            scores = jax.nn.sigmoid(x2 @ gate_weight.T)
            s = scores + gate_bias
            sv = s.reshape(T, G, E // G)
            top2, _ = lax.top_k(sv, 2)
            group_scores = top2.sum(-1)
            _, gidx = lax.top_k(group_scores, TOPK_G)
            gmask = jnp.zeros((T, G), bool).at[jnp.arange(T)[:, None], gidx].set(True)
            masked = jnp.where(gmask[:, :, None], sv, -jnp.inf).reshape(T, E)
            _, idx = lax.top_k(masked, TOPK)
            w = jnp.take_along_axis(scores, idx, axis=1)
            w = w / (w.sum(-1, keepdims=True) + 1e-06) * ROUTE_SCALE
            return (w, idx)
        B, S, D = x.shape
        x2 = x.reshape(-1, D)
        T = x2.shape[0]
        weights, indices = _gate(x2, gate_weight, gate_bias)
        cw = jnp.zeros((T, E), x.dtype).at[jnp.arange(T)[:, None], indices].add(weights)
        h1 = jnp.einsum('td,eid->tei', x2, w1)
        h3 = jnp.einsum('td,eid->tei', x2, w3)
        h = jax.nn.silu(h1) * h3
        y = jnp.einsum('tei,edi,te->td', h, w2, cw)
        z = jax.nn.silu(x2 @ sw1.T) * (x2 @ sw3.T) @ sw2.T
        return (y + z).reshape(B, S, D)
    h = _L0_tok_ref(x, L0_tok_ln1_g, L0_tok_ln1_b, L0_tok_W, L0_tok_b, L0_tok_ln2_g, L0_tok_ln2_b, L0_tok_cls_token, L0_tok_pos_embed)
    h = h + _L0_attn_ref(_layernorm(h, axis=-1), L0_attn_log_slope, L0_attn_Wq, L0_attn_Wk, L0_attn_Wv, L0_attn_Wo, L0_attn_Wg1, L0_attn_Wg2, L0_attn_ln_w, L0_attn_ln_b)
    h = h + _L0_ffn_ref(_layernorm(h, axis=-1), L0_ffn_norm1_w, L0_ffn_w_qkv, L0_ffn_w_out, L0_ffn_norm2_w, L0_ffn_w_router, L0_ffn_w_gate_up, L0_ffn_w_down)
    h = h + _L1_attn_ref(_layernorm(h, axis=-1), L1_attn_w_qkv, L1_attn_g_qkv, L1_attn_w_proj, L1_attn_g_proj)
    h = h + _L1_ffn_ref(_layernorm(h, axis=-1), L1_ffn_gate_weight, L1_ffn_gate_bias, L1_ffn_w1, L1_ffn_w2, L1_ffn_w3, L1_ffn_sw1, L1_ffn_sw2, L1_ffn_sw3)
    return h

_drawn_inputs = setup_inputs


def setup_inputs(seed=0):
    import zlib

    import numpy as np

    out = dict(_drawn_inputs(seed))
    spreads = {'L0_tok_ln1_g': (1.0, 0.2),
     'L0_tok_ln1_b': (0.0, 0.1),
     'L0_tok_b': (0.0, 0.1),
     'L0_tok_ln2_g': (1.0, 0.2),
     'L0_tok_ln2_b': (0.0, 0.1),
     'L0_attn_ln_w': (1.0, 0.2),
     'L0_attn_ln_b': (0.0, 0.1),
     'L0_ffn_norm1_w': (1.0, 0.6),
     'L0_ffn_norm2_w': (1.0, 0.6),
     'L1_attn_g_qkv': (1.0, 0.6),
     'L1_attn_g_proj': (1.0, 0.6),
     'L1_ffn_gate_bias': (0.0, 2.0)}
    factors = {'L0_ffn_w_router': 8.0,
     'L0_ffn_w_gate_up': 8.0,
     'L0_ffn_w_down': 8.0,
     'L1_attn_w_qkv': 4.07,
     'L1_attn_w_proj': 4.303,
     'L1_ffn_gate_weight': 8.0,
     'L1_ffn_w1': 8.0,
     'L1_ffn_w2': 8.0,
     'L1_ffn_w3': 8.0,
     'L1_ffn_sw1': 8.0,
     'L1_ffn_sw2': 8.0,
     'L1_ffn_sw3': 8.0}
    for name, (base, spread) in spreads.items():
        noise = np.random.default_rng([zlib.crc32(name.encode()), seed]).standard_normal(out[name].shape)
        drawn = base * np.exp(spread * noise) if base else spread * noise
        out[name] = jnp.asarray(drawn.astype(out[name].dtype))
    for name, factor in factors.items():
        out[name] = (out[name] * factor).astype(out[name].dtype)
    return out
```

```python
from contextlib import ExitStack

import numpy as np

import concourse.bass as bass
from concourse import mybir

ALU = mybir.AluOpType
ACT = mybir.ActivationFunctionType
AX = mybir.AxisListType
F32 = mybir.dt.float32
BF16 = mybir.dt.bfloat16
U32 = mybir.dt.uint32

IMAGES = 16
PATCHES = 36
SEQ = PATCHES + 1
PER_TILE = 3
ROWS = PER_TILE * SEQ
TILES = -(-IMAGES // PER_TILE)
GROUP = 3
GROUPS = TILES // GROUP
COLS = GROUP * ROWS
TOKENS = IMAGES * SEQ
E = 192
KH = E // 2
PD = 768
PCH = PD // 128
HEADS = 12
HD1 = E // HEADS
HD2 = 64
KV = 3
REP = HEADS // KV
EXPERTS0, FF0 = 16, 384
EXPERTS1, FF1 = 8, 128
MASKED = -1e30
MAGIC = 1.5 * 2.0 ** 23
RING = 4

CONST_PARTS = (("ident", 128), ("swap", 128), ("causal", ROWS), ("block", ROWS), ("ahead", ROWS),
               ("keep", ROWS), ("is_patch", 1), ("iota", EXPERTS0), ("cos", 2 * SEQ), ("sin", 2 * SEQ),
               ("lower", 64))
CONST_AT = {}
_at = 0
for _name, _width in CONST_PARTS:
    CONST_AT[_name] = (_at, _width)
    _at += _width
CONST_WIDTH = _at

LN_PATCH, LN_EMBED, LN_H0, LN_DECAY, LN_H1, RMS_GQA, RMS_MOE, LN_H2, RMS_TERN, RMS_PROJ, LN_H3 = range(11)
NORMS = 11
EPS = {n: 1e-6 if n in (RMS_GQA, RMS_MOE) else 1e-5 for n in range(NORMS)}


def live_cols(g):
    return min(COLS, TOKENS - g * COLS)


class Semaphores(dict):

    def __init__(self, nc, ctx):
        super().__init__()
        self.nc, self.ctx = nc, ctx

    def __missing__(self, name):
        self[name] = self.ctx.enter_context(self.nc.semaphore(name))
        return self[name]


def vit_tower(nc, consts, patches, w_patch, ln1_gb, rows_e, pos_rows, cls_rows, slopes, wqk1, wvo1, wg1, wg2,
              norm_cols, wqk2, wv2, wout2, wrouter0, w_gate_up, w_down, w_tern, g_tern, w_gate1, gate_bias,
              w13, w2, out):
    with ExitStack() as ctx:
        S = Semaphores(nc, ctx)

        def sb(name, shape, dt=F32):
            return ctx.enter_context(nc.sbuf_tensor(name, shape, dt))

        c_sb = sb("consts_sb", [128, CONST_WIDTH])
        ln1_sb = sb("ln1_gb_sb", [128, 2, PCH])
        re_sb = sb("rows_e_sb", [ROWS, 5, E])
        slope_sb = sb("slope_sb", [ROWS, HEADS])
        wqk1_sb = sb("wqk1_sb", [KH, 2, 2, 3, 128])
        wvo1_sb = sb("wvo1_sb", [KH, 2, 2, E])
        wg1_sb = sb("wg1_sb", [KH, 2, 16])
        wg2_sb = sb("wg2_sb", [16, E])
        ncol_sb = sb("norm_cols_sb", [KH, 2, 2])
        wqk2_sb = sb("wqk2_sb", [KH, 2, 8, 128])
        wv2_sb = sb("wv2_sb", [KH, 2, E])
        wout2_sb = sb("wout2_sb", [128, 6, E])
        wr0_sb = sb("wr0_sb", [KH, 2, EXPERTS0])
        wt_sb = sb("w_tern_sb", [KH, 2, 5 * E + E])
        gt_sb = sb("g_tern_sb", [ROWS, 2, E])
        wr1_sb = sb("wr1_sb", [KH, 2, EXPERTS1])
        gb_sb = sb("gate_bias_sb", [ROWS, EXPERTS1])
        WSLOTS = 3

        def const(name, rows=128):
            at, width = CONST_AT[name]
            return c_sb[0:rows, at:at + width]

        ident = const("ident")

        decay = sb("decay", [ROWS, 4, 3, ROWS])
        ident_bf = sb("ident_bf", [128, 128], BF16)
        causal_bf = sb("causal_bf", [ROWS, ROWS], BF16)
        block_bf = sb("block_bf", [ROWS, ROWS], BF16)
        ones = sb("ones", [128, 128])
        half_neg = sb("half_neg", [ROWS, TILES])
        tern = sb("tern", [KH, 2, 6 * E], BF16)
        tern_f = wt_sb
        tern_abs = sb("tern_abs", [KH, 2])
        tern_mean = sb("tern_mean", [128, 2])
        tern_scale = sb("tern_scale", [128, 2])

        area_a = sb("area_a", [128, TILES * PD])
        area_b = sb("area_b", [128, PCH * TILES * ROWS])
        area_c = sb("area_c", [128, 8 * TILES * ROWS])
        area_d = sb("area_d", [128, 12 * COLS])

        def part(area, at, rows, pattern, **sizes):
            n = 1
            for size in sizes.values():
                n *= size
            return area[0:rows, at:at + n].rearrange(f"rows ({pattern}) -> rows {pattern}", **sizes)

        patch_x = part(area_a, 0, ROWS, "t n", t=TILES, n=PD)
        w13_sb = part(area_a, 0, KH, "c e n", c=2, e=EXPERTS1 + 1, n=2 * FF1)
        patch_t = part(area_b, 0, 128, "c n", c=PCH, n=TILES * ROWS)
        w2_sb = part(area_b, 0, FF1, "e n", e=EXPERTS1 + 1, n=E)
        stats = sb("stats", [ROWS, TILES, 2, 6])
        mv = sb("mean_var", [ROWS, NORMS, TILES, 2])
        ve = sb("var_eps", [ROWS, NORMS, TILES])
        vt = sb("var_tmp", [ROWS, NORMS, TILES])
        rstd = sb("rstd", [ROWS, NORMS, TILES])
        y0 = sb("y0", [ROWS, TILES, E])
        z0 = sb("z0", [ROWS, TILES, E])
        h = [sb(f"h{n}", [ROWS, TILES, E]) for n in range(3)]
        h.append(h[0])
        xn = sb("xn", [ROWS, TILES, E])
        x_t = sb("x_t", [KH, 2, TILES * ROWS])
        qk1 = part(area_c, 0, 128, "a m n", a=2, m=3, n=TILES * ROWS)
        v1 = part(area_d, 0, ROWS, "t n", t=TILES, n=E)
        gate1 = part(area_d, TILES * E, ROWS, "t n", t=TILES, n=E)
        g1_t = area_d[0:16, 2 * TILES * E:2 * TILES * E + TILES * ROWS]
        o_rows = sb("o_rows", [ROWS, TILES, E])
        PB = 3
        area_e = sb("area_e", [128, 2 * PB * HEADS * ROWS])
        p_buf = part(area_e, 0, ROWS, "s p n", s=PB, p=HEADS, n=ROWS)
        pt_buf = part(area_e, PB * HEADS * ROWS, ROWS, "s p n", s=PB, p=HEADS, n=ROWS)
        wp_sb = part(area_e, 0, 128, "c n", c=PCH, n=E)
        pos_sb, cls_sb, gm_rows, add_rows = (area_e[0:ROWS, (PCH + n) * E:(PCH + n + 1) * E] for n in range(4))
        wgu_sb = part(area_e, 0, KH, "s c n", s=WSLOTS, c=2, n=2 * FF0)
        wdn_sb = part(area_e, WSLOTS * 4 * FF0, 128, "s c n", s=WSLOTS, c=3, n=E)
        x2 = y0
        raw, rsin, rcos = (part(area_d, 4 * n * COLS, 128, "s b n", s=2, b=2, n=COLS) for n in range(3))
        qk2 = part(area_c, 0, 128, "m n", m=8, n=TILES * ROWS)
        v2 = sb("v2", [ROWS, TILES, KV, HD2 + 1])
        nmax = sb("nmax", [ROWS, TILES, HEADS])
        rsum = sb("rsum", [ROWS, TILES, HEADS])
        o2 = patch_x
        o2_t = patch_t
        hh = z0
        m_t = x_t
        lg = sb("lg", [ROWS, TILES, EXPERTS0])
        top = sb("top", [ROWS, TILES, 8])
        top_i = sb("top_i", [ROWS, TILES, 8], U32)
        top_f = sb("top_f", [ROWS, TILES, 2])
        rt = [sb(f"rt{n}", [ROWS, TILES, EXPERTS0]) for n in range(6)]
        rden = sb("rden", [ROWS, TILES, 2])
        comb0 = sb("comb0", [ROWS, TILES, EXPERTS0])
        silu_buf = part(area_c, 0, 128, "s n", s=2, n=TOKENS)
        hid = part(area_c, 2 * TOKENS, 128, "s c n", s=2, c=3, n=TOKENS)

        x3 = xn
        amax = sb("amax", [ROWS, TILES, 4])
        q_int = sb("q_int", [ROWS, TILES, E], BF16)
        q_int_t = area_d[0:KH, 4 * COLS:6 * COLS].bitcast(BF16).rearrange("p (c n) -> p c n", c=2)
        qa = y0
        qb = z0
        diag = part(area_d, 6 * COLS + TILES * HEADS * (HD1 + 1), ROWS, "s n", s=2, n=ROWS)
        dq = area_d[:, 0:TILES * ROWS]
        qk3 = qk1
        v3 = part(area_d, 6 * COLS, ROWS, "t h n", t=TILES, h=HEADS, n=HD1 + 1)
        o3 = o_rows
        comb1 = sb("comb1", [ROWS, TILES, EXPERTS1])

        psum = [ctx.enter_context(nc.psum_tensor(f"slot{n}", [128, 2, 512], F32)) for n in range(RING)]

        def by_tile(slot, width=E, rows=ROWS):
            return slot[:].rearrange("p b (s x) -> p (b s) x", s=2)[0:rows, 0:GROUP, 0:width]

        def tile_cols(t):
            return slice(t * ROWS, (t + 1) * ROWS)

        def group_tiles(g):
            return range(g * GROUP, (g + 1) * GROUP)

        def gt(g):
            return slice(g * GROUP, (g + 1) * GROUP)

        def gcols(g, n=COLS):
            return slice(g * COLS, g * COLS + n)

        def on_tiles(ap, n=GROUP):
            return ap.unsqueeze(1).to_broadcast([ap.shape[0], n, ap.shape[1]])

        def along(ap, n):
            return ap.unsqueeze(2).to_broadcast([ap.shape[0], ap.shape[1], n])

        slot_of = {}
        ring = {"uses": 0, "freed": [[] for _ in range(RING)]}

        def take(pe, key, *freed_by):
            n = ring["uses"] % RING
            for s, value in ring["freed"][n]:
                pe.wait_ge(S[s], value)
            ring["freed"][n] = list(freed_by)
            ring["uses"] += 1
            slot_of[key] = psum[n]
            return psum[n]

        def nth(norm, g):
            return GROUPS * norm + g + 1

        block = ctx.enter_context(nc.Block())

        @block.tensor
        def _(pe):
            mm, tr = nc.tensor.matmul, nc.tensor.transpose

            def rows_to_columns(src, g, key, ready, *freed_by):
                slot = take(pe, key, *freed_by)
                for c in range(2):
                    for i, t in enumerate(group_tiles(g)):
                        last = tr(slot[0:KH, c, i * ROWS:(i + 1) * ROWS], src[:, t, c * KH:(c + 1) * KH],
                                  ident[0:ROWS, 0:ROWS])
                last.then_inc(S[ready], 1)

            def project_rows(lhs, w, g, key, ready, *freed_by):
                slot = take(pe, key, *freed_by)
                for i, t in enumerate(group_tiles(g)):
                    for c in range(2):
                        last = mm(by_tile(slot, w.shape[2])[:, i, :], lhs[:, c, tile_cols(t)], w[:, c, :],
                                  start=(c == 0), stop=(c == 1))
                last.then_inc(S[ready], 1)

            pe.wait_ge(S["consts_loaded"], 16)
            for g in range(GROUPS):
                pe.wait_ge(S["patch_normed"], g + 1)
                for u in range(PCH // 2):
                    slot = take(pe, ("patch_t", g, u), ("patch_t_dve", g * 3 + u + 1), ("patch_t_act", g * 3 + u + 1))
                    for b in range(2):
                        c = 2 * u + b
                        for i, t in enumerate(group_tiles(g)):
                            last = tr(slot[:, b, i * ROWS:(i + 1) * ROWS], patch_x[:, t, c * 128:(c + 1) * 128],
                                      ident[0:ROWS, 0:ROWS])
                    last.then_inc(S["patch_turned"], 1)
            pe.wait_ge(S["w_patch_loaded"], 16)
            for g in range(GROUPS):
                pe.wait_ge(S["patch_t_dve"], 3 * g + 3)
                pe.wait_ge(S["patch_t_act"], 3 * g + 3)
                slot = take(pe, ("embed", g), ("embed_biased", g + 1))
                for i, t in enumerate(group_tiles(g)):
                    for c in range(PCH):
                        last = mm(by_tile(slot)[:, i, :], patch_t[:, c, tile_cols(t)], wp_sb[:, c, :],
                                  start=(c == 0), stop=(c == PCH - 1))
                last.then_inc(S["embed_done"], 1)

            pe.wait_ge(S["w_attn1_loaded"], 64)
            for g in range(GROUPS):
                pe.wait_ge(S["x_normed"], g + 1)
                rows_to_columns(xn, g, ("x0_t", g), "x_turned", ("x_t_ready", g + 1))
            for g in range(GROUPS):
                pe.wait_ge(S["x_t_ready"], g + 1)
                for m in range(3):
                    slot = take(pe, ("qk1", g, m), ("qk1_silu", 3 * g + m + 1))
                    for b in range(2):
                        for c in range(2):
                            last = mm(slot[:, b, 0:COLS], wqk1_sb[:, c, b, m, :], x_t[:, c, gcols(g)],
                                      start=(c == 0), stop=(c == 1))
                    last.then_inc(S["qk1_done"], 1)
                project_rows(x_t, wvo1_sb[:, :, 0, :], g, ("v1", g), "v1_done", ("v1_silu", g + 1))
                slot = take(pe, ("g1", g), ("g1_copied", g + 1))
                for c in range(2):
                    last = mm(slot[0:16, 0, 0:COLS], wg1_sb[:, c, :], x_t[:, c, gcols(g)], start=(c == 0), stop=(c == 1))
                last.then_inc(S["g1_done"], 1)
                pe.wait_ge(S["g1_copied"], g + 1)
                slot = take(pe, ("gate1", g), ("gate1_tanh", g + 1))
                for i, t in enumerate(group_tiles(g)):
                    last = mm(by_tile(slot)[:, i, :], g1_t[:, tile_cols(t)], wg2_sb[:], start=True, stop=True)
                last.then_inc(S["gate1_done"], 1)

            def energies(t):
                for jp in range(2):
                    slot = take(pe, ("energy", t, jp), ("energy_decayed", 2 * t + jp + 1))
                    for m in range(3):
                        for b in range(2):
                            r = 32 * (2 * jp + b)
                            last = mm(slot[0:ROWS, b, m * ROWS:(m + 1) * ROWS], qk1[r:r + 32, 1, m, tile_cols(t)],
                                      qk1[r:r + 32, 0, m, tile_cols(t)], start=True, stop=True)
                    last.then_inc(S["energy_done"], 1)

            def decay_values(t):
                g, i = divmod(t, GROUP)
                if i == 0:
                    take(pe, ("decay_out", g), ("o1_gated", g + 1))
                slot = slot_of[("decay_out", g)]
                pe.wait_ge(S["energy_decayed"], 2 * t + 2)
                for hd in range(HEADS):
                    m, j = divmod(hd, 4)
                    last = mm(by_tile(slot)[:, i, hd * HD1:(hd + 1) * HD1],
                              p_buf[:, t % PB, j * 3 + m, :], v1[:, t, hd * HD1:(hd + 1) * HD1], start=True, stop=True)
                last.then_inc(S["decay_out_done"], 1)

            for g in range(GROUPS):
                pe.wait_ge(S["qk1_silu"], 3 * g + 3)
                pe.wait_ge(S["v1_silu"], g + 1)
                for i, t in enumerate(group_tiles(g)):
                    energies(t)
                    if i:
                        decay_values(t - 1)
                decay_values(t)
            for g in range(GROUPS):
                pe.wait_ge(S["o1_gated"], g + 1)
                rows_to_columns(o_rows, g, ("o1_t", g), "o1_turned", ("o1_t_ready", g + 1))
            for g in range(GROUPS):
                pe.wait_ge(S["o1_t_ready"], g + 1)
                project_rows(x_t, wvo1_sb[:, :, 1, :], g, ("attn1", g), "attn1_done", ("attn1_normed", g + 1))

            pe.wait_ge(S["w_attn2_loaded"], 64)
            for g in range(GROUPS):
                pe.wait_ge(S["x_normed"], 2 + g + 1)
                rows_to_columns(xn, g, ("x1_t", g), "x_turned", ("x_t_ready", 2 + g + 1))

            def project_qk2(g, u):
                n = 4 * g + u
                slot = take(pe, ("qk2", g, u), ("qk2_raw", n + 1))
                for b in range(2):
                    for c in range(2):
                        last = mm(slot[:, b, 0:COLS], wqk2_sb[:, c, 2 * u + b, :], x_t[:, c, gcols(g)],
                                  start=(c == 0), stop=(c == 1))
                last.then_inc(S["qk2_done"], 1)

            def swap_qk2(g, u):
                n = 4 * g + u
                pe.wait_ge(S["qk2_raw"], n + 1)
                slot = take(pe, ("swap", g, u), ("qk2_sin", n + 1))
                for b in range(2):
                    last = mm(slot[:, b, 0:COLS], const("swap"), raw[:, n % 2, b, :], start=True, stop=True)
                last.then_inc(S["qk2_swapped"], 1)

            for g in range(GROUPS):
                pe.wait_ge(S["x_t_ready"], 2 + g + 1)
                for u in range(4):
                    project_qk2(g, u)
                    if u:
                        swap_qk2(g, u - 1)
                project_rows(x_t, wv2_sb, g, ("v2", g), "v2_done", ("v2_copied", g + 1))
                swap_qk2(g, 3)

            pe.wait_ge(S["masks_made"], 1)

            def masked_scores2(t):
                for u, heads in enumerate((REP, 2)):
                    slot = take(pe, ("score2", t, u), ("probs", 2 * t + u + 1))
                    for b in range(2):
                        mm(slot[0:ROWS, b, 0:heads * ROWS], ident_bf[0:ROWS, 0:ROWS],
                           on_tiles(causal_bf[:], heads), start=True, stop=False, skip_group_check=True)
                    for i in range(heads):
                        for b in range(2):
                            q, k = (i, 6) if u == 0 else (4 + i, 7)
                            r = 64 * b
                            last = mm(slot[0:ROWS, b, i * ROWS:(i + 1) * ROWS], qk2[r:r + 64, q, tile_cols(t)],
                                      qk2[r:r + 64, k, tile_cols(t)], start=False, stop=True, skip_group_check=True)
                    last.then_inc(S["score_done"], 1)

            def turn_probs(base, t):
                for u, heads in enumerate((8, 4)):
                    n = base + t
                    slot = take(pe, ("probs_t", n, u), ("probs_t_dve" if u == 0 else "probs_t_act", n + 1))
                    pe.wait_ge(S["probs"], 2 * n + 2)
                    for i in range(heads):
                        last = tr(slot[0:ROWS, i // 4, (i % 4) * ROWS:(i % 4 + 1) * ROWS],
                                  p_buf[:, (TILES + n) % PB, 8 * u + i, :], ident[0:ROWS, 0:ROWS])
                    last.then_inc(S["probs_turned"], 1)

            def attend2(t):
                pe.wait_ge(S["probs_t_dve"], t + 1)
                pe.wait_ge(S["probs_t_act"], t + 1)
                slot = take(pe, ("attend2", t), ("o2_scaled", t + 1))
                for p in range(HEADS):
                    kv = p // 4
                    at = (p % 6) * (HD2 + 1)
                    last = mm(slot[0:ROWS, p // 6, at:at + HD2 + 1], pt_buf[:, t % PB, p, :], v2[:, t, kv, :],
                              start=True, stop=True)
                last.then_inc(S["attended"], 1)

            for g in range(GROUPS):
                pe.wait_ge(S["qk2_rotated"], 4 * g + 4)
                pe.wait_ge(S["v2_copied"], g + 1)
                for i, t in enumerate(group_tiles(g)):
                    masked_scores2(t)
                    if t >= 1:
                        turn_probs(0, t - 1)
                    if t >= 2:
                        attend2(t - 2)
            turn_probs(0, TILES - 1)
            attend2(TILES - 2)
            attend2(TILES - 1)
            for g in range(GROUPS):
                pe.wait_ge(S["o2_scaled"], 3 * g + 3)
                for u in range(3):
                    slot = take(pe, ("o2_t", g, u), ("o2_t_dve" if u % 2 else "o2_t_act", 3 * g + u + 1))
                    for b in range(2):
                        for i, t in enumerate(group_tiles(g)):
                            c = 2 * u + b
                            last = tr(slot[:, b, i * ROWS:(i + 1) * ROWS], o2[:, t, c * 128:(c + 1) * 128],
                                      ident[0:ROWS, 0:ROWS])
                    last.then_inc(S["o2_turned"], 1)
            for g in range(GROUPS):
                pe.wait_ge(S["o2_t_act"], 3 * g + 3)
                pe.wait_ge(S["o2_t_dve"], 3 * g + 2)
                slot = take(pe, ("attn2", g), ("hh_ready", g + 1))
                for i, t in enumerate(group_tiles(g)):
                    for c in range(6):
                        last = mm(by_tile(slot)[:, i, :], o2_t[:, c, tile_cols(t)], wout2_sb[:, c, :],
                                  start=(c == 0), stop=(c == 5))
                last.then_inc(S["attn2_done"], 1)

            for g in range(GROUPS):
                pe.wait_ge(S["x_normed"], 4 + g + 1)
                rows_to_columns(xn, g, ("m_t", g), "x_turned", ("m_t_ready", g + 1))
            for g in range(GROUPS):
                pe.wait_ge(S["m_t_ready"], g + 1)
                project_rows(m_t, wr0_sb, g, ("logits0", g), "logits0_done", ("logits0_copied", g + 1))

            def feed_up(n, w, sub, columns):
                for part in range(2):
                    slot = take(pe, ("ff", n, part), ("ff_silu" if part == 0 else "ff_hidden", n + 1))
                    for c in range(2):
                        for g in range(GROUPS):
                            last = mm(slot[:, g, 0:live_cols(g)], w(c, part), columns[:, c, gcols(g, live_cols(g))],
                                      start=(c == 0), stop=(c == 1))
                    last.then_inc(S["ff_up"], 1)

            def feed_down(n, down, pieces, hidden_after):
                for g in range(GROUPS):
                    slot = take(pe, ("down", n, g), ("ff_added", GROUPS * n + g + 1))
                    pe.wait_ge(S["ff_hidden"], hidden_after)
                    for i, t in enumerate(group_tiles(g)):
                        rows = min(ROWS, TOKENS - t * ROWS)
                        for c in range(pieces):
                            last = mm(by_tile(slot, rows=rows)[:, i, :], hid[:, n % 2, c, t * ROWS:t * ROWS + rows],
                                      down[:, c, :], start=(c == 0), stop=(c == pieces - 1))
                    last.then_inc(S["ff_down"], 1)

            for e in range(EXPERTS0 + 1):
                if e < EXPERTS0:
                    pe.wait_ge(S[f"expert_loaded{e % WSLOTS}"], 32 * (e // WSLOTS + 1))
                    for m in range(3):
                        if m == 2 and e >= 1:
                            feed_down(e - 1, wdn_sb[:, (e - 1) % WSLOTS], 3, 3 * e)
                        feed_up(3 * e + m, lambda c, part: wgu_sb[:, e % WSLOTS, c, part * FF0 + m * 128:
                                                                  part * FF0 + (m + 1) * 128], m, m_t)
                else:
                    feed_down(e - 1, wdn_sb[:, (e - 1) % WSLOTS], 3, 3 * e)

            pe.wait_ge(S["tern_summed"], 2)
            slot = take(pe, "tern_sum", ("tern_mean_ready", 1))
            mm(slot[:, 0, 0:2], ones[0:KH, :], tern_abs[:], start=True, stop=True).then_inc(S["tern_sum_done"], 1)

            def turn_ints(g, n):
                pe.wait_ge(S["quantised"], n + 1)
                slot = take(pe, ("ints_t", n), ("ints_t_ready", n + 1))
                view = slot[:].bitcast(BF16)
                for c in range(2):
                    for i, t in enumerate(group_tiles(g)):
                        last = tr(view[0:KH, c, i * 112:i * 112 + ROWS], q_int[:, t, c * KH:(c + 1) * KH],
                                  ident_bf[0:ROWS, 0:ROWS])
                last.then_inc(S["ints_turned"], 1)

            for g in range(GROUPS):
                turn_ints(g, g)
                slot = take(pe, ("dq", g), ("dq_ready", g + 1))
                for i, t in enumerate(group_tiles(g)):
                    pe.wait_ge(S["diag_ready"], t + 1)
                    last = mm(slot[:, 0, i * ROWS:(i + 1) * ROWS], ones[0:ROWS, :], diag[:, t % 2, :],
                              start=True, stop=True)
                    last.then_inc(S["dq_done"], 1)
            pe.wait_ge(S["tern_ready"], 1)
            for g in range(GROUPS):
                pe.wait_ge(S["ints_t_ready"], g + 1)
                for m in range(3):
                    slot = take(pe, ("qk3", g, m), ("qk3_scaled", 3 * g + m + 1))
                    for b in range(2):
                        for c in range(2):
                            at = b * 384 + m * 128
                            last = mm(slot[:, b, 0:COLS], tern[:, c, at:at + 128], q_int_t[:, c, gcols(g)],
                                      start=(c == 0), stop=(c == 1))
                    last.then_inc(S["qk3_done"], 1)
                project_rows(q_int_t, tern[:, :, 768:960], g, ("v3", g), "v3_done", ("v3_scaled", g + 1))

            def masked_scores3(t):
                n = TILES + t
                for jp in range(2):
                    slot = take(pe, ("score3", t, jp), ("probs", 2 * n + jp + 1))
                    for b in range(2):
                        mm(slot[0:ROWS, b, 0:COLS], ident_bf[0:ROWS, 0:ROWS], on_tiles(block_bf[:], 3),
                           start=True, stop=False, skip_group_check=True)
                    for m in range(3):
                        for b in range(2):
                            r = 32 * (2 * jp + b)
                            last = mm(slot[0:ROWS, b, m * ROWS:(m + 1) * ROWS], qk3[r:r + 32, 0, m, tile_cols(t)],
                                      qk3[r:r + 32, 1, m, tile_cols(t)], start=False, stop=True, skip_group_check=True)
                    last.then_inc(S["score_done"], 1)

            def attend3(t):
                n = TILES + t
                pe.wait_ge(S["probs_t_dve"], n + 1)
                pe.wait_ge(S["probs_t_act"], n + 1)
                slot = take(pe, ("attend3", t), ("o3_scaled", t + 1))
                for p in range(HEADS):
                    hd = (p % 3) * 4 + p // 3
                    last = mm(slot[0:ROWS, 0, hd * 17:hd * 17 + 17], pt_buf[:, n % PB, p, :], v3[:, t, hd, :],
                              start=True, stop=True)
                last.then_inc(S["attended"], 1)

            for g in range(GROUPS):
                pe.wait_ge(S["qk3_scaled"], 3 * g + 3)
                pe.wait_ge(S["v3_scaled"], g + 1)
                for i, t in enumerate(group_tiles(g)):
                    masked_scores3(t)
                    if t >= 1:
                        turn_probs(TILES, t - 1)
                    if t >= 2:
                        attend3(t - 2)
            turn_probs(TILES, TILES - 1)
            attend3(TILES - 2)
            attend3(TILES - 1)
            for g in range(GROUPS):
                turn_ints(g, 2 + g)
            for g in range(GROUPS):
                pe.wait_ge(S["ints_t_ready"], 2 + g + 1)
                project_rows(q_int_t, tern[:, :, 960:1152], g, ("attn3", g), "attn3_done", ("h3_ready", g + 1))

            pe.wait_ge(S["w_ff1_loaded"], 80)
            for g in range(GROUPS):
                pe.wait_ge(S["x_normed"], 6 + g + 1)
                rows_to_columns(xn, g, ("x4_t", g), "x_turned", ("x_t_ready", 4 + g + 1))
            for g in range(GROUPS):
                pe.wait_ge(S["x_t_ready"], 4 + g + 1)
                project_rows(x_t, wr1_sb, g, ("logits1", g), "logits1_done", ("logits1_sigmoid", g + 1))
            base = 3 * EXPERTS0
            order = [EXPERTS1] + list(range(EXPERTS1))
            for n in range(EXPERTS1 + 2):
                if n <= EXPERTS1:
                    e = order[n]
                    feed_up(base + n, lambda c, part: w13_sb[:, c, e, part * FF1:(part + 1) * FF1], 0, x_t)
                if n >= 1:
                    feed_down(EXPERTS0 + n - 1, w2_sb[:, order[n - 1]].unsqueeze(1), 1, base + n)

        @block.sync
        def _(sp):
            def load(dst, src, sem):
                sp.dma_start(dst, src).then_inc(S[sem], 16)

            for t in range(TILES):
                load(patch_x[:, t, :], patches[t], f"patch_loaded{t // GROUP}")
            load(c_sb[:], consts, "consts_loaded")
            load(ln1_sb[:], ln1_gb, "ln1_loaded")
            load(wp_sb[:], w_patch.rearrange("(c p) e -> p c e", p=128), "w_patch_loaded")
            load(re_sb[:], rows_e.unsqueeze(0).to_broadcast([ROWS, 5, E]), "rows_loaded")
            load(pos_sb[:], pos_rows, "rows_loaded")
            load(cls_sb[:], cls_rows, "rows_loaded")
            load(slope_sb[:], slopes.unsqueeze(0).to_broadcast([ROWS, HEADS]), "slopes_loaded")
            load(wqk1_sb[:], wqk1.rearrange("(c p) a m n -> p c a m n", p=KH), "w_attn1_loaded")
            load(wvo1_sb[:], wvo1.rearrange("(c p) a n -> p c a n", p=KH), "w_attn1_loaded")
            load(wg1_sb[:], wg1.rearrange("(c p) n -> p c n", p=KH), "w_attn1_loaded")
            load(wg2_sb[:], wg2, "w_attn1_loaded")
            load(ncol_sb[:], norm_cols, "norm_cols_loaded")
            load(wqk2_sb[:], wqk2.rearrange("(c p) m n -> p c m n", p=KH), "w_attn2_loaded")
            load(wv2_sb[:], wv2.rearrange("(c p) n -> p c n", p=KH), "w_attn2_loaded")
            load(wout2_sb[:], wout2.rearrange("(c p) n -> p c n", p=128), "w_attn2_loaded")
            load(wr0_sb[:], wrouter0.rearrange("(c p) n -> p c n", p=KH), "w_attn2_loaded")
            load(wt_sb[:], w_tern.rearrange("(c p) n -> p c n", p=KH), "w_tern_loaded")
            load(gt_sb[:], g_tern.unsqueeze(0).to_broadcast([ROWS, 2, E]), "g_tern_loaded")
            load(wr1_sb[:], w_gate1.rearrange("(c p) n -> p c n", p=KH), "w_ff1_loaded")
            load(gb_sb[:], gate_bias.unsqueeze(0).to_broadcast([ROWS, EXPERTS1]), "w_ff1_loaded")
            sp.wait_ge(S["attended"], TILES)
            for e in range(EXPERTS0):
                if e >= WSLOTS:
                    sp.wait_ge(S["ff_down"], GROUPS * (e - WSLOTS + 1))
                load(wgu_sb[:, e % WSLOTS], w_gate_up[e].rearrange("(c p) n -> p c n", p=KH), f"expert_loaded{e % WSLOTS}")
                load(wdn_sb[:, e % WSLOTS], w_down[e].rearrange("(c p) n -> p c n", p=128), f"expert_loaded{e % WSLOTS}")
            for c in range(2):
                load(w13_sb[:, c], w13.rearrange("e (c p) n -> c p e n", p=KH)[c], "w_ff1_loaded")
            load(w2_sb[:], w2.rearrange("e p n -> p e n"), "w_ff1_loaded")
            for t in range(TILES):
                rows = min(ROWS, TOKENS - t * ROWS)
                sp.wait_ge(S["ff_added"], GROUPS * (EXPERTS0 + EXPERTS1 + 1) - (GROUPS - 1 - t // GROUP))
                sp.dma_start(out[t * ROWS:t * ROWS + rows, :], h[3][0:rows, t, :]).then_inc(S["stored"], 16)
            sp.wait_ge(S["stored"], 16 * TILES)

        @block.gpsimd
        def _(pool):
            def power(norm, g):
                pool.wait_ge(S["norm_var"], nth(norm, g))
                nc.gpsimd.tensor_tensor(rstd[:, norm, gt(g)], ve[:, norm, gt(g)], half_neg[:, gt(g)],
                                        ALU.pow).then_inc(S["norm_rstd"], 1)

            nc.gpsimd.memset(half_neg[:], -0.5)
            nc.gpsimd.memset(ones[:], 1.0)
            nc.gpsimd.memset(v2[:, :, :, HD2:HD2 + 1], 1.0).then_inc(S["pool_consts"], 1)
            pool.wait_ge(S["pool_consts"], 1)
            power(LN_PATCH, 0)
            power(LN_PATCH, 1)
            pool.wait_ge(S["rows_loaded"], 48)
            pool.wait_ge(S["consts_loaded"], 16)
            patch_row = const("is_patch", ROWS)
            nc.gpsimd.tensor_tensor(gm_rows[:], re_sb[:, 1, :], patch_row.to_broadcast([ROWS, E]), ALU.mult)
            nc.gpsimd.tensor_tensor(add_rows[:], re_sb[:, 2, :], patch_row.to_broadcast([ROWS, E]),
                                    ALU.mult).then_inc(S["embed_rows"], 1)
            pool.wait_ge(S["embed_rows"], 1)
            nc.gpsimd.tensor_tensor(add_rows[:], add_rows[:], pos_sb[:], ALU.add).then_inc(S["embed_rows"], 1)
            pool.wait_ge(S["embed_rows"], 2)
            nc.gpsimd.tensor_tensor(add_rows[:], add_rows[:], cls_sb[:], ALU.add).then_inc(S["embed_rows"], 1)
            nc.gpsimd.tensor_copy(causal_bf[:], const("causal", ROWS))
            nc.gpsimd.tensor_copy(block_bf[:], const("block", ROWS))
            nc.gpsimd.tensor_copy(ident_bf[:], ident).then_inc(S["masks_made"], 1)
            for norm in (LN_EMBED, LN_H0, LN_DECAY, LN_H1):
                for g in range(GROUPS):
                    power(norm, g)
                    if norm == LN_H0:
                        pool.wait_ge(S["h0_ready"], g + 1)
                        nc.gpsimd.tensor_tensor(h[1][:, gt(g), :], h[0][:, gt(g), :], on_tiles(re_sb[:, 4, :]),
                                                ALU.add).then_inc(S["h0_shifted"], 1)
            for g in range(GROUPS):
                power(RMS_GQA, g)
            cos = const("cos").rearrange("p (a s) -> p a s", a=2)
            for g in range(GROUPS):
                for u in range(4):
                    n = 4 * g + u
                    pool.wait_ge(S["qk2_raw"], n + 1)
                    if n >= 2:
                        pool.wait_ge(S["qk2_rotated"], n - 1)
                    for b in range(2):
                        last = nc.gpsimd.tensor_tensor(
                            rcos[:, n % 2, b, :].rearrange("p (i s) -> p i s", s=SEQ),
                            raw[:, n % 2, b, :].rearrange("p (i s) -> p i s", s=SEQ),
                            cos[:, u // 3, :].unsqueeze(1).to_broadcast([128, COLS // SEQ, SEQ]), ALU.mult)
                    last.then_inc(S["qk2_cos"], 1)
            for g in range(GROUPS):
                power(RMS_MOE, g)
                pool.wait_ge(S["hh_ready"], g + 1)
                nc.gpsimd.tensor_tensor(h[2][:, gt(g), :], h[1][:, gt(g), :], hh[:, gt(g), :],
                                        ALU.add).then_inc(S["h2_base"], 1)
            for norm in (LN_H2, RMS_TERN, RMS_PROJ, LN_H3):
                for g in range(GROUPS):
                    power(norm, g)

        @block.scalar
        def _(act):
            fn = nc.scalar.activation

            act.wait_ge(S["consts_loaded"], 16)
            act.wait_ge(S["slopes_loaded"], 16)
            for hd in range(HEADS):
                last = fn(decay[:, hd % 4, hd // 4, :], const("ahead", ROWS), ACT.Exp, scale=slope_sb[:, hd:hd + 1])
            last.then_inc(S["decay_exp"], 1)
            act.wait_ge(S["ln1_loaded"], 16)
            for g in range(GROUPS):
                for u in range(PCH // 2):
                    c = 2 * u + 1
                    act.wait_ge(S["patch_turned"], 3 * g + u + 1)
                    fn(patch_t[:, c, gcols(g)], slot_of[("patch_t", g, u)][:, 1, 0:COLS], ACT.Identity,
                       scale=ln1_sb[:, 0, c:c + 1], bias=ln1_sb[:, 1, c:c + 1]).then_inc(S["patch_t_act"], 1)

            def columns(key, turned, n, g, dst, ready, scale=1.0):
                act.wait_ge(S[turned], n)
                fn(dst[:, :, gcols(g)], slot_of[key][0:KH, :, 0:COLS], ACT.Copy, scale=scale).then_inc(S[ready], 1)

            for g in range(GROUPS):
                columns(("x0_t", g), "x_turned", g + 1, g, x_t, "x_t_ready")
            for g in range(GROUPS):
                for m in range(3):
                    act.wait_ge(S["qk1_done"], 3 * g + m + 1)
                    fn(qk1[:, :, m, gcols(g)], slot_of[("qk1", g, m)][:, :, 0:COLS], ACT.Silu).then_inc(S["qk1_silu"], 1)
                act.wait_ge(S["v1_done"], g + 1)
                fn(v1[:, gt(g), :], by_tile(slot_of[("v1", g)]), ACT.Silu).then_inc(S["v1_silu"], 1)
                act.wait_ge(S["gate1_done"], g + 1)
                fn(gate1[:, gt(g), :], by_tile(slot_of[("gate1", g)]), ACT.Tanh, scale=0.5).then_inc(S["gate1_tanh"], 1)
            for g in range(GROUPS):
                columns(("o1_t", g), "o1_turned", g + 1, g, x_t, "o1_t_ready", scale=0.5)

            act.wait_ge(S["norm_cols_loaded"], 16)
            for g in range(GROUPS):
                act.wait_ge(S["x_turned"], 2 + g + 1)
                act.wait_ge(S["attn1_done"], g + 1)
                for c in range(2):
                    last = fn(x_t[:, c, gcols(g)], slot_of[("x1_t", g)][0:KH, c, 0:COLS], ACT.Copy,
                              scale=ncol_sb[:, c, 0:1])
                last.then_inc(S["x_t_ready"], 1)
            act.wait_ge(S["pool_consts"], 1)
            for g in range(GROUPS):
                for u in range(4):
                    n = 4 * g + u
                    act.wait_ge(S["qk2_done"], n + 1)
                    if n >= 2:
                        act.wait_ge(S["qk2_swapped"], n - 1)
                        act.wait_ge(S["qk2_cos"], n - 1)
                    fn(raw[:, n % 2], slot_of[("qk2", g, u)][:, :, 0:COLS], ACT.Copy).then_inc(S["qk2_raw"], 1)
                act.wait_ge(S["v2_done"], g + 1)
                src = by_tile(slot_of[("v2", g)])
                for i, t in enumerate(group_tiles(g)):
                    last = fn(v2[:, t, :, 0:HD2], src[:, i, :].rearrange("p (k d) -> p k d", k=KV), ACT.Copy)
                last.then_inc(S["v2_copied"], 1)

            def exps(n, unit, heads, src, scale):
                act.wait_ge(S["nmax_ready"], 2 * n + unit + 1)
                if n >= PB:
                    act.wait_ge(S["probs_turned"], 2 * (n - PB + 1))
                for i in range(heads):
                    at = (8 if heads == 4 else 6) * unit + i
                    last = fn(p_buf[:, (TILES + n) % PB, at, :], src(i), ACT.Exp,
                              bias=nmax[:, n % TILES, at:at + 1], scale=scale)
                last.then_inc(S["probs"], 1)

            def turned_probs(n):
                act.wait_ge(S["probs_turned"], 2 * n + 2)
                if n >= PB:
                    act.wait_ge(S["attended"], n - PB + 1)
                fn(pt_buf[:, n % PB, 8:12, :], slot_of[("probs_t", n, 1)][0:ROWS, 0, 0:4 * ROWS].rearrange(
                    "p (i x) -> p i x", x=ROWS), ACT.Copy).then_inc(S["probs_t_act"], 1)

            act.wait_ge(S["decay_out_done"], TILES)
            for t in range(TILES):
                s0, s1 = slot_of[("score2", t, 0)], slot_of[("score2", t, 1)]
                exps(t, 0, 8, lambda i: s0[0:ROWS, i // 4, (i % 4) * ROWS:(i % 4 + 1) * ROWS], 1.0)
                exps(t, 1, 4, lambda i: s1[0:ROWS, i // 2, (i % 2) * ROWS:(i % 2 + 1) * ROWS], 1.0)
                if t >= 1:
                    turned_probs(t - 1)
            turned_probs(TILES - 1)
            for g in range(GROUPS):
                for u in (0, 2):
                    act.wait_ge(S["o2_turned"], 3 * g + u + 1)
                    last = fn(o2_t[:, 2 * u:2 * u + 2, gcols(g)], slot_of[("o2_t", g, u)][:, :, 0:COLS], ACT.Copy)
                    last.then_inc(S["o2_t_act"], 1 if u == 0 else 2)

            for g in range(GROUPS):
                act.wait_ge(S["x_turned"], 4 + g + 1)
                for c in range(2):
                    last = fn(m_t[:, c, gcols(g)], slot_of[("m_t", g)][0:KH, c, 0:COLS], ACT.Copy,
                              scale=ncol_sb[:, c, 1:2])
                last.then_inc(S["m_t_ready"], 1)
            act.wait_ge(S["top0_ready"], 1)
            fn(rt[1][:], rt[0][:], ACT.Exp).then_inc(S["router_exp"], 1)

            def silu(n):
                act.wait_ge(S["ff_up"], 2 * n + 1)
                if n >= 2:
                    act.wait_ge(S["ff_hidden"], n - 1)
                for g in range(GROUPS):
                    last = fn(silu_buf[:, n % 2, gcols(g, live_cols(g))], slot_of[("ff", n, 0)][:, g, 0:live_cols(g)],
                              ACT.Silu)
                last.then_inc(S["ff_silu"], 1)

            for n in range(3 * EXPERTS0):
                silu(n)

            def int_columns(n, g):
                act.wait_ge(S["ints_turned"], n + 1)
                view = slot_of[("ints_t", n)][:].bitcast(BF16)
                for c in range(2):
                    last = fn(q_int_t[:, c, gcols(g)].rearrange("p (i x) -> p i x", x=ROWS),
                              view[0:KH, c, 0:3 * 112].rearrange("p (i x) -> p i x", x=112)[:, :, 0:ROWS], ACT.Copy)
                last.then_inc(S["ints_t_ready"], 1)

            for g in range(GROUPS):
                int_columns(g, g)
                act.wait_ge(S["dq_done"], 3 * g + 3)
                fn(dq[:, gcols(g)], slot_of[("dq", g)][:, 0, 0:COLS], ACT.Copy).then_inc(S["dq_ready"], 1)
            for t in range(TILES):
                for jp in range(2):
                    s = slot_of[("score3", t, jp)]
                    exps(TILES + t, jp, 6, lambda i: s[0:ROWS, i // 3, (i % 3) * ROWS:(i % 3 + 1) * ROWS], 0.25)
                if t >= 1:
                    turned_probs(TILES + t - 1)
            turned_probs(2 * TILES - 1)
            for g in range(GROUPS):
                int_columns(2 + g, g)
            for g in range(GROUPS):
                columns(("x4_t", g), "x_turned", 6 + g + 1, g, x_t, "x_t_ready")
            for g in range(GROUPS):
                act.wait_ge(S["logits1_done"], g + 1)
                fn(lg[:, gt(g), 0:EXPERTS1], by_tile(slot_of[("logits1", g)], EXPERTS1),
                   ACT.Sigmoid).then_inc(S["logits1_sigmoid"], 1)
            for n in range(EXPERTS1 + 1):
                silu(3 * EXPERTS0 + n)

        @block.vector
        def _(dve):
            v = nc.vector
            link = {"n": 0}

            def after(ins):
                link["n"] += 1
                ins.then_inc(S["dve_step"], 1)
                dve.wait_ge(S["dve_step"], link["n"])

            def statistics(norm, g, src, square=False, pieces=1):
                width = src.shape[2] // pieces
                for i, t in enumerate(group_tiles(g)):
                    for p in range(pieces):
                        last = v.bn_stats(stats[:, t, p, :], src[:, i, p * width:(p + 1) * width])
                after(last)
                for t in group_tiles(g):
                    last = v.bn_aggr(mv[:, norm, t, :], stats[:, t, 0:pieces, :].rearrange("p a b -> p (a b)"))
                after(last)
                if square:
                    after(v.tensor_tensor(vt[:, norm, gt(g)], mv[:, norm, gt(g), 0], mv[:, norm, gt(g), 0], ALU.mult))
                    v.scalar_tensor_tensor(ve[:, norm, gt(g)], vt[:, norm, gt(g)], EPS[norm], mv[:, norm, gt(g), 1],
                                           ALU.add, ALU.add).then_inc(S["norm_var"], 1)
                else:
                    v.tensor_scalar(ve[:, norm, gt(g)], mv[:, norm, gt(g), 1], EPS[norm], None,
                                    ALU.add).then_inc(S["norm_var"], 1)

            def second_moment(norm, of, g):
                dve.wait_ge(S["norm_rstd"], nth(of, g))
                after(v.tensor_tensor(vt[:, norm, gt(g)], rstd[:, of, gt(g)], rstd[:, of, gt(g)], ALU.mult))
                after(v.tensor_tensor(vt[:, norm, gt(g)], vt[:, norm, gt(g)], mv[:, of, gt(g), 1], ALU.mult))
                v.tensor_scalar(ve[:, norm, gt(g)], vt[:, norm, gt(g)], EPS[norm], None,
                                ALU.add).then_inc(S["norm_var"], 1)

            def normalise(norm, g, dst, src, centre=True):
                dve.wait_ge(S["norm_rstd"], nth(norm, g))
                for i, t in enumerate(group_tiles(g)):
                    r = rstd[:, norm, t:t + 1]
                    if centre:
                        last = v.tensor_scalar(dst[:, i, :], src[:, i, :], mv[:, norm, t, 0:1], r, ALU.subtract, ALU.mult)
                    else:
                        last = v.tensor_scalar(dst[:, i, :], src[:, i, :], r, None, ALU.mult)
                return last

            for g in range(GROUPS):
                dve.wait_ge(S[f"patch_loaded{g}"], 16 * GROUP)
                statistics(LN_PATCH, g, patch_x[:, gt(g), :], pieces=2)
            for g in range(GROUPS):
                normalise(LN_PATCH, g, patch_x[:, gt(g), :], patch_x[:, gt(g), :]).then_inc(S["patch_normed"], 1)
            dve.wait_ge(S["decay_exp"], 1)
            keep = const("keep", ROWS)
            flat = decay[:].rearrange("p j m n -> p (j m) n")
            v.tensor_tensor(flat, flat, on_tiles(keep, HEADS), ALU.mult).then_inc(S["decay_ready"], 1)
            dve.wait_ge(S["ln1_loaded"], 16)
            for g in range(GROUPS):
                for u in range(PCH // 2):
                    c = 2 * u
                    dve.wait_ge(S["patch_turned"], 3 * g + u + 1)
                    v.tensor_scalar(patch_t[:, c, gcols(g)], slot_of[("patch_t", g, u)][:, 0, 0:COLS],
                                    ln1_sb[:, 0, c:c + 1], ln1_sb[:, 1, c:c + 1], ALU.mult,
                                    ALU.add).then_inc(S["patch_t_dve"], 1)
            dve.wait_ge(S["rows_loaded"], 48)
            for g in range(GROUPS):
                dve.wait_ge(S["embed_done"], g + 1)
                v.tensor_tensor(y0[:, gt(g), :], by_tile(slot_of[("embed", g)]), on_tiles(re_sb[:, 0, :]),
                                ALU.add).then_inc(S["embed_biased"], 1)
                dve.wait_ge(S["embed_biased"], g + 1)
                statistics(LN_EMBED, g, y0[:, gt(g), :])
            dve.wait_ge(S["embed_rows"], 3)
            for g in range(GROUPS):
                after(normalise(LN_EMBED, g, z0[:, gt(g), :], y0[:, gt(g), :]))
                after(v.tensor_tensor(z0[:, gt(g), :], z0[:, gt(g), :], on_tiles(gm_rows[:]), ALU.mult))
                v.tensor_tensor(h[0][:, gt(g), :], z0[:, gt(g), :], on_tiles(add_rows[:]),
                                ALU.add).then_inc(S["h0_ready"], 1)
                dve.wait_ge(S["h0_ready"], g + 1)
                statistics(LN_H0, g, h[0][:, gt(g), :])
            for g in range(GROUPS):
                normalise(LN_H0, g, xn[:, gt(g), :], h[0][:, gt(g), :]).then_inc(S["x_normed"], 1)

            for g in range(GROUPS):
                dve.wait_ge(S["g1_done"], g + 1)
                v.tensor_copy(g1_t[:, gcols(g)], slot_of[("g1", g)][0:16, 0, 0:COLS]).then_inc(S["g1_copied"], 1)
            dve.wait_ge(S["decay_ready"], 1)
            for g in range(GROUPS):
                for t in group_tiles(g):
                    for jp in range(2):
                        dve.wait_ge(S["energy_done"], 2 * t + jp + 1)
                        if t >= PB:
                            dve.wait_ge(S["decay_out_done"], t - PB + 1)
                        v.tensor_tensor(p_buf[:, t % PB, 6 * jp:6 * jp + 6, :].rearrange("p (b m) n -> p b (m n)", b=2),
                                        slot_of[("energy", t, jp)][0:ROWS, :, 0:COLS],
                                        decay[:, 2 * jp:2 * jp + 2].rearrange("p b m n -> p b (m n)"),
                                        ALU.mult).then_inc(S["energy_decayed"], 1)
                dve.wait_ge(S["decay_out_done"], 3 * g + 3)
                dve.wait_ge(S["gate1_tanh"], g + 1)
                v.scalar_tensor_tensor(o_rows[:, gt(g), :], gate1[:, gt(g), :], 1.0, by_tile(slot_of[("decay_out", g)]),
                                       ALU.add, ALU.mult).then_inc(S["o1_gated"], 1)
            for g in range(GROUPS):
                dve.wait_ge(S["attn1_done"], g + 1)
                statistics(LN_DECAY, g, by_tile(slot_of[("attn1", g)]))
            for g in range(GROUPS):
                last = normalise(LN_DECAY, g, z0[:, gt(g), :], by_tile(slot_of[("attn1", g)]))
                last.then_inc(S["attn1_normed"], 1)
                dve.wait_ge(S["attn1_normed"], g + 1)
                after(v.tensor_tensor(z0[:, gt(g), :], z0[:, gt(g), :], on_tiles(re_sb[:, 3, :]), ALU.mult))
                dve.wait_ge(S["h0_shifted"], g + 1)
                v.tensor_tensor(h[1][:, gt(g), :], h[1][:, gt(g), :], z0[:, gt(g), :], ALU.add).then_inc(S["h1_ready"], 1)
                dve.wait_ge(S["h1_ready"], g + 1)
                statistics(LN_H1, g, h[1][:, gt(g), :])

            for g in range(GROUPS):
                second_moment(RMS_GQA, LN_H1, g)
                after(normalise(LN_H1, g, x2[:, gt(g), :], h[1][:, gt(g), :]))
            for g in range(GROUPS):
                normalise(RMS_GQA, g, xn[:, gt(g), :], x2[:, gt(g), :], centre=False).then_inc(S["x_normed"], 1)
            sin = const("sin").rearrange("p (a s) -> p a s", a=2)
            for g in range(GROUPS):
                for u in range(4):
                    n = 4 * g + u
                    dve.wait_ge(S["qk2_swapped"], n + 1)
                    for b in range(2):
                        last = v.tensor_tensor(rsin[:, n % 2, b, :].rearrange("p (i s) -> p i s", s=SEQ),
                                               slot_of[("swap", g, u)][:, b, 0:COLS].rearrange("p (i s) -> p i s", s=SEQ),
                                               sin[:, u // 3, :].unsqueeze(1).to_broadcast([128, COLS // SEQ, SEQ]),
                                               ALU.mult)
                    last.then_inc(S["qk2_sin"], 1)
                    dve.wait_ge(S["qk2_sin"], n + 1)
                    dve.wait_ge(S["qk2_cos"], n + 1)
                    v.tensor_tensor(qk2[:, 2 * u:2 * u + 2, gcols(g)], rsin[:, n % 2], rcos[:, n % 2],
                                    ALU.add).then_inc(S["qk2_rotated"], 1)

            def negative_max(n, unit, views, scale):
                dve.wait_ge(S["score_done"], 2 * n + unit + 1)
                src, banks, per = views
                at = 8 * unit if per != 3 else 6 * unit
                dst = nmax[:, n % TILES, at:at + banks * per].rearrange("p (b i) -> p b i", b=banks)
                last = v.tensor_reduce(dst, src, AX.X, ALU.max, negate=True)
                if scale != 1.0:
                    after(last)
                    last = v.tensor_scalar(dst, dst, scale, None, ALU.mult)
                last.then_inc(S["nmax_ready"], 1)

            def turned_probs(n):
                dve.wait_ge(S["probs_turned"], 2 * n + 1)
                if n >= PB:
                    dve.wait_ge(S["attended"], n - PB + 1)
                v.tensor_copy(pt_buf[:, n % PB, 0:8, :].rearrange("p (b i) x -> p b (i x)", b=2),
                              slot_of[("probs_t", n, 0)][0:ROWS, :, 0:4 * ROWS]).then_inc(S["probs_t_dve"], 1)

            def scaled2(t):
                dve.wait_ge(S["attended"], t + 1)
                src = slot_of[("attend2", t)][0:ROWS, :, 0:6 * (HD2 + 1)].rearrange("p b (i d) -> p b i d", d=HD2 + 1)
                rs = rsum[:, t, :].rearrange("p (b i) -> p b i", b=2)
                after(v.reciprocal(rs, src[:, :, :, HD2]))
                v.tensor_tensor(o2[:, t, :].rearrange("p (b i d) -> p b i d", b=2, d=HD2), src[:, :, :, 0:HD2],
                                rs.unsqueeze(3).to_broadcast([ROWS, 2, 6, HD2]), ALU.mult).then_inc(S["o2_scaled"], 1)

            for t in range(TILES):
                for u, per in enumerate((4, 2)):
                    src = slot_of[("score2", t, u)][0:ROWS, :, 0:per * ROWS].rearrange("p b (i x) -> p b i x", x=ROWS)
                    negative_max(t, u, (src, 2, per), 1.0)
                if t >= 1:
                    turned_probs(t - 1)
                if t >= 2:
                    scaled2(t - 2)
            turned_probs(TILES - 1)
            scaled2(TILES - 2)
            scaled2(TILES - 1)
            for g in range(GROUPS):
                dve.wait_ge(S["o2_turned"], 3 * g + 2)
                last = v.tensor_copy(o2_t[:, 2:4, gcols(g)], slot_of[("o2_t", g, 1)][:, :, 0:COLS])
                last.then_inc(S["o2_t_dve"], 2 if g == 0 else 3)
            for g in range(GROUPS):
                dve.wait_ge(S["attn2_done"], g + 1)
                v.tensor_tensor(hh[:, gt(g), :], by_tile(slot_of[("attn2", g)]), x2[:, gt(g), :],
                                ALU.add).then_inc(S["hh_ready"], 1)
                dve.wait_ge(S["hh_ready"], g + 1)
                statistics(RMS_MOE, g, hh[:, gt(g), :], square=True)
            for g in range(GROUPS):
                normalise(RMS_MOE, g, xn[:, gt(g), :], hh[:, gt(g), :], centre=False).then_inc(S["x_normed"], 1)

            for g in range(GROUPS):
                dve.wait_ge(S["logits0_done"], g + 1)
                v.tensor_copy(lg[:, gt(g), :], by_tile(slot_of[("logits0", g)], EXPERTS0)).then_inc(S["logits0_copied"], 1)
            dve.wait_ge(S["logits0_copied"], 2)
            for t in range(TILES):
                last = v.max(top[:, t, :], lg[:, t, :])
            after(last)
            for t in range(TILES):
                last = v.max_index(top_i[:, t, :], top[:, t, :], lg[:, t, :])
            after(last)
            after(v.tensor_copy(top_f[:], top_i[:, :, 0:2]))
            iota = on_tiles(const("iota", ROWS), TILES)
            v.tensor_tensor(rt[2][:], iota, along(top_f[:, :, 0], EXPERTS0), ALU.is_equal)
            v.tensor_tensor(rt[3][:], iota, along(top_f[:, :, 1], EXPERTS0), ALU.is_equal)
            v.tensor_tensor(rt[0][:], lg[:], along(top[:, :, 0], EXPERTS0), ALU.subtract).then_inc(S["top0_ready"], 1)
            dve.wait_ge(S["top0_ready"], 1)
            after(v.tensor_tensor(rt[2][:], rt[2][:], rt[3][:], ALU.add))
            dve.wait_ge(S["router_exp"], 1)
            after(v.tensor_tensor(rt[4][:], rt[1][:], rt[2][:], ALU.mult))
            after(v.tensor_reduce(rden[:, :, 0:1], rt[4][:], AX.X, ALU.add))
            after(v.reciprocal(rden[:, :, 1:2], rden[:, :, 0:1]))
            after(v.tensor_tensor(comb0[:], rt[4][:], along(rden[:, :, 1], EXPERTS0), ALU.mult))

            def hidden(n, buffer, piece):
                dve.wait_ge(S["ff_silu"], n + 1)
                dve.wait_ge(S["ff_up"], 2 * n + 2)
                for g in range(GROUPS):
                    cols = gcols(g, live_cols(g))
                    last = v.tensor_tensor(hid[:, buffer, piece, cols], silu_buf[:, n % 2, cols],
                                           slot_of[("ff", n, 1)][:, g, 0:live_cols(g)], ALU.mult)
                last.then_inc(S["ff_hidden"], 1)

            def add_expert(n, dst, weight):
                for g in range(GROUPS):
                    dve.wait_ge(S["ff_down"], GROUPS * n + g + 1)
                    for i, t in enumerate(group_tiles(g)):
                        rows = min(ROWS, TOKENS - t * ROWS)
                        last = v.scalar_tensor_tensor(dst[0:rows, t, :], by_tile(slot_of[("down", n, g)], rows=rows)[:, i, :],
                                                      weight(t, rows), dst[0:rows, t, :], ALU.mult, ALU.add)
                    last.then_inc(S["ff_added"], 1)

            dve.wait_ge(S["h2_base"], 2)
            for n in range(3 * EXPERTS0):
                e, m = divmod(n, 3)
                hidden(n, e % 2, m)
                if m == 1 and e >= 1:
                    if e >= 2:
                        dve.wait_ge(S["ff_added"], GROUPS * (e - 1))
                    add_expert(e - 1, h[2], lambda t, rows: comb0[0:rows, t, e - 1:e])
            dve.wait_ge(S["ff_added"], GROUPS * (EXPERTS0 - 1))
            add_expert(EXPERTS0 - 1, h[2], lambda t, rows: comb0[0:rows, t, EXPERTS0 - 1:EXPERTS0])
            dve.wait_ge(S["ff_added"], GROUPS * EXPERTS0)

            dve.wait_ge(S["w_tern_loaded"], 16)
            dve.wait_ge(S["g_tern_loaded"], 16)
            for n, cols in enumerate((slice(0, 5 * E), slice(5 * E, 6 * E))):
                v.tensor_reduce(tern_abs[:, n:n + 1], wt_sb[:, :, cols], AX.XY, ALU.add,
                                apply_absolute_value=True).then_inc(S["tern_summed"], 1)
            dve.wait_ge(S["tern_sum_done"], 1)
            for n, count in enumerate((3 * E * E, E * E)):
                last = v.tensor_scalar(tern_mean[:, n:n + 1], slot_of["tern_sum"][:, 0, n:n + 1], 1.0 / count, 1e-5,
                                       ALU.mult, ALU.max)
            last.then_inc(S["tern_mean_ready"], 1)
            dve.wait_ge(S["tern_mean_ready"], 1)
            after(v.reciprocal(tern_scale[:], tern_mean[:]))
            for n, cols in enumerate((slice(0, 5 * E), slice(5 * E, 6 * E))):
                last = v.tensor_scalar(tern_f[:, :, cols], wt_sb[:, :, cols], tern_scale[0:KH, n:n + 1], MAGIC,
                                       ALU.mult, ALU.add)
            after(last)
            after(v.tensor_scalar(tern_f[:], tern_f[:], MAGIC, 1.0, ALU.subtract, ALU.min))
            v.tensor_scalar(tern[:], tern_f[:], -1.0, None, ALU.max).then_inc(S["tern_ready"], 1)

            def quantise(g, n, src, gain):
                k = n // 2
                after(v.tensor_tensor(qa[:, gt(g), :], src, on_tiles(gt_sb[:, gain, :]), ALU.mult))
                after(v.tensor_reduce(amax[:, gt(g), 0:1], qa[:, gt(g), :], AX.X, ALU.max, apply_absolute_value=True))
                after(v.tensor_scalar(amax[:, gt(g), 1:2], amax[:, gt(g), 0:1], 1e-5, 1.0 / 127.0, ALU.max, ALU.mult))
                after(v.reciprocal(amax[:, gt(g), 2:3], amax[:, gt(g), 1:2]))
                last = v.tensor_scalar(amax[:, gt(g), 3:4], amax[:, gt(g), 1:2], tern_mean[0:ROWS, k:k + 1], None,
                                       ALU.mult)
                for t in group_tiles(g):
                    last = v.tensor_scalar(qb[:, t, :], qa[:, t, :], amax[:, t, 2:3], 127.0, ALU.mult, ALU.min)
                after(last)
                after(v.tensor_scalar(qb[:, gt(g), :], qb[:, gt(g), :], -128.0, MAGIC, ALU.max, ALU.add))
                v.tensor_scalar(q_int[:, gt(g), :], qb[:, gt(g), :], MAGIC, None, ALU.subtract).then_inc(S["quantised"], 1)

            for g in range(GROUPS):
                statistics(LN_H2, g, h[2][:, gt(g), :])
            for g in range(GROUPS):
                second_moment(RMS_TERN, LN_H2, g)
                after(normalise(LN_H2, g, x3[:, gt(g), :], h[2][:, gt(g), :]))
            for g in range(GROUPS):
                after(normalise(RMS_TERN, g, x3[:, gt(g), :], x3[:, gt(g), :], centre=False))
                quantise(g, g, x3[:, gt(g), :], 0)
                for t in group_tiles(g):
                    if t >= 2:
                        dve.wait_ge(S["dq_done"], t - 1)
                    v.tensor_scalar(diag[:, t % 2, :], ident[0:ROWS, 0:ROWS], amax[:, t, 3:4], None,
                                    ALU.mult).then_inc(S["diag_ready"], 1)
            v.memset(v3[:, :, :, HD1:HD1 + 1], 1.0)
            for g in range(GROUPS):
                dve.wait_ge(S["dq_ready"], g + 1)
                for m in range(3):
                    dve.wait_ge(S["qk3_done"], 3 * g + m + 1)
                    v.tensor_tensor(qk3[:, :, m, gcols(g)], slot_of[("qk3", g, m)][:, :, 0:COLS],
                                    dq[:, gcols(g)].unsqueeze(1).to_broadcast([128, 2, COLS]),
                                    ALU.mult).then_inc(S["qk3_scaled"], 1)
                dve.wait_ge(S["v3_done"], g + 1)
                src = by_tile(slot_of[("v3", g)])
                for i, t in enumerate(group_tiles(g)):
                    last = v.tensor_scalar(v3[:, t, :, 0:HD1], src[:, i, :].rearrange("p (k d) -> p k d", k=HEADS),
                                           amax[:, t, 3:4], None, ALU.mult)
                last.then_inc(S["v3_scaled"], 1)

            def scaled3(t):
                dve.wait_ge(S["attended"], TILES + t + 1)
                src = slot_of[("attend3", t)][0:ROWS, 0, 0:HEADS * 17].rearrange("p (i d) -> p i d", d=17)
                after(v.reciprocal(rsum[:, t, :], src[:, :, HD1]))
                v.tensor_tensor(o3[:, t, :].rearrange("p (i d) -> p i d", d=HD1), src[:, :, 0:HD1],
                                along(rsum[:, t, :], HD1), ALU.mult).then_inc(S["o3_scaled"], 1)

            for t in range(TILES):
                for jp in range(2):
                    src = slot_of[("score3", t, jp)][0:ROWS, :, 0:COLS].rearrange("p b (i x) -> p b i x", x=ROWS)
                    negative_max(TILES + t, jp, (src, 2, 3), 0.25)
                if t >= 1:
                    turned_probs(TILES + t - 1)
                if t >= 2:
                    scaled3(t - 2)
            turned_probs(2 * TILES - 1)
            scaled3(TILES - 2)
            scaled3(TILES - 1)
            for g in range(GROUPS):
                dve.wait_ge(S["o3_scaled"], 3 * g + 3)
                statistics(RMS_PROJ, g, o3[:, gt(g), :], square=True)
            for g in range(GROUPS):
                after(normalise(RMS_PROJ, g, o3[:, gt(g), :], o3[:, gt(g), :], centre=False))
                quantise(g, 2 + g, o3[:, gt(g), :], 1)
            for g in range(GROUPS):
                dve.wait_ge(S["attn3_done"], g + 1)
                src = by_tile(slot_of[("attn3", g)])
                for i, t in enumerate(group_tiles(g)):
                    last = v.scalar_tensor_tensor(h[3][:, t, :], src[:, i, :], amax[:, t, 3:4], h[2][:, t, :],
                                                  ALU.mult, ALU.add)
                last.then_inc(S["h3_ready"], 1)
                dve.wait_ge(S["h3_ready"], g + 1)
                statistics(LN_H3, g, h[3][:, gt(g), :])
            for g in range(GROUPS):
                normalise(LN_H3, g, xn[:, gt(g), :], h[3][:, gt(g), :]).then_inc(S["x_normed"], 1)

            dve.wait_ge(S["w_ff1_loaded"], 80)
            dve.wait_ge(S["logits1_sigmoid"], 2)
            score = lg[:, :, 0:EXPERTS1]
            after(v.tensor_tensor(rt[0][:, :, 0:8], score, on_tiles(gb_sb[:], TILES), ALU.add))
            pairs = rt[0][:, :, 0:8].rearrange("p t (g e) -> p t g e", e=2)
            after(v.memset(rt[1][:], MASKED))
            after(v.tensor_tensor(rt[1][:, :, 0:4], pairs[:, :, :, 0], pairs[:, :, :, 1], ALU.add))

            def two_largest(values, width, hot):
                for t in range(TILES):
                    last = v.max(top[:, t, :], values[:, t, 0:8])
                after(last)
                for t in range(TILES):
                    last = v.max_index(top_i[:, t, :], top[:, t, :], values[:, t, 0:8])
                after(last)
                after(v.tensor_copy(top_f[:], top_i[:, :, 0:2]))
                numbers = on_tiles(const("iota", ROWS)[:, 0:width], TILES)
                v.tensor_tensor(hot, numbers, along(top_f[:, :, 0], width), ALU.is_equal)
                after(v.tensor_tensor(rt[3][:, :, 0:width], numbers, along(top_f[:, :, 1], width), ALU.is_equal))
                after(v.tensor_tensor(hot, hot, rt[3][:, :, 0:width], ALU.add))

            two_largest(rt[1][:], 4, rt[2][:, :, 0:4])
            in_group = along2 = rt[4][:, :, 0:8].rearrange("p t (g e) -> p t g e", e=2)
            v.tensor_copy(in_group[:, :, :, 0], rt[2][:, :, 0:4])
            after(v.tensor_copy(in_group[:, :, :, 1], rt[2][:, :, 0:4]))
            v.tensor_tensor(rt[1][:, :, 0:8], rt[0][:, :, 0:8], rt[4][:, :, 0:8], ALU.mult)
            after(v.tensor_scalar(rt[5][:, :, 0:8], rt[4][:, :, 0:8], -MASKED, MASKED, ALU.mult, ALU.add))
            after(v.tensor_tensor(rt[1][:, :, 0:8], rt[1][:, :, 0:8], rt[5][:, :, 0:8], ALU.add))
            two_largest(rt[1][:], 8, rt[2][:, :, 0:8])
            after(v.tensor_tensor(rt[4][:, :, 0:8], rt[2][:, :, 0:8], score, ALU.mult))
            after(v.tensor_reduce(rden[:, :, 0:1], rt[4][:, :, 0:8], AX.X, ALU.add))
            after(v.tensor_scalar(rden[:, :, 0:1], rden[:, :, 0:1], 1e-6, None, ALU.add))
            after(v.reciprocal(rden[:, :, 1:2], rden[:, :, 0:1]))
            after(v.tensor_tensor(comb1[:], rt[4][:, :, 0:8], along(rden[:, :, 1], 8), ALU.mult))
            for n in range(EXPERTS1 + 2):
                k = EXPERTS0 + n
                if n <= EXPERTS1:
                    hidden(3 * EXPERTS0 + n, k % 2, 0)
                if n >= 1:
                    dve.wait_ge(S["ff_added"], GROUPS * (k - 1))
                    if n == 1:
                        add_expert(k - 1, h[3], lambda t, rows: 1.0)
                    else:
                        add_expert(k - 1, h[3], lambda t, rows: comb1[0:rows, t, n - 2:n - 1])


def constants():
    c = np.zeros((128, CONST_WIDTH), np.float32)

    def put(name, value):
        at, width = CONST_AT[name]
        c[:value.shape[0], at:at + width] = value.reshape(value.shape[0], width)

    put("ident", np.eye(128))
    n = np.arange(128)
    put("swap", np.eye(128)[n ^ 1])
    r = np.arange(ROWS)
    same = r[:, None] // SEQ == r[None, :] // SEQ
    back = r[:, None] - r[None, :]
    put("causal", np.where(same & (back >= 0), 0.0, MASKED))
    put("block", np.where(same, 0.0, MASKED))
    put("ahead", np.where(same & (back <= 0), -back, 0))
    put("keep", (same & (back <= 0)).astype(np.float32))
    put("is_patch", (r % SEQ > 0).astype(np.float32)[:, None])
    put("iota", np.broadcast_to(np.arange(EXPERTS0, dtype=np.float32), (128, EXPERTS0)))
    inverse = (1.0 / np.float32(10000.0) ** (np.arange(0, HD2, 2, dtype=np.float32) / np.float32(HD2))).astype(np.float32)
    angle = np.arange(SEQ, dtype=np.float32)[None, :] * inverse[(n % HD2) // 2][:, None]
    sign = np.where(n % 2 == 0, -1.0, 1.0)[:, None]
    share = np.array([HD2 ** -0.5, 1.0])[None, :, None]
    put("cos", np.cos(angle)[:, None, :] * share)
    put("sin", (sign * np.sin(angle))[:, None, :] * share)
    return c


_OUT = (IMAGES, SEQ, E)


def kernel(**inputs):
    import concourse.bacc as _bacc
    from concourse.bass_utils import run_bass_kernel_spmd as _run

    a = {k: np.asarray(x) for k, x in inputs.items()}
    x = a["x"].reshape(IMAGES, 3, 6, 16, 6, 16).transpose(0, 2, 4, 1, 3, 5).reshape(IMAGES, PATCHES, PD)
    patches = np.zeros((TILES * PER_TILE, SEQ, PD), np.float32)
    patches[:IMAGES, 1:] = x

    def channels_first(w):
        return w.reshape(16, 16, 3, -1).transpose(2, 0, 1, 3).reshape(PD, -1)

    ln1 = np.stack([channels_first(a["L0_tok_ln1_g"])[:, 0], channels_first(a["L0_tok_ln1_b"])[:, 0]])
    pos = a["L0_tok_pos_embed"][0]
    cls_rows = np.zeros((PER_TILE, SEQ, E), np.float32)
    cls_rows[:, 0] = a["L0_tok_cls_token"]

    def padded_heads(w):
        p = np.zeros((w.shape[0], HEADS, 32), np.float32)
        p[:, :, :HD1] = w.reshape(w.shape[0], HEADS, HD1)
        return p.reshape(w.shape[0], 3, 128)

    qkv2 = a["L0_ffn_w_qkv"].reshape(E, HEADS + 2 * KV, HD2)
    pair_heads = [(0, 4), (1, 5), (2, 6), (3, 7), (8, 9), (10, 11), (12, 13), (14, 14)]
    wqk2 = np.stack([np.concatenate([qkv2[:, p], qkv2[:, q]], axis=1) for p, q in pair_heads], axis=1)
    row_heads = [0, 1, 2, 3, 4, 5, 6, 7, 8, 10, 9, 11]
    qkv3 = a["L1_attn_w_qkv"].T
    arrays = {
        "consts": constants(),
        "patches": patches.reshape(TILES, ROWS, PD),
        "w_patch": channels_first(a["L0_tok_W"]),
        "ln1_gb": ln1.reshape(2, PCH, 128).transpose(2, 0, 1),
        "rows_e": np.stack([a["L0_tok_b"], a["L0_tok_ln2_g"], a["L0_tok_ln2_b"], a["L0_attn_ln_w"], a["L0_attn_ln_b"]]),
        "pos_rows": np.concatenate([pos] * PER_TILE),
        "cls_rows": cls_rows.reshape(ROWS, E),
        "slopes": a["L0_attn_log_slope"],
        "wqk1": np.stack([padded_heads(a["L0_attn_Wq"]), padded_heads(a["L0_attn_Wk"])], axis=1),
        "wvo1": np.stack([a["L0_attn_Wv"], a["L0_attn_Wo"]], axis=1),
        "wg1": a["L0_attn_Wg1"],
        "wg2": a["L0_attn_Wg2"],
        "norm_cols": np.stack([a["L0_ffn_norm1_w"], a["L0_ffn_norm2_w"]]).reshape(2, 2, KH).transpose(2, 1, 0),
        "wqk2": wqk2,
        "wv2": qkv2[:, HEADS + KV:].reshape(E, E),
        "wout2": a["L0_ffn_w_out"].reshape(HEADS, HD2, E)[row_heads].reshape(HEADS * HD2, E),
        "wrouter0": a["L0_ffn_w_router"],
        "w_gate_up": a["L0_ffn_w_gate_up"],
        "w_down": a["L0_ffn_w_down"],
        "w_tern": np.concatenate([padded_heads(qkv3[:, :E]).reshape(E, 384), padded_heads(qkv3[:, E:2 * E]).reshape(E, 384),
                                  qkv3[:, 2 * E:], a["L1_attn_w_proj"].T], axis=1),
        "g_tern": np.stack([a["L1_attn_g_qkv"], a["L1_attn_g_proj"]]),
        "w_gate1": a["L1_ffn_gate_weight"].T,
        "gate_bias": a["L1_ffn_gate_bias"],
        "w13": np.concatenate([np.concatenate([a["L1_ffn_w1"], a["L1_ffn_sw1"][None]]).transpose(0, 2, 1),
                               np.concatenate([a["L1_ffn_w3"], a["L1_ffn_sw3"][None]]).transpose(0, 2, 1)], axis=2),
        "w2": np.concatenate([a["L1_ffn_w2"], a["L1_ffn_sw2"][None]]).transpose(0, 2, 1),
    }
    nc = _bacc.Bacc("TRN2", target_bir_lowering=False, num_devices=1)
    args = []
    for name, value in arrays.items():
        arrays[name] = value = np.ascontiguousarray(value)
        args.append(nc.dram_tensor(name, value.shape, mybir.dt.from_np(value.dtype), kind="ExternalInput").ap())
    out = nc.dram_tensor("out", (TOKENS, E), F32, kind="ExternalOutput").ap()
    vit_tower(nc, *args, out)
    r = _run(nc, [arrays], core_ids=[0])
    return r.results[0]["out"].reshape(_OUT)
```

```python
from contextlib import ExitStack

import numpy as np

import concourse.bass as bass
from concourse import mybir

ALU = mybir.AluOpType
ACT = mybir.ActivationFunctionType
AX = mybir.AxisListType
F32 = mybir.dt.float32
BF16 = mybir.dt.bfloat16
U32 = mybir.dt.uint32

IMAGES = 16
PATCHES = 36
SEQ = PATCHES + 1
PER_TILE = 3
ROWS = PER_TILE * SEQ
TILES = -(-IMAGES // PER_TILE)
GROUP = 3
GROUPS = TILES // GROUP
COLS = GROUP * ROWS
TOKENS = IMAGES * SEQ
E = 192
KH = E // 2
PD = 768
PCH = PD // 128
HEADS = 12
HD1 = E // HEADS
HD2 = 64
KV = 3
REP = HEADS // KV
EXPERTS0, FF0 = 16, 384
EXPERTS1, FF1 = 8, 128
MASKED = -1e30
MAGIC = 1.5 * 2.0 ** 23
RING = 4

BLOCK = 128
ASSIGNED = 2 * TOKENS
BLOCKS = (ASSIGNED + EXPERTS0 * (BLOCK - 1)) // BLOCK
OVERFLOW = BLOCKS - EXPERTS0
MORE = -(-TOKENS // BLOCK) - 1
SLOTS = BLOCKS * BLOCK
STAGES = {"first": range(EXPERTS0 + 3), "late": range(EXPERTS0 + 3, BLOCKS)}

CONST_PARTS = (("ident", 128), ("swap", 128), ("causal", ROWS), ("block", ROWS), ("ahead", ROWS),
               ("keep", ROWS), ("is_patch", 1), ("iota", EXPERTS0), ("cos", 2 * SEQ), ("sin", 2 * SEQ),
               ("before", 128), ("is_one", EXPERTS0), ("own_slot", EXPERTS0), ("over_slot", EXPERTS0), ("steps", MORE),
               ("block_no", OVERFLOW))
CONST_AT = {}
_at = 0
for _name, _width in CONST_PARTS:
    CONST_AT[_name] = (_at, _width)
    _at += _width
CONST_WIDTH = _at

LN_PATCH, LN_EMBED, LN_H0, LN_DECAY, LN_H1, RMS_GQA, RMS_MOE, LN_H2, RMS_TERN, RMS_PROJ, LN_H3 = range(11)
NORMS = 11
EPS = {n: 1e-6 if n in (RMS_GQA, RMS_MOE) else 1e-5 for n in range(NORMS)}


def live_cols(g):
    return min(COLS, TOKENS - g * COLS)


class Semaphores(dict):

    def __init__(self, nc, ctx):
        super().__init__()
        self.nc, self.ctx = nc, ctx

    def __missing__(self, name):
        self[name] = self.ctx.enter_context(self.nc.semaphore(name))
        return self[name]


def vit_tower(nc, consts, patches, w_patch, ln1_gb, rows_e, pos_rows, cls_rows, slopes, wqk1, wvo1, wg1, wg2,
              norm_cols, wqk2, wv2, wout2, wrouter0, w_gate_up, w_down, w_tern, g_tern, w_gate1, gate_bias,
              w13, w2, out):
    with ExitStack() as ctx:
        S = Semaphores(nc, ctx)

        def sb(name, shape, dt=F32):
            return ctx.enter_context(nc.sbuf_tensor(name, shape, dt))

        c_sb = sb("consts_sb", [128, CONST_WIDTH])
        xs_dram = nc.dram_tensor("xs_dram", (SLOTS, E), F32, kind="Internal").ap()
        ys_dram = nc.dram_tensor("ys_dram", (SLOTS, E), F32, kind="Internal").ap()
        ln1_sb = sb("ln1_gb_sb", [128, 2, PCH])
        re_sb = sb("rows_e_sb", [ROWS, 5, E])
        slope_sb = sb("slope_sb", [ROWS, HEADS])
        wqk1_sb = sb("wqk1_sb", [KH, 2, 2, 3, 128])
        wvo1_sb = sb("wvo1_sb", [KH, 2, 2, E])
        wg1_sb = sb("wg1_sb", [KH, 2, 16])
        wg2_sb = sb("wg2_sb", [16, E])
        ncol_sb = sb("norm_cols_sb", [KH, 2, 2])
        wqk2_sb = sb("wqk2_sb", [KH, 2, 8, 128])
        wv2_sb = sb("wv2_sb", [KH, 2, E])
        wout2_sb = sb("wout2_sb", [128, 6, E])
        wr0_sb = sb("wr0_sb", [KH, 2, EXPERTS0])
        wt_sb = sb("w_tern_sb", [KH, 2, 5 * E + E])
        gt_sb = sb("g_tern_sb", [ROWS, 2, E])
        wr1_sb = sb("wr1_sb", [KH, 2, EXPERTS1])
        gb_sb = sb("gate_bias_sb", [ROWS, EXPERTS1])
        UP_SLOTS, DOWN_SLOTS = 3, 4

        def const(name, rows=128):
            at, width = CONST_AT[name]
            return c_sb[0:rows, at:at + width]

        ident = const("ident")

        decay = sb("decay", [ROWS, 4, 3, ROWS])
        ident_bf = sb("ident_bf", [128, 128], BF16)
        causal_bf = sb("causal_bf", [ROWS, ROWS], BF16)
        block_bf = sb("block_bf", [ROWS, ROWS], BF16)
        ones = sb("ones", [128, 128])
        half_neg = sb("half_neg", [ROWS, TILES])
        tern = sb("tern", [KH, 2, 6 * E], BF16)
        tern_f = wt_sb
        tern_abs = sb("tern_abs", [KH, 2])
        tern_mean = sb("tern_mean", [128, 2])
        tern_scale = sb("tern_scale", [128, 2])

        area_a = sb("area_a", [128, TILES * PD])
        area_b = sb("area_b", [128, PCH * TILES * ROWS])
        area_c = sb("area_c", [128, 8 * TILES * ROWS])
        area_d = sb("area_d", [128, 12 * COLS])

        def part(area, at, rows, pattern, **sizes):
            n = 1
            for size in sizes.values():
                n *= size
            return area[0:rows, at:at + n].rearrange(f"rows ({pattern}) -> rows {pattern}", **sizes)

        patch_x = part(area_a, 0, ROWS, "t n", t=TILES, n=PD)
        w13_sb = part(area_a, 0, KH, "c e n", c=2, e=EXPERTS1 + 1, n=2 * FF1)
        patch_t = part(area_b, 0, 128, "c n", c=PCH, n=TILES * ROWS)
        w2_sb = part(area_b, 0, FF1, "e n", e=EXPERTS1 + 1, n=E)
        stats = sb("stats", [ROWS, TILES, 2, 6])
        mv = sb("mean_var", [ROWS, NORMS, TILES, 2])
        ve = sb("var_eps", [ROWS, NORMS, TILES])
        vt = sb("var_tmp", [ROWS, NORMS, TILES])
        rstd = sb("rstd", [ROWS, NORMS, TILES])
        y0 = sb("y0", [ROWS, TILES, E])
        z0 = sb("z0", [ROWS, TILES, E])
        h = [sb(f"h{n}", [ROWS, TILES, E]) for n in range(3)]
        h.append(h[0])
        xn = sb("xn", [ROWS, TILES, E])
        x_t = sb("x_t", [KH, 2, TILES * ROWS])
        qk1 = part(area_c, 0, 128, "a m n", a=2, m=3, n=TILES * ROWS)
        v1 = part(area_d, 0, ROWS, "t n", t=TILES, n=E)
        gate1 = part(area_d, TILES * E, ROWS, "t n", t=TILES, n=E)
        g1_t = area_d[0:16, 2 * TILES * E:2 * TILES * E + TILES * ROWS]
        o_rows = sb("o_rows", [ROWS, TILES, E])
        PB = 3
        area_e = sb("area_e", [128, 2 * PB * HEADS * ROWS])
        p_buf = part(area_e, 0, ROWS, "s p n", s=PB, p=HEADS, n=ROWS)
        pt_buf = part(area_e, PB * HEADS * ROWS, ROWS, "s p n", s=PB, p=HEADS, n=ROWS)
        wp_sb = part(area_e, 0, 128, "c n", c=PCH, n=E)
        pos_sb, cls_sb, gm_rows, add_rows = (area_e[0:ROWS, (PCH + n) * E:(PCH + n + 1) * E] for n in range(4))
        wgu_sb = part(area_e, 0, KH, "s c n", s=UP_SLOTS, c=2, n=2 * FF0)
        wdn_sb = part(area_e, UP_SLOTS * 4 * FF0, 128, "s c n", s=DOWN_SLOTS, c=3, n=E)
        x2 = y0
        raw, rsin, rcos = (part(area_d, 4 * n * COLS, 128, "s b n", s=2, b=2, n=COLS) for n in range(3))
        qk2 = part(area_c, 0, 128, "m n", m=8, n=TILES * ROWS)
        v2 = sb("v2", [ROWS, TILES, KV, HD2 + 1])
        nmax = sb("nmax", [ROWS, TILES, HEADS])
        rsum = sb("rsum", [ROWS, TILES, HEADS])
        o2 = patch_x
        o2_t = patch_t
        hh = z0
        m_t = x_t
        lg = sb("lg", [ROWS, TILES, EXPERTS0])
        top = sb("top", [ROWS, TILES, 8])
        top_i = sb("top_i", [ROWS, TILES, 8], U32)
        top_f = sb("top_f", [ROWS, TILES, 2])
        zeros = sb("zeros", [128, E])
        before_bf = sb("before_bf", [128, 128], BF16)
        ones_bf = sb("ones_bf", [128, 128], BF16)
        hot = sb("hot", [ROWS, 2, TILES, EXPERTS0])
        hot_bf = sb("hot_bf", [ROWS, TILES, EXPERTS0], BF16)
        over = sb("over", [ROWS, EXPERTS0, MORE])
        share = sb("share", [ROWS, 4, EXPERTS0])
        slot_f = sb("slot_f", [ROWS, 2, TILES, 1])
        slot_u = sb("slot_u", [ROWS, 2, TILES], U32)
        over_f = sb("over_f", [1, OVERFLOW, EXPERTS0])
        over_n = sb("over_n", [1, OVERFLOW])
        over_u = sb("over_u", [1, OVERFLOW], U32)
        used_u = sb("used_u", [1, 1], U32)
        pair_w = sb("pair_w", [ROWS, 2, TILES])
        rt = [sb(f"rt{n}", [ROWS, TILES, EXPERTS0]) for n in range(6)]
        rden = sb("rden", [ROWS, TILES, 2])
        XB, YB = 3, 3
        xb = part(area_c, 0, 128, "s n", s=XB, n=E)
        xb_t = part(area_c, XB * E, KH, "s c n", s=2, c=2, n=BLOCK)
        sb_silu = part(area_c, XB * E + 512, 128, "s n", s=2, n=FF0)
        hid_t = part(area_c, XB * E + 512 + 4 * FF0, 128, "s c n", s=2, c=3, n=BLOCK)
        yb = part(area_c, XB * E + 512 + 6 * FF0, 128, "s n", s=YB, n=E)
        yg = part(area_d, 0, ROWS, "k t n", k=2, t=TILES, n=E)
        silu_buf = part(area_c, 0, 128, "s n", s=2, n=TOKENS)
        hid = part(area_c, 2 * TOKENS, 128, "s c n", s=2, c=3, n=TOKENS)

        x3 = xn
        amax = sb("amax", [ROWS, TILES, 4])
        q_int = sb("q_int", [ROWS, TILES, E], BF16)
        q_int_t = area_d[0:KH, 4 * COLS:6 * COLS].bitcast(BF16).rearrange("p (c n) -> p c n", c=2)
        qa = y0
        qb = z0
        diag = part(area_d, 6 * COLS + TILES * HEADS * (HD1 + 1), ROWS, "s n", s=2, n=ROWS)
        dq = area_d[:, 0:TILES * ROWS]
        qk3 = qk1
        v3 = part(area_d, 6 * COLS, ROWS, "t h n", t=TILES, h=HEADS, n=HD1 + 1)
        o3 = o_rows
        comb1 = sb("comb1", [ROWS, TILES, EXPERTS1])

        psum = [ctx.enter_context(nc.psum_tensor(f"slot{n}", [128, 2, 512], F32)) for n in range(RING)]

        def by_tile(slot, width=E, rows=ROWS):
            return slot[:].rearrange("p b (s x) -> p (b s) x", s=2)[0:rows, 0:GROUP, 0:width]

        def tile_cols(t):
            return slice(t * ROWS, (t + 1) * ROWS)

        def group_tiles(g):
            return range(g * GROUP, (g + 1) * GROUP)

        def gt(g):
            return slice(g * GROUP, (g + 1) * GROUP)

        def gcols(g, n=COLS):
            return slice(g * COLS, g * COLS + n)

        def on_tiles(ap, n=GROUP):
            return ap.unsqueeze(1).to_broadcast([ap.shape[0], n, ap.shape[1]])

        def along(ap, n):
            return ap.unsqueeze(2).to_broadcast([ap.shape[0], ap.shape[1], n])

        slot_of = {}
        ring = {"uses": 0, "freed": [[] for _ in range(RING)]}

        def take(pe, key, *freed_by):
            n = ring["uses"] % RING
            for s, value in ring["freed"][n]:
                pe.wait_ge(S[s], value)
            ring["freed"][n] = list(freed_by)
            ring["uses"] += 1
            slot_of[key] = psum[n]
            return psum[n]

        def nth(norm, g):
            return GROUPS * norm + g + 1

        def late_needed(engine):
            used = engine.value_load(used_u[0:1, 0:1], min_val=0, max_val=OVERFLOW)
            return used > len(STAGES["first"]) - EXPERTS0

        block = ctx.enter_context(nc.Block())

        @block.tensor
        def _(pe):
            mm, tr = nc.tensor.matmul, nc.tensor.transpose

            def rows_to_columns(src, g, key, ready, *freed_by):
                slot = take(pe, key, *freed_by)
                for c in range(2):
                    for i, t in enumerate(group_tiles(g)):
                        last = tr(slot[0:KH, c, i * ROWS:(i + 1) * ROWS], src[:, t, c * KH:(c + 1) * KH],
                                  ident[0:ROWS, 0:ROWS])
                last.then_inc(S[ready], 1)

            def project_rows(lhs, w, g, key, ready, *freed_by):
                slot = take(pe, key, *freed_by)
                for i, t in enumerate(group_tiles(g)):
                    for c in range(2):
                        last = mm(by_tile(slot, w.shape[2])[:, i, :], lhs[:, c, tile_cols(t)], w[:, c, :],
                                  start=(c == 0), stop=(c == 1))
                last.then_inc(S[ready], 1)

            pe.wait_ge(S["consts_loaded"], 16)
            for g in range(GROUPS):
                pe.wait_ge(S["patch_normed"], g + 1)
                for u in range(PCH // 2):
                    slot = take(pe, ("patch_t", g, u), ("patch_t_dve", g * 3 + u + 1), ("patch_t_act", g * 3 + u + 1))
                    for b in range(2):
                        c = 2 * u + b
                        for i, t in enumerate(group_tiles(g)):
                            last = tr(slot[:, b, i * ROWS:(i + 1) * ROWS], patch_x[:, t, c * 128:(c + 1) * 128],
                                      ident[0:ROWS, 0:ROWS])
                    last.then_inc(S["patch_turned"], 1)
            pe.wait_ge(S["w_patch_loaded"], 16)
            for g in range(GROUPS):
                pe.wait_ge(S["patch_t_dve"], 3 * g + 3)
                pe.wait_ge(S["patch_t_act"], 3 * g + 3)
                slot = take(pe, ("embed", g), ("embed_biased", g + 1))
                for i, t in enumerate(group_tiles(g)):
                    for c in range(PCH):
                        last = mm(by_tile(slot)[:, i, :], patch_t[:, c, tile_cols(t)], wp_sb[:, c, :],
                                  start=(c == 0), stop=(c == PCH - 1))
                last.then_inc(S["embed_done"], 1)

            pe.wait_ge(S["w_attn1_loaded"], 64)
            for g in range(GROUPS):
                pe.wait_ge(S["x_normed"], g + 1)
                rows_to_columns(xn, g, ("x0_t", g), "x_turned", ("x_t_ready", g + 1))
            for g in range(GROUPS):
                pe.wait_ge(S["x_t_ready"], g + 1)
                for m in range(3):
                    slot = take(pe, ("qk1", g, m), ("qk1_silu", 3 * g + m + 1))
                    for b in range(2):
                        for c in range(2):
                            last = mm(slot[:, b, 0:COLS], wqk1_sb[:, c, b, m, :], x_t[:, c, gcols(g)],
                                      start=(c == 0), stop=(c == 1))
                    last.then_inc(S["qk1_done"], 1)
                project_rows(x_t, wvo1_sb[:, :, 0, :], g, ("v1", g), "v1_done", ("v1_silu", g + 1))
                slot = take(pe, ("g1", g), ("g1_copied", g + 1))
                for c in range(2):
                    last = mm(slot[0:16, 0, 0:COLS], wg1_sb[:, c, :], x_t[:, c, gcols(g)], start=(c == 0), stop=(c == 1))
                last.then_inc(S["g1_done"], 1)
                pe.wait_ge(S["g1_copied"], g + 1)
                slot = take(pe, ("gate1", g), ("gate1_tanh", g + 1))
                for i, t in enumerate(group_tiles(g)):
                    last = mm(by_tile(slot)[:, i, :], g1_t[:, tile_cols(t)], wg2_sb[:], start=True, stop=True)
                last.then_inc(S["gate1_done"], 1)

            def energies(t):
                for jp in range(2):
                    slot = take(pe, ("energy", t, jp), ("energy_decayed", 2 * t + jp + 1))
                    for m in range(3):
                        for b in range(2):
                            r = 32 * (2 * jp + b)
                            last = mm(slot[0:ROWS, b, m * ROWS:(m + 1) * ROWS], qk1[r:r + 32, 1, m, tile_cols(t)],
                                      qk1[r:r + 32, 0, m, tile_cols(t)], start=True, stop=True)
                    last.then_inc(S["energy_done"], 1)

            def decay_values(t):
                g, i = divmod(t, GROUP)
                if i == 0:
                    take(pe, ("decay_out", g), ("o1_gated", g + 1))
                slot = slot_of[("decay_out", g)]
                pe.wait_ge(S["energy_decayed"], 2 * t + 2)
                for hd in range(HEADS):
                    m, j = divmod(hd, 4)
                    last = mm(by_tile(slot)[:, i, hd * HD1:(hd + 1) * HD1],
                              p_buf[:, t % PB, j * 3 + m, :], v1[:, t, hd * HD1:(hd + 1) * HD1], start=True, stop=True)
                last.then_inc(S["decay_out_done"], 1)

            for g in range(GROUPS):
                pe.wait_ge(S["qk1_silu"], 3 * g + 3)
                pe.wait_ge(S["v1_silu"], g + 1)
                for i, t in enumerate(group_tiles(g)):
                    energies(t)
                    if i:
                        decay_values(t - 1)
                decay_values(t)
            for g in range(GROUPS):
                pe.wait_ge(S["o1_gated"], g + 1)
                rows_to_columns(o_rows, g, ("o1_t", g), "o1_turned", ("o1_t_ready", g + 1))
            for g in range(GROUPS):
                pe.wait_ge(S["o1_t_ready"], g + 1)
                project_rows(x_t, wvo1_sb[:, :, 1, :], g, ("attn1", g), "attn1_done", ("attn1_normed", g + 1))

            pe.wait_ge(S["w_attn2_loaded"], 64)
            for g in range(GROUPS):
                pe.wait_ge(S["x_normed"], 2 + g + 1)
                rows_to_columns(xn, g, ("x1_t", g), "x_turned", ("x_t_ready", 2 + g + 1))

            def project_qk2(g, u):
                n = 4 * g + u
                slot = take(pe, ("qk2", g, u), ("qk2_raw", n + 1))
                for b in range(2):
                    for c in range(2):
                        last = mm(slot[:, b, 0:COLS], wqk2_sb[:, c, 2 * u + b, :], x_t[:, c, gcols(g)],
                                  start=(c == 0), stop=(c == 1))
                last.then_inc(S["qk2_done"], 1)

            def swap_qk2(g, u):
                n = 4 * g + u
                pe.wait_ge(S["qk2_raw"], n + 1)
                slot = take(pe, ("swap", g, u), ("qk2_sin", n + 1))
                for b in range(2):
                    last = mm(slot[:, b, 0:COLS], const("swap"), raw[:, n % 2, b, :], start=True, stop=True)
                last.then_inc(S["qk2_swapped"], 1)

            for g in range(GROUPS):
                pe.wait_ge(S["x_t_ready"], 2 + g + 1)
                for u in range(4):
                    project_qk2(g, u)
                    if u:
                        swap_qk2(g, u - 1)
                project_rows(x_t, wv2_sb, g, ("v2", g), "v2_done", ("v2_copied", g + 1))
                swap_qk2(g, 3)

            pe.wait_ge(S["masks_made"], 1)

            def masked_scores2(t):
                for u, heads in enumerate((REP, 2)):
                    slot = take(pe, ("score2", t, u), ("probs", 2 * t + u + 1))
                    for b in range(2):
                        mm(slot[0:ROWS, b, 0:heads * ROWS], ident_bf[0:ROWS, 0:ROWS],
                           on_tiles(causal_bf[:], heads), start=True, stop=False, skip_group_check=True)
                    for i in range(heads):
                        for b in range(2):
                            q, k = (i, 6) if u == 0 else (4 + i, 7)
                            r = 64 * b
                            last = mm(slot[0:ROWS, b, i * ROWS:(i + 1) * ROWS], qk2[r:r + 64, q, tile_cols(t)],
                                      qk2[r:r + 64, k, tile_cols(t)], start=False, stop=True, skip_group_check=True)
                    last.then_inc(S["score_done"], 1)

            def turn_probs(base, t):
                for u, heads in enumerate((8, 4)):
                    n = base + t
                    slot = take(pe, ("probs_t", n, u), ("probs_t_dve" if u == 0 else "probs_t_act", n + 1))
                    pe.wait_ge(S["probs"], 2 * n + 2)
                    for i in range(heads):
                        last = tr(slot[0:ROWS, i // 4, (i % 4) * ROWS:(i % 4 + 1) * ROWS],
                                  p_buf[:, (TILES + n) % PB, 8 * u + i, :], ident[0:ROWS, 0:ROWS])
                    last.then_inc(S["probs_turned"], 1)

            def attend2(t):
                pe.wait_ge(S["probs_t_dve"], t + 1)
                pe.wait_ge(S["probs_t_act"], t + 1)
                slot = take(pe, ("attend2", t), ("o2_scaled", t + 1))
                for p in range(HEADS):
                    kv = p // 4
                    at = (p % 6) * (HD2 + 1)
                    last = mm(slot[0:ROWS, p // 6, at:at + HD2 + 1], pt_buf[:, t % PB, p, :], v2[:, t, kv, :],
                              start=True, stop=True)
                last.then_inc(S["attended"], 1)

            for g in range(GROUPS):
                pe.wait_ge(S["qk2_rotated"], 4 * g + 4)
                pe.wait_ge(S["v2_copied"], g + 1)
                for i, t in enumerate(group_tiles(g)):
                    masked_scores2(t)
                    if t >= 1:
                        turn_probs(0, t - 1)
                    if t >= 2:
                        attend2(t - 2)
            turn_probs(0, TILES - 1)
            attend2(TILES - 2)
            attend2(TILES - 1)
            for g in range(GROUPS):
                pe.wait_ge(S["o2_scaled"], 3 * g + 3)
                for u in range(3):
                    slot = take(pe, ("o2_t", g, u), ("o2_t_dve" if u % 2 else "o2_t_act", 3 * g + u + 1))
                    for b in range(2):
                        for i, t in enumerate(group_tiles(g)):
                            c = 2 * u + b
                            last = tr(slot[:, b, i * ROWS:(i + 1) * ROWS], o2[:, t, c * 128:(c + 1) * 128],
                                      ident[0:ROWS, 0:ROWS])
                    last.then_inc(S["o2_turned"], 1)
            for g in range(GROUPS):
                pe.wait_ge(S["o2_t_act"], 3 * g + 3)
                pe.wait_ge(S["o2_t_dve"], 3 * g + 2)
                slot = take(pe, ("attn2", g), ("hh_ready", g + 1))
                for i, t in enumerate(group_tiles(g)):
                    for c in range(6):
                        last = mm(by_tile(slot)[:, i, :], o2_t[:, c, tile_cols(t)], wout2_sb[:, c, :],
                                  start=(c == 0), stop=(c == 5))
                last.then_inc(S["attn2_done"], 1)

            for g in range(GROUPS):
                pe.wait_ge(S["x_normed"], 4 + g + 1)
                rows_to_columns(xn, g, ("m_t", g), "x_turned", ("m_t_ready", g + 1))
            for g in range(GROUPS):
                pe.wait_ge(S["m_t_ready"], g + 1)
                project_rows(m_t, wr0_sb, g, ("logits0", g), "logits0_done", ("logits0_copied", g + 1))

            def feed_up(n, w, sub, columns):
                for part in range(2):
                    slot = take(pe, ("ff", n, part), ("ff_silu" if part == 0 else "ff_hidden", n + 1))
                    for c in range(2):
                        for g in range(GROUPS):
                            last = mm(slot[:, g, 0:live_cols(g)], w(c, part), columns[:, c, gcols(g, live_cols(g))],
                                      start=(c == 0), stop=(c == 1))
                    last.then_inc(S["ff_up"], 1)

            def feed_down(n, down, pieces, hidden_after):
                for g in range(GROUPS):
                    slot = take(pe, ("down", n, g), ("ff_added", GROUPS * n + g + 1))
                    pe.wait_ge(S["ff_hidden"], hidden_after)
                    for i, t in enumerate(group_tiles(g)):
                        rows = min(ROWS, TOKENS - t * ROWS)
                        for c in range(pieces):
                            last = mm(by_tile(slot, rows=rows)[:, i, :], hid[:, n % 2, c, t * ROWS:t * ROWS + rows],
                                      down[:, c, :], start=(c == 0), stop=(c == pieces - 1))
                    last.then_inc(S["ff_down"], 1)

            pe.wait_ge(S["hot_ready"], 1)
            slot = take(pe, "ranks", ("slots_ready", 1))
            for t in range(TILES + 1):
                at = slot[0:ROWS, 0, t * EXPERTS0:(t + 1) * EXPERTS0]
                for u in range(min(t + 1, TILES)):
                    rows = min(ROWS, TOKENS - u * ROWS)
                    last = mm(at, (before_bf if u == t else ones_bf)[0:rows, 0:ROWS], hot_bf[0:rows, u, :],
                              start=(u == 0), stop=(u == min(t, TILES - 1)))
            last.then_inc(S["ranks_done"], 1)

            def run_blocks(when):
                blocks = STAGES[when]

                def turn_block(n):
                    pe.wait_ge(S[f"{when}_in{n % XB}"], 16 * (n // XB + 1))
                    slot = take(pe, (when, "turned", n), (f"{when}_columns", n + 1))
                    for c in range(2):
                        last = tr(slot[0:KH, 0, c * BLOCK:(c + 1) * BLOCK], xb[:, n % XB, c * KH:(c + 1) * KH], ident)
                    last.then_inc(S[f"{when}_turned"], 1)

                def block_up(n):
                    pe.wait_ge(S[f"{when}_columns"], n + 1)
                    pe.wait_ge(S[f"{when}_up_loaded{n % UP_SLOTS}"], 16 * (n // UP_SLOTS + 1))
                    slot = take(pe, (when, "up", n), (f"{when}_hidden", n + 1))
                    for gate_or_up in range(2):
                        for m in range(FF0 // 128):
                            at = gate_or_up * FF0 + m * 128
                            for c in range(2):
                                last = mm(slot[:, gate_or_up, m * BLOCK:(m + 1) * BLOCK],
                                          wgu_sb[:, n % UP_SLOTS, c, at:at + 128], xb_t[:, n % 2, c, :],
                                          start=(c == 0), stop=(c == 1))
                        last.then_inc(S[f"{when}_up"], 1)

                def block_down(n):
                    pe.wait_ge(S[f"{when}_hidden"], n + 1)
                    pe.wait_ge(S[f"{when}_down_loaded{n % DOWN_SLOTS}"], 16 * (n // DOWN_SLOTS + 1))
                    slot = take(pe, (when, "down", n), (f"{when}_out", n + 1))
                    for c in range(3):
                        last = mm(slot[:, 0, 0:E], hid_t[:, n % 2, c, :], wdn_sb[:, n % DOWN_SLOTS, c, :],
                                  start=(c == 0), stop=(c == 2))
                    last.then_inc(S[f"{when}_down"], 1)

                turn_block(0)
                for n in range(len(blocks) + 1):
                    if n + 1 < len(blocks):
                        turn_block(n + 1)
                    if n < len(blocks):
                        block_up(n)
                    if n >= 1:
                        block_down(n - 1)
                pe.wait_ge(S[f"{when}_out"], len(blocks))
                ring["freed"] = [[] for _ in range(RING)]

            pe.wait_ge(S["slots_ready"], 1)
            late = late_needed(pe)
            run_blocks("first")
            with pe.If(late):
                run_blocks("late")

            pe.wait_ge(S["tern_summed"], 2)
            slot = take(pe, "tern_sum", ("tern_mean_ready", 1))
            mm(slot[:, 0, 0:2], ones[0:KH, :], tern_abs[:], start=True, stop=True).then_inc(S["tern_sum_done"], 1)

            def turn_ints(g, n):
                pe.wait_ge(S["quantised"], n + 1)
                slot = take(pe, ("ints_t", n), ("ints_t_ready", n + 1))
                view = slot[:].bitcast(BF16)
                for c in range(2):
                    for i, t in enumerate(group_tiles(g)):
                        last = tr(view[0:KH, c, i * 112:i * 112 + ROWS], q_int[:, t, c * KH:(c + 1) * KH],
                                  ident_bf[0:ROWS, 0:ROWS])
                last.then_inc(S["ints_turned"], 1)

            for g in range(GROUPS):
                turn_ints(g, g)
                slot = take(pe, ("dq", g), ("dq_ready", g + 1))
                for i, t in enumerate(group_tiles(g)):
                    pe.wait_ge(S["diag_ready"], t + 1)
                    last = mm(slot[:, 0, i * ROWS:(i + 1) * ROWS], ones[0:ROWS, :], diag[:, t % 2, :],
                              start=True, stop=True)
                    last.then_inc(S["dq_done"], 1)
            pe.wait_ge(S["tern_ready"], 1)
            for g in range(GROUPS):
                pe.wait_ge(S["ints_t_ready"], g + 1)
                for m in range(3):
                    slot = take(pe, ("qk3", g, m), ("qk3_scaled", 3 * g + m + 1))
                    for b in range(2):
                        for c in range(2):
                            at = b * 384 + m * 128
                            last = mm(slot[:, b, 0:COLS], tern[:, c, at:at + 128], q_int_t[:, c, gcols(g)],
                                      start=(c == 0), stop=(c == 1))
                    last.then_inc(S["qk3_done"], 1)
                project_rows(q_int_t, tern[:, :, 768:960], g, ("v3", g), "v3_done", ("v3_scaled", g + 1))

            def masked_scores3(t):
                n = TILES + t
                for jp in range(2):
                    slot = take(pe, ("score3", t, jp), ("probs", 2 * n + jp + 1))
                    for b in range(2):
                        mm(slot[0:ROWS, b, 0:COLS], ident_bf[0:ROWS, 0:ROWS], on_tiles(block_bf[:], 3),
                           start=True, stop=False, skip_group_check=True)
                    for m in range(3):
                        for b in range(2):
                            r = 32 * (2 * jp + b)
                            last = mm(slot[0:ROWS, b, m * ROWS:(m + 1) * ROWS], qk3[r:r + 32, 0, m, tile_cols(t)],
                                      qk3[r:r + 32, 1, m, tile_cols(t)], start=False, stop=True, skip_group_check=True)
                    last.then_inc(S["score_done"], 1)

            def attend3(t):
                n = TILES + t
                pe.wait_ge(S["probs_t_dve"], n + 1)
                pe.wait_ge(S["probs_t_act"], n + 1)
                slot = take(pe, ("attend3", t), ("o3_scaled", t + 1))
                for p in range(HEADS):
                    hd = (p % 3) * 4 + p // 3
                    last = mm(slot[0:ROWS, 0, hd * 17:hd * 17 + 17], pt_buf[:, n % PB, p, :], v3[:, t, hd, :],
                              start=True, stop=True)
                last.then_inc(S["attended"], 1)

            for g in range(GROUPS):
                pe.wait_ge(S["qk3_scaled"], 3 * g + 3)
                pe.wait_ge(S["v3_scaled"], g + 1)
                for i, t in enumerate(group_tiles(g)):
                    masked_scores3(t)
                    if t >= 1:
                        turn_probs(TILES, t - 1)
                    if t >= 2:
                        attend3(t - 2)
            turn_probs(TILES, TILES - 1)
            attend3(TILES - 2)
            attend3(TILES - 1)
            for g in range(GROUPS):
                turn_ints(g, 2 + g)
            for g in range(GROUPS):
                pe.wait_ge(S["ints_t_ready"], 2 + g + 1)
                project_rows(q_int_t, tern[:, :, 960:1152], g, ("attn3", g), "attn3_done", ("h3_ready", g + 1))

            pe.wait_ge(S["w_ff1_loaded"], 80)
            for g in range(GROUPS):
                pe.wait_ge(S["x_normed"], 6 + g + 1)
                rows_to_columns(xn, g, ("x4_t", g), "x_turned", ("x_t_ready", 4 + g + 1))
            for g in range(GROUPS):
                pe.wait_ge(S["x_t_ready"], 4 + g + 1)
                project_rows(x_t, wr1_sb, g, ("logits1", g), "logits1_done", ("logits1_sigmoid", g + 1))
            order = [EXPERTS1] + list(range(EXPERTS1))
            for n in range(EXPERTS1 + 2):
                if n <= EXPERTS1:
                    e = order[n]
                    feed_up(n, lambda c, part: w13_sb[:, c, e, part * FF1:(part + 1) * FF1], 0, x_t)
                if n >= 1:
                    feed_down(n - 1, w2_sb[:, order[n - 1]].unsqueeze(1), 1, n)

        @block.sync
        def _(sp):
            def load(dst, src, sem):
                sp.dma_start(dst, src).then_inc(S[sem], 16)

            for t in range(TILES):
                load(patch_x[:, t, :], patches[t], f"patch_loaded{t // GROUP}")
            load(c_sb[:], consts, "consts_loaded")
            load(ln1_sb[:], ln1_gb, "ln1_loaded")
            load(wp_sb[:], w_patch.rearrange("(c p) e -> p c e", p=128), "w_patch_loaded")
            load(re_sb[:], rows_e.unsqueeze(0).to_broadcast([ROWS, 5, E]), "rows_loaded")
            load(pos_sb[:], pos_rows, "rows_loaded")
            load(cls_sb[:], cls_rows, "rows_loaded")
            load(slope_sb[:], slopes.unsqueeze(0).to_broadcast([ROWS, HEADS]), "slopes_loaded")
            load(wqk1_sb[:], wqk1.rearrange("(c p) a m n -> p c a m n", p=KH), "w_attn1_loaded")
            load(wvo1_sb[:], wvo1.rearrange("(c p) a n -> p c a n", p=KH), "w_attn1_loaded")
            load(wg1_sb[:], wg1.rearrange("(c p) n -> p c n", p=KH), "w_attn1_loaded")
            load(wg2_sb[:], wg2, "w_attn1_loaded")
            load(ncol_sb[:], norm_cols, "norm_cols_loaded")
            load(wqk2_sb[:], wqk2.rearrange("(c p) m n -> p c m n", p=KH), "w_attn2_loaded")
            load(wv2_sb[:], wv2.rearrange("(c p) n -> p c n", p=KH), "w_attn2_loaded")
            load(wout2_sb[:], wout2.rearrange("(c p) n -> p c n", p=128), "w_attn2_loaded")
            load(wr0_sb[:], wrouter0.rearrange("(c p) n -> p c n", p=KH), "w_attn2_loaded")
            load(wt_sb[:], w_tern.rearrange("(c p) n -> p c n", p=KH), "w_tern_loaded")
            load(gt_sb[:], g_tern.unsqueeze(0).to_broadcast([ROWS, 2, E]), "g_tern_loaded")
            load(wr1_sb[:], w_gate1.rearrange("(c p) n -> p c n", p=KH), "w_ff1_loaded")
            load(gb_sb[:], gate_bias.unsqueeze(0).to_broadcast([ROWS, EXPERTS1]), "w_ff1_loaded")
            sp.wait_ge(S["zeros_made"], 1)
            sp.dma_start(xs_dram.rearrange("(b p) n -> p b n", p=BLOCK),
                         zeros[:].unsqueeze(1).to_broadcast([128, BLOCKS, E])).then_inc(S["slots_cleared"], 16)
            late = STAGES["late"]
            sp.dma_start(ys_dram[late[0] * BLOCK:].rearrange("(b p) n -> p b n", p=BLOCK),
                         zeros[:].unsqueeze(1).to_broadcast([128, len(late), E])).then_inc(S["late_cleared"], 16)

            def expert_of(b):
                return b if b < EXPERTS0 else overflow_expert[b - EXPERTS0]

            def load_up(when, n):
                if n < len(STAGES[when]):
                    if n >= UP_SLOTS:
                        sp.wait_ge(S[f"{when}_up"], 2 * (n - UP_SLOTS + 1))
                    load(wgu_sb[:, n % UP_SLOTS], w_gate_up[expert_of(STAGES[when][n])].rearrange("(c p) n -> p c n", p=KH),
                         f"{when}_up_loaded{n % UP_SLOTS}")

            def load_down(when, n):
                if n < len(STAGES[when]):
                    if n >= DOWN_SLOTS:
                        sp.wait_ge(S[f"{when}_down"], n - DOWN_SLOTS + 1)
                    load(wdn_sb[:, n % DOWN_SLOTS], w_down[expert_of(STAGES[when][n])].rearrange("(c p) n -> p c n", p=128),
                         f"{when}_down_loaded{n % DOWN_SLOTS}")

            def load_block(when, n):
                if n >= len(STAGES[when]):
                    return
                if n >= XB:
                    sp.wait_ge(S[f"{when}_turned"], n - XB + 1)
                b = STAGES[when][n]
                load(xb[:, n % XB, :], xs_dram[b * BLOCK:(b + 1) * BLOCK, :], f"{when}_in{n % XB}")

            def first_weights(when):
                for n in range(UP_SLOTS):
                    load_up(when, n)
                    load_down(when, n)

            def stream_blocks(when):
                for n in range(XB):
                    load_block(when, n)
                for n in range(len(STAGES[when]) + 1):
                    load_block(when, n + XB)
                    load_up(when, n + UP_SLOTS)
                    load_down(when, n + UP_SLOTS)
                    if n >= 1:
                        b = STAGES[when][n - 1]
                        sp.wait_ge(S[f"{when}_out"], n)
                        sp.dma_start(ys_dram[b * BLOCK:(b + 1) * BLOCK, :], yb[:, (n - 1) % YB, :]).then_inc(
                            S[f"{when}_stored{(n - 1) % YB}"], 16)

            sp.wait_ge(S["attended"], TILES)
            first_weights("first")
            sp.wait_ge(S["slots_ready"], 1)
            late = late_needed(sp)
            overflow_expert = [sp.value_load(over_u[0:1, n:n + 1], min_val=0, max_val=EXPERTS0 - 1) for n in range(OVERFLOW)]
            sp.wait_ge(S["tokens_out"], 16 * 2 * TILES)
            stream_blocks("first")
            with sp.If(late):
                sp.wait_ge(S["late_cleared"], 16)
                first_weights("late")
                stream_blocks("late")
            for c in range(2):
                load(w13_sb[:, c], w13.rearrange("e (c p) n -> c p e n", p=KH)[c], "w_ff1_loaded")
            load(w2_sb[:], w2.rearrange("e p n -> p e n"), "w_ff1_loaded")
            for t in range(TILES):
                rows = min(ROWS, TOKENS - t * ROWS)
                sp.wait_ge(S["ff_added"], GROUPS * (EXPERTS1 + 1) - (GROUPS - 1 - t // GROUP))
                sp.dma_start(out[t * ROWS:t * ROWS + rows, :], h[3][0:rows, t, :]).then_inc(S["stored"], 16)
            sp.wait_ge(S["stored"], 16 * TILES)

        @block.gpsimd
        def _(pool):
            def power(norm, g):
                pool.wait_ge(S["norm_var"], nth(norm, g))
                nc.gpsimd.tensor_tensor(rstd[:, norm, gt(g)], ve[:, norm, gt(g)], half_neg[:, gt(g)],
                                        ALU.pow).then_inc(S["norm_rstd"], 1)

            nc.gpsimd.memset(zeros[:], 0.0).then_inc(S["zeros_made"], 1)
            nc.gpsimd.memset(ones_bf[:], 1.0)
            nc.gpsimd.memset(half_neg[:], -0.5)
            nc.gpsimd.memset(ones[:], 1.0)
            nc.gpsimd.memset(v2[:, :, :, HD2:HD2 + 1], 1.0).then_inc(S["pool_consts"], 1)
            pool.wait_ge(S["pool_consts"], 1)
            power(LN_PATCH, 0)
            power(LN_PATCH, 1)
            pool.wait_ge(S["rows_loaded"], 48)
            pool.wait_ge(S["consts_loaded"], 16)
            patch_row = const("is_patch", ROWS)
            nc.gpsimd.tensor_tensor(gm_rows[:], re_sb[:, 1, :], patch_row.to_broadcast([ROWS, E]), ALU.mult)
            nc.gpsimd.tensor_tensor(add_rows[:], re_sb[:, 2, :], patch_row.to_broadcast([ROWS, E]),
                                    ALU.mult).then_inc(S["embed_rows"], 1)
            pool.wait_ge(S["embed_rows"], 1)
            nc.gpsimd.tensor_tensor(add_rows[:], add_rows[:], pos_sb[:], ALU.add).then_inc(S["embed_rows"], 1)
            pool.wait_ge(S["embed_rows"], 2)
            nc.gpsimd.tensor_tensor(add_rows[:], add_rows[:], cls_sb[:], ALU.add).then_inc(S["embed_rows"], 1)
            nc.gpsimd.tensor_copy(causal_bf[:], const("causal", ROWS))
            nc.gpsimd.tensor_copy(block_bf[:], const("block", ROWS))
            nc.gpsimd.tensor_copy(before_bf[:], const("before"))
            nc.gpsimd.tensor_copy(ident_bf[:], ident).then_inc(S["masks_made"], 1)
            for norm in (LN_EMBED, LN_H0, LN_DECAY, LN_H1):
                for g in range(GROUPS):
                    power(norm, g)
                    if norm == LN_H0:
                        pool.wait_ge(S["h0_ready"], g + 1)
                        nc.gpsimd.tensor_tensor(h[1][:, gt(g), :], h[0][:, gt(g), :], on_tiles(re_sb[:, 4, :]),
                                                ALU.add).then_inc(S["h0_shifted"], 1)
            for g in range(GROUPS):
                power(RMS_GQA, g)
            cos = const("cos").rearrange("p (a s) -> p a s", a=2)
            for g in range(GROUPS):
                for u in range(4):
                    n = 4 * g + u
                    pool.wait_ge(S["qk2_raw"], n + 1)
                    if n >= 2:
                        pool.wait_ge(S["qk2_rotated"], n - 1)
                    for b in range(2):
                        last = nc.gpsimd.tensor_tensor(
                            rcos[:, n % 2, b, :].rearrange("p (i s) -> p i s", s=SEQ),
                            raw[:, n % 2, b, :].rearrange("p (i s) -> p i s", s=SEQ),
                            cos[:, u // 3, :].unsqueeze(1).to_broadcast([128, COLS // SEQ, SEQ]), ALU.mult)
                    last.then_inc(S["qk2_cos"], 1)
            for g in range(GROUPS):
                power(RMS_MOE, g)
                pool.wait_ge(S["hh_ready"], g + 1)
                nc.gpsimd.tensor_tensor(h[2][:, gt(g), :], h[1][:, gt(g), :], hh[:, gt(g), :],
                                        ALU.add).then_inc(S["h2_base"], 1)

            pool.wait_ge(S["slots_cleared"], 16)
            pool.wait_ge(S["slots_ready"], 1)
            for t in range(TILES):
                rows = min(ROWS, TOKENS - t * ROWS)
                for k in range(2):
                    nc.gpsimd.indirect_dma_start(
                        xs_dram, bass.IndirectOffsetOnAxis(ap=slot_u[0:rows, k, t:t + 1], axis=0),
                        xn[0:rows, t, :], None).then_inc(S["tokens_out"], 16)
            for n in range(YB):
                pool.wait_ge(S[f"first_stored{n}"], 16 * len(STAGES["first"][n::YB]))
            pool.wait_ge(S["late_cleared"], 16)
            with pool.If(late_needed(pool)):
                for n in range(YB):
                    pool.wait_ge(S[f"late_stored{n}"], 16 * len(STAGES["late"][n::YB]))
            for t in range(TILES):
                rows = min(ROWS, TOKENS - t * ROWS)
                for k in range(2):
                    nc.gpsimd.indirect_dma_start(
                        yg[0:rows, k, t, :], None, ys_dram,
                        bass.IndirectOffsetOnAxis(ap=slot_u[0:rows, k, t:t + 1], axis=0)).then_inc(S[f"tokens_back{t}"], 16)
            for norm in (LN_H2, RMS_TERN, RMS_PROJ, LN_H3):
                for g in range(GROUPS):
                    power(norm, g)

        @block.scalar
        def _(act):
            fn = nc.scalar.activation

            act.wait_ge(S["consts_loaded"], 16)
            act.wait_ge(S["slopes_loaded"], 16)
            for hd in range(HEADS):
                last = fn(decay[:, hd % 4, hd // 4, :], const("ahead", ROWS), ACT.Exp, scale=slope_sb[:, hd:hd + 1])
            last.then_inc(S["decay_exp"], 1)
            act.wait_ge(S["ln1_loaded"], 16)
            for g in range(GROUPS):
                for u in range(PCH // 2):
                    c = 2 * u + 1
                    act.wait_ge(S["patch_turned"], 3 * g + u + 1)
                    fn(patch_t[:, c, gcols(g)], slot_of[("patch_t", g, u)][:, 1, 0:COLS], ACT.Identity,
                       scale=ln1_sb[:, 0, c:c + 1], bias=ln1_sb[:, 1, c:c + 1]).then_inc(S["patch_t_act"], 1)

            def columns(key, turned, n, g, dst, ready, scale=1.0):
                act.wait_ge(S[turned], n)
                fn(dst[:, :, gcols(g)], slot_of[key][0:KH, :, 0:COLS], ACT.Copy, scale=scale).then_inc(S[ready], 1)

            for g in range(GROUPS):
                columns(("x0_t", g), "x_turned", g + 1, g, x_t, "x_t_ready")
            for g in range(GROUPS):
                for m in range(3):
                    act.wait_ge(S["qk1_done"], 3 * g + m + 1)
                    fn(qk1[:, :, m, gcols(g)], slot_of[("qk1", g, m)][:, :, 0:COLS], ACT.Silu).then_inc(S["qk1_silu"], 1)
                act.wait_ge(S["v1_done"], g + 1)
                fn(v1[:, gt(g), :], by_tile(slot_of[("v1", g)]), ACT.Silu).then_inc(S["v1_silu"], 1)
                act.wait_ge(S["gate1_done"], g + 1)
                fn(gate1[:, gt(g), :], by_tile(slot_of[("gate1", g)]), ACT.Tanh, scale=0.5).then_inc(S["gate1_tanh"], 1)
            for g in range(GROUPS):
                columns(("o1_t", g), "o1_turned", g + 1, g, x_t, "o1_t_ready", scale=0.5)

            act.wait_ge(S["norm_cols_loaded"], 16)
            for g in range(GROUPS):
                act.wait_ge(S["x_turned"], 2 + g + 1)
                act.wait_ge(S["attn1_done"], g + 1)
                for c in range(2):
                    last = fn(x_t[:, c, gcols(g)], slot_of[("x1_t", g)][0:KH, c, 0:COLS], ACT.Copy,
                              scale=ncol_sb[:, c, 0:1])
                last.then_inc(S["x_t_ready"], 1)
            act.wait_ge(S["pool_consts"], 1)
            for g in range(GROUPS):
                for u in range(4):
                    n = 4 * g + u
                    act.wait_ge(S["qk2_done"], n + 1)
                    if n >= 2:
                        act.wait_ge(S["qk2_swapped"], n - 1)
                        act.wait_ge(S["qk2_cos"], n - 1)
                    fn(raw[:, n % 2], slot_of[("qk2", g, u)][:, :, 0:COLS], ACT.Copy).then_inc(S["qk2_raw"], 1)
                act.wait_ge(S["v2_done"], g + 1)
                src = by_tile(slot_of[("v2", g)])
                for i, t in enumerate(group_tiles(g)):
                    last = fn(v2[:, t, :, 0:HD2], src[:, i, :].rearrange("p (k d) -> p k d", k=KV), ACT.Copy)
                last.then_inc(S["v2_copied"], 1)

            def exps(n, unit, heads, src, scale):
                act.wait_ge(S["nmax_ready"], 2 * n + unit + 1)
                if n >= PB:
                    act.wait_ge(S["probs_turned"], 2 * (n - PB + 1))
                for i in range(heads):
                    at = (8 if heads == 4 else 6) * unit + i
                    last = fn(p_buf[:, (TILES + n) % PB, at, :], src(i), ACT.Exp,
                              bias=nmax[:, n % TILES, at:at + 1], scale=scale)
                last.then_inc(S["probs"], 1)

            def turned_probs(n):
                act.wait_ge(S["probs_turned"], 2 * n + 2)
                if n >= PB:
                    act.wait_ge(S["attended"], n - PB + 1)
                fn(pt_buf[:, n % PB, 8:12, :], slot_of[("probs_t", n, 1)][0:ROWS, 0, 0:4 * ROWS].rearrange(
                    "p (i x) -> p i x", x=ROWS), ACT.Copy).then_inc(S["probs_t_act"], 1)

            act.wait_ge(S["decay_out_done"], TILES)
            for t in range(TILES):
                s0, s1 = slot_of[("score2", t, 0)], slot_of[("score2", t, 1)]
                exps(t, 0, 8, lambda i: s0[0:ROWS, i // 4, (i % 4) * ROWS:(i % 4 + 1) * ROWS], 1.0)
                exps(t, 1, 4, lambda i: s1[0:ROWS, i // 2, (i % 2) * ROWS:(i % 2 + 1) * ROWS], 1.0)
                if t >= 1:
                    turned_probs(t - 1)
            turned_probs(TILES - 1)
            for g in range(GROUPS):
                for u in (0, 2):
                    act.wait_ge(S["o2_turned"], 3 * g + u + 1)
                    last = fn(o2_t[:, 2 * u:2 * u + 2, gcols(g)], slot_of[("o2_t", g, u)][:, :, 0:COLS], ACT.Copy)
                    last.then_inc(S["o2_t_act"], 1 if u == 0 else 2)

            for g in range(GROUPS):
                act.wait_ge(S["x_turned"], 4 + g + 1)
                for c in range(2):
                    last = fn(m_t[:, c, gcols(g)], slot_of[("m_t", g)][0:KH, c, 0:COLS], ACT.Copy,
                              scale=ncol_sb[:, c, 1:2])
                last.then_inc(S["m_t_ready"], 1)
            act.wait_ge(S["top0_ready"], 1)
            fn(pair_w[:, 1, :], rt[0][:, :, 0], ACT.Exp).then_inc(S["router_exp"], 1)

            def run_blocks(when):
                blocks = STAGES[when]

                def block_columns(n):
                    act.wait_ge(S[f"{when}_turned"], n + 1)
                    if n >= 2:
                        act.wait_ge(S[f"{when}_up"], 2 * (n - 1))
                    for c in range(2):
                        last = fn(xb_t[:, n % 2, c, :], slot_of[(when, "turned", n)][0:KH, 0, c * BLOCK:(c + 1) * BLOCK],
                                  ACT.Copy, scale=ncol_sb[:, c, 1:2])
                    last.then_inc(S[f"{when}_columns"], 1)

                block_columns(0)
                for n in range(len(blocks)):
                    if n + 1 < len(blocks):
                        block_columns(n + 1)
                    act.wait_ge(S[f"{when}_up"], 2 * n + 1)
                    if n >= 2:
                        act.wait_ge(S[f"{when}_hidden"], n - 1)
                    fn(sb_silu[:, n % 2, :], slot_of[(when, "up", n)][:, 0, 0:3 * BLOCK],
                       ACT.Silu).then_inc(S[f"{when}_silu"], 1)

            act.wait_ge(S["slots_ready"], 1)
            late = late_needed(act)
            run_blocks("first")
            with act.If(late):
                run_blocks("late")

            def silu(n):
                act.wait_ge(S["ff_up"], 2 * n + 1)
                if n >= 2:
                    act.wait_ge(S["ff_hidden"], n - 1)
                for g in range(GROUPS):
                    last = fn(silu_buf[:, n % 2, gcols(g, live_cols(g))], slot_of[("ff", n, 0)][:, g, 0:live_cols(g)],
                              ACT.Silu)
                last.then_inc(S["ff_silu"], 1)

            def int_columns(n, g):
                act.wait_ge(S["ints_turned"], n + 1)
                view = slot_of[("ints_t", n)][:].bitcast(BF16)
                for c in range(2):
                    last = fn(q_int_t[:, c, gcols(g)].rearrange("p (i x) -> p i x", x=ROWS),
                              view[0:KH, c, 0:3 * 112].rearrange("p (i x) -> p i x", x=112)[:, :, 0:ROWS], ACT.Copy)
                last.then_inc(S["ints_t_ready"], 1)

            for g in range(GROUPS):
                int_columns(g, g)
                act.wait_ge(S["dq_done"], 3 * g + 3)
                fn(dq[:, gcols(g)], slot_of[("dq", g)][:, 0, 0:COLS], ACT.Copy).then_inc(S["dq_ready"], 1)
            for t in range(TILES):
                for jp in range(2):
                    s = slot_of[("score3", t, jp)]
                    exps(TILES + t, jp, 6, lambda i: s[0:ROWS, i // 3, (i % 3) * ROWS:(i % 3 + 1) * ROWS], 0.25)
                if t >= 1:
                    turned_probs(TILES + t - 1)
            turned_probs(2 * TILES - 1)
            for g in range(GROUPS):
                int_columns(2 + g, g)
            for g in range(GROUPS):
                columns(("x4_t", g), "x_turned", 6 + g + 1, g, x_t, "x_t_ready")
            for g in range(GROUPS):
                act.wait_ge(S["logits1_done"], g + 1)
                fn(lg[:, gt(g), 0:EXPERTS1], by_tile(slot_of[("logits1", g)], EXPERTS1),
                   ACT.Sigmoid).then_inc(S["logits1_sigmoid"], 1)
            for n in range(EXPERTS1 + 1):
                silu(n)

        @block.vector
        def _(dve):
            v = nc.vector
            link = {"n": 0}

            def after(ins):
                link["n"] += 1
                ins.then_inc(S["dve_step"], 1)
                dve.wait_ge(S["dve_step"], link["n"])

            def statistics(norm, g, src, square=False, pieces=1):
                width = src.shape[2] // pieces
                for i, t in enumerate(group_tiles(g)):
                    for p in range(pieces):
                        last = v.bn_stats(stats[:, t, p, :], src[:, i, p * width:(p + 1) * width])
                after(last)
                for t in group_tiles(g):
                    last = v.bn_aggr(mv[:, norm, t, :], stats[:, t, 0:pieces, :].rearrange("p a b -> p (a b)"))
                after(last)
                if square:
                    after(v.tensor_tensor(vt[:, norm, gt(g)], mv[:, norm, gt(g), 0], mv[:, norm, gt(g), 0], ALU.mult))
                    v.scalar_tensor_tensor(ve[:, norm, gt(g)], vt[:, norm, gt(g)], EPS[norm], mv[:, norm, gt(g), 1],
                                           ALU.add, ALU.add).then_inc(S["norm_var"], 1)
                else:
                    v.tensor_scalar(ve[:, norm, gt(g)], mv[:, norm, gt(g), 1], EPS[norm], None,
                                    ALU.add).then_inc(S["norm_var"], 1)

            def second_moment(norm, of, g):
                dve.wait_ge(S["norm_rstd"], nth(of, g))
                after(v.tensor_tensor(vt[:, norm, gt(g)], rstd[:, of, gt(g)], rstd[:, of, gt(g)], ALU.mult))
                after(v.tensor_tensor(vt[:, norm, gt(g)], vt[:, norm, gt(g)], mv[:, of, gt(g), 1], ALU.mult))
                v.tensor_scalar(ve[:, norm, gt(g)], vt[:, norm, gt(g)], EPS[norm], None,
                                ALU.add).then_inc(S["norm_var"], 1)

            def normalise(norm, g, dst, src, centre=True):
                dve.wait_ge(S["norm_rstd"], nth(norm, g))
                for i, t in enumerate(group_tiles(g)):
                    r = rstd[:, norm, t:t + 1]
                    if centre:
                        last = v.tensor_scalar(dst[:, i, :], src[:, i, :], mv[:, norm, t, 0:1], r, ALU.subtract, ALU.mult)
                    else:
                        last = v.tensor_scalar(dst[:, i, :], src[:, i, :], r, None, ALU.mult)
                return last

            for g in range(GROUPS):
                dve.wait_ge(S[f"patch_loaded{g}"], 16 * GROUP)
                statistics(LN_PATCH, g, patch_x[:, gt(g), :], pieces=2)
            for g in range(GROUPS):
                normalise(LN_PATCH, g, patch_x[:, gt(g), :], patch_x[:, gt(g), :]).then_inc(S["patch_normed"], 1)
            dve.wait_ge(S["decay_exp"], 1)
            keep = const("keep", ROWS)
            flat = decay[:].rearrange("p j m n -> p (j m) n")
            v.tensor_tensor(flat, flat, on_tiles(keep, HEADS), ALU.mult).then_inc(S["decay_ready"], 1)
            dve.wait_ge(S["ln1_loaded"], 16)
            for g in range(GROUPS):
                for u in range(PCH // 2):
                    c = 2 * u
                    dve.wait_ge(S["patch_turned"], 3 * g + u + 1)
                    v.tensor_scalar(patch_t[:, c, gcols(g)], slot_of[("patch_t", g, u)][:, 0, 0:COLS],
                                    ln1_sb[:, 0, c:c + 1], ln1_sb[:, 1, c:c + 1], ALU.mult,
                                    ALU.add).then_inc(S["patch_t_dve"], 1)
            dve.wait_ge(S["rows_loaded"], 48)
            for g in range(GROUPS):
                dve.wait_ge(S["embed_done"], g + 1)
                v.tensor_tensor(y0[:, gt(g), :], by_tile(slot_of[("embed", g)]), on_tiles(re_sb[:, 0, :]),
                                ALU.add).then_inc(S["embed_biased"], 1)
                dve.wait_ge(S["embed_biased"], g + 1)
                statistics(LN_EMBED, g, y0[:, gt(g), :])
            dve.wait_ge(S["embed_rows"], 3)
            for g in range(GROUPS):
                after(normalise(LN_EMBED, g, z0[:, gt(g), :], y0[:, gt(g), :]))
                after(v.tensor_tensor(z0[:, gt(g), :], z0[:, gt(g), :], on_tiles(gm_rows[:]), ALU.mult))
                v.tensor_tensor(h[0][:, gt(g), :], z0[:, gt(g), :], on_tiles(add_rows[:]),
                                ALU.add).then_inc(S["h0_ready"], 1)
                dve.wait_ge(S["h0_ready"], g + 1)
                statistics(LN_H0, g, h[0][:, gt(g), :])
            for g in range(GROUPS):
                normalise(LN_H0, g, xn[:, gt(g), :], h[0][:, gt(g), :]).then_inc(S["x_normed"], 1)

            for g in range(GROUPS):
                dve.wait_ge(S["g1_done"], g + 1)
                v.tensor_copy(g1_t[:, gcols(g)], slot_of[("g1", g)][0:16, 0, 0:COLS]).then_inc(S["g1_copied"], 1)
            dve.wait_ge(S["decay_ready"], 1)
            for g in range(GROUPS):
                for t in group_tiles(g):
                    for jp in range(2):
                        dve.wait_ge(S["energy_done"], 2 * t + jp + 1)
                        if t >= PB:
                            dve.wait_ge(S["decay_out_done"], t - PB + 1)
                        v.tensor_tensor(p_buf[:, t % PB, 6 * jp:6 * jp + 6, :].rearrange("p (b m) n -> p b (m n)", b=2),
                                        slot_of[("energy", t, jp)][0:ROWS, :, 0:COLS],
                                        decay[:, 2 * jp:2 * jp + 2].rearrange("p b m n -> p b (m n)"),
                                        ALU.mult).then_inc(S["energy_decayed"], 1)
                dve.wait_ge(S["decay_out_done"], 3 * g + 3)
                dve.wait_ge(S["gate1_tanh"], g + 1)
                v.scalar_tensor_tensor(o_rows[:, gt(g), :], gate1[:, gt(g), :], 1.0, by_tile(slot_of[("decay_out", g)]),
                                       ALU.add, ALU.mult).then_inc(S["o1_gated"], 1)
            for g in range(GROUPS):
                dve.wait_ge(S["attn1_done"], g + 1)
                statistics(LN_DECAY, g, by_tile(slot_of[("attn1", g)]))
            for g in range(GROUPS):
                last = normalise(LN_DECAY, g, z0[:, gt(g), :], by_tile(slot_of[("attn1", g)]))
                last.then_inc(S["attn1_normed"], 1)
                dve.wait_ge(S["attn1_normed"], g + 1)
                after(v.tensor_tensor(z0[:, gt(g), :], z0[:, gt(g), :], on_tiles(re_sb[:, 3, :]), ALU.mult))
                dve.wait_ge(S["h0_shifted"], g + 1)
                v.tensor_tensor(h[1][:, gt(g), :], h[1][:, gt(g), :], z0[:, gt(g), :], ALU.add).then_inc(S["h1_ready"], 1)
                dve.wait_ge(S["h1_ready"], g + 1)
                statistics(LN_H1, g, h[1][:, gt(g), :])

            for g in range(GROUPS):
                second_moment(RMS_GQA, LN_H1, g)
                after(normalise(LN_H1, g, x2[:, gt(g), :], h[1][:, gt(g), :]))
            for g in range(GROUPS):
                normalise(RMS_GQA, g, xn[:, gt(g), :], x2[:, gt(g), :], centre=False).then_inc(S["x_normed"], 1)
            sin = const("sin").rearrange("p (a s) -> p a s", a=2)
            for g in range(GROUPS):
                for u in range(4):
                    n = 4 * g + u
                    dve.wait_ge(S["qk2_swapped"], n + 1)
                    for b in range(2):
                        last = v.tensor_tensor(rsin[:, n % 2, b, :].rearrange("p (i s) -> p i s", s=SEQ),
                                               slot_of[("swap", g, u)][:, b, 0:COLS].rearrange("p (i s) -> p i s", s=SEQ),
                                               sin[:, u // 3, :].unsqueeze(1).to_broadcast([128, COLS // SEQ, SEQ]),
                                               ALU.mult)
                    last.then_inc(S["qk2_sin"], 1)
                    dve.wait_ge(S["qk2_sin"], n + 1)
                    dve.wait_ge(S["qk2_cos"], n + 1)
                    v.tensor_tensor(qk2[:, 2 * u:2 * u + 2, gcols(g)], rsin[:, n % 2], rcos[:, n % 2],
                                    ALU.add).then_inc(S["qk2_rotated"], 1)

            def negative_max(n, unit, views, scale):
                dve.wait_ge(S["score_done"], 2 * n + unit + 1)
                src, banks, per = views
                at = 8 * unit if per != 3 else 6 * unit
                dst = nmax[:, n % TILES, at:at + banks * per].rearrange("p (b i) -> p b i", b=banks)
                last = v.tensor_reduce(dst, src, AX.X, ALU.max, negate=True)
                if scale != 1.0:
                    after(last)
                    last = v.tensor_scalar(dst, dst, scale, None, ALU.mult)
                last.then_inc(S["nmax_ready"], 1)

            def turned_probs(n):
                dve.wait_ge(S["probs_turned"], 2 * n + 1)
                if n >= PB:
                    dve.wait_ge(S["attended"], n - PB + 1)
                v.tensor_copy(pt_buf[:, n % PB, 0:8, :].rearrange("p (b i) x -> p b (i x)", b=2),
                              slot_of[("probs_t", n, 0)][0:ROWS, :, 0:4 * ROWS]).then_inc(S["probs_t_dve"], 1)

            def scaled2(t):
                dve.wait_ge(S["attended"], t + 1)
                src = slot_of[("attend2", t)][0:ROWS, :, 0:6 * (HD2 + 1)].rearrange("p b (i d) -> p b i d", d=HD2 + 1)
                rs = rsum[:, t, :].rearrange("p (b i) -> p b i", b=2)
                after(v.reciprocal(rs, src[:, :, :, HD2]))
                v.tensor_tensor(o2[:, t, :].rearrange("p (b i d) -> p b i d", b=2, d=HD2), src[:, :, :, 0:HD2],
                                rs.unsqueeze(3).to_broadcast([ROWS, 2, 6, HD2]), ALU.mult).then_inc(S["o2_scaled"], 1)

            for t in range(TILES):
                for u, per in enumerate((4, 2)):
                    src = slot_of[("score2", t, u)][0:ROWS, :, 0:per * ROWS].rearrange("p b (i x) -> p b i x", x=ROWS)
                    negative_max(t, u, (src, 2, per), 1.0)
                if t >= 1:
                    turned_probs(t - 1)
                if t >= 2:
                    scaled2(t - 2)
            turned_probs(TILES - 1)
            scaled2(TILES - 2)
            scaled2(TILES - 1)
            for g in range(GROUPS):
                dve.wait_ge(S["o2_turned"], 3 * g + 2)
                last = v.tensor_copy(o2_t[:, 2:4, gcols(g)], slot_of[("o2_t", g, 1)][:, :, 0:COLS])
                last.then_inc(S["o2_t_dve"], 2 if g == 0 else 3)
            for g in range(GROUPS):
                dve.wait_ge(S["attn2_done"], g + 1)
                v.tensor_tensor(hh[:, gt(g), :], by_tile(slot_of[("attn2", g)]), x2[:, gt(g), :],
                                ALU.add).then_inc(S["hh_ready"], 1)
                dve.wait_ge(S["hh_ready"], g + 1)
                statistics(RMS_MOE, g, hh[:, gt(g), :], square=True)
            for g in range(GROUPS):
                normalise(RMS_MOE, g, xn[:, gt(g), :], hh[:, gt(g), :], centre=False).then_inc(S["x_normed"], 1)

            for g in range(GROUPS):
                dve.wait_ge(S["logits0_done"], g + 1)
                v.tensor_copy(lg[:, gt(g), :], by_tile(slot_of[("logits0", g)], EXPERTS0)).then_inc(S["logits0_copied"], 1)
            dve.wait_ge(S["logits0_copied"], 2)
            for t in range(TILES):
                last = v.max(top[:, t, :], lg[:, t, :])
            after(last)
            for t in range(TILES):
                last = v.max_index(top_i[:, t, :], top[:, t, :], lg[:, t, :])
            after(last)
            after(v.tensor_copy(top_f[:], top_i[:, :, 0:2]))
            iota = on_tiles(const("iota", ROWS), TILES)
            for k in range(2):
                last = v.tensor_tensor(hot[:, k], iota, along(top_f[:, :, k], EXPERTS0), ALU.is_equal)
            after(last)
            v.tensor_tensor(hot_bf[:], hot[:, 0], hot[:, 1], ALU.add).then_inc(S["hot_ready"], 1)
            v.tensor_tensor(rt[0][:, :, 0:1], top[:, :, 1:2], top[:, :, 0:1], ALU.subtract).then_inc(S["top0_ready"], 1)

            dve.wait_ge(S["ranks_done"], 1)
            ranks = slot_of["ranks"]
            counts = ranks[0:ROWS, 0, TILES * EXPERTS0:(TILES + 1) * EXPERTS0]
            after(v.tensor_tensor(over[:], counts.unsqueeze(2).to_broadcast([ROWS, EXPERTS0, MORE]),
                                  const("steps", ROWS).unsqueeze(1).to_broadcast([ROWS, EXPERTS0, MORE]), ALU.is_gt))
            after(v.tensor_reduce(share[:, 0, :], over[:], AX.X, ALU.add))
            after(v.tensor_tensor_scan(share[:, 1, :], const("is_one", ROWS), share[:, 0, :], 0.0, ALU.mult, ALU.add))
            v.tensor_tensor(over_f[:], share[0:1, 1, :].unsqueeze(1).to_broadcast([1, OVERFLOW, EXPERTS0]),
                            const("block_no", 1).unsqueeze(2).to_broadcast([1, OVERFLOW, EXPERTS0]), ALU.is_le)
            after(v.tensor_tensor(share[:, 2, :], share[:, 1, :], share[:, 0, :], ALU.subtract))
            v.tensor_reduce(over_n[:], over_f[:], AX.X, ALU.add)
            after(v.scalar_tensor_tensor(share[:, 3, :], share[:, 2, :], float(BLOCK), const("over_slot", ROWS),
                                         ALU.mult, ALU.add))
            v.tensor_scalar(over_u[:], over_n[:], EXPERTS0 - 1.0, None, ALU.min)
            v.tensor_copy(used_u[:], share[0:1, 1, EXPERTS0 - 1:EXPERTS0])
            rank = ranks[0:ROWS, 0, 0:TILES * EXPERTS0].rearrange("p (t e) -> p t e", e=EXPERTS0)
            v.scalar_tensor_tensor(rt[2][:], rank, float(BLOCK), on_tiles(share[:, 3, :], TILES), ALU.is_ge, ALU.mult)
            after(v.tensor_tensor(rt[3][:], rank, on_tiles(const("own_slot", ROWS), TILES), ALU.add))
            after(v.tensor_tensor(rt[2][:], rt[2][:], rt[3][:], ALU.add))
            for k in range(2):
                last = v.tensor_tensor(hot[:, k], hot[:, k], rt[2][:], ALU.mult)
            after(last)
            after(v.tensor_reduce(slot_f[:].rearrange("p k t o -> p (k t) o"), hot[:].rearrange("p k t e -> p (k t) e"),
                                  AX.X, ALU.add))
            v.tensor_copy(slot_u[:], slot_f[:, :, :, 0]).then_inc(S["slots_ready"], 1)
            dve.wait_ge(S["router_exp"], 1)
            after(v.tensor_scalar(rden[:, :, 0], pair_w[:, 1, :], 1.0, None, ALU.add))
            after(v.reciprocal(pair_w[:, 0, :], rden[:, :, 0]))
            after(v.tensor_tensor(pair_w[:, 1, :], pair_w[:, 1, :], pair_w[:, 0, :], ALU.mult))

            def run_blocks(when):
                blocks = STAGES[when]
                for n in range(len(blocks) + 1):
                    if n < len(blocks):
                        dve.wait_ge(S[f"{when}_up"], 2 * n + 2)
                        dve.wait_ge(S[f"{when}_silu"], n + 1)
                        if n >= 2:
                            dve.wait_ge(S[f"{when}_down"], n - 1)
                        v.tensor_tensor(hid_t[:, n % 2].rearrange("p c n -> p (c n)"), sb_silu[:, n % 2, :],
                                        slot_of[(when, "up", n)][:, 1, 0:3 * BLOCK], ALU.mult).then_inc(S[f"{when}_hidden"], 1)
                    if n >= 1:
                        dve.wait_ge(S[f"{when}_down"], n)
                        if n > YB:
                            dve.wait_ge(S[f"{when}_stored{(n - 1) % YB}"], 16 * ((n - 1) // YB))
                        v.tensor_copy(yb[:, (n - 1) % YB, :], slot_of[(when, "down", n - 1)][:, 0, 0:E]).then_inc(
                            S[f"{when}_out"], 1)

            dve.wait_ge(S["slots_ready"], 1)
            late = late_needed(dve)
            run_blocks("first")
            with dve.If(late):
                for n in range(YB):
                    dve.wait_ge(S[f"first_stored{n}"], 16 * len(STAGES["first"][n::YB]))
                run_blocks("late")
            dve.wait_ge(S["h2_base"], 2)
            for t in range(TILES):
                rows = min(ROWS, TOKENS - t * ROWS)
                dve.wait_ge(S[f"tokens_back{t}"], 32)
                for k in range(2):
                    after(v.scalar_tensor_tensor(h[2][0:rows, t, :], yg[0:rows, k, t, :], pair_w[0:rows, k, t:t + 1],
                                                 h[2][0:rows, t, :], ALU.mult, ALU.add))

            def hidden(n, buffer, piece):
                dve.wait_ge(S["ff_silu"], n + 1)
                dve.wait_ge(S["ff_up"], 2 * n + 2)
                for g in range(GROUPS):
                    cols = gcols(g, live_cols(g))
                    last = v.tensor_tensor(hid[:, buffer, piece, cols], silu_buf[:, n % 2, cols],
                                           slot_of[("ff", n, 1)][:, g, 0:live_cols(g)], ALU.mult)
                last.then_inc(S["ff_hidden"], 1)

            def add_expert(n, dst, weight):
                for g in range(GROUPS):
                    dve.wait_ge(S["ff_down"], GROUPS * n + g + 1)
                    for i, t in enumerate(group_tiles(g)):
                        rows = min(ROWS, TOKENS - t * ROWS)
                        last = v.scalar_tensor_tensor(dst[0:rows, t, :], by_tile(slot_of[("down", n, g)], rows=rows)[:, i, :],
                                                      weight(t, rows), dst[0:rows, t, :], ALU.mult, ALU.add)
                    last.then_inc(S["ff_added"], 1)

            dve.wait_ge(S["w_tern_loaded"], 16)
            dve.wait_ge(S["g_tern_loaded"], 16)
            for n, cols in enumerate((slice(0, 5 * E), slice(5 * E, 6 * E))):
                v.tensor_reduce(tern_abs[:, n:n + 1], wt_sb[:, :, cols], AX.XY, ALU.add,
                                apply_absolute_value=True).then_inc(S["tern_summed"], 1)
            dve.wait_ge(S["tern_sum_done"], 1)
            for n, count in enumerate((3 * E * E, E * E)):
                last = v.tensor_scalar(tern_mean[:, n:n + 1], slot_of["tern_sum"][:, 0, n:n + 1], 1.0 / count, 1e-5,
                                       ALU.mult, ALU.max)
            last.then_inc(S["tern_mean_ready"], 1)
            dve.wait_ge(S["tern_mean_ready"], 1)
            after(v.reciprocal(tern_scale[:], tern_mean[:]))
            for n, cols in enumerate((slice(0, 5 * E), slice(5 * E, 6 * E))):
                last = v.tensor_scalar(tern_f[:, :, cols], wt_sb[:, :, cols], tern_scale[0:KH, n:n + 1], MAGIC,
                                       ALU.mult, ALU.add)
            after(last)
            after(v.tensor_scalar(tern_f[:], tern_f[:], MAGIC, 1.0, ALU.subtract, ALU.min))
            v.tensor_scalar(tern[:], tern_f[:], -1.0, None, ALU.max).then_inc(S["tern_ready"], 1)

            def quantise(g, n, src, gain):
                k = n // 2
                after(v.tensor_tensor(qa[:, gt(g), :], src, on_tiles(gt_sb[:, gain, :]), ALU.mult))
                after(v.tensor_reduce(amax[:, gt(g), 0:1], qa[:, gt(g), :], AX.X, ALU.max, apply_absolute_value=True))
                after(v.tensor_scalar(amax[:, gt(g), 1:2], amax[:, gt(g), 0:1], 1e-5, 1.0 / 127.0, ALU.max, ALU.mult))
                after(v.reciprocal(amax[:, gt(g), 2:3], amax[:, gt(g), 1:2]))
                last = v.tensor_scalar(amax[:, gt(g), 3:4], amax[:, gt(g), 1:2], tern_mean[0:ROWS, k:k + 1], None,
                                       ALU.mult)
                for t in group_tiles(g):
                    last = v.tensor_scalar(qb[:, t, :], qa[:, t, :], amax[:, t, 2:3], 127.0, ALU.mult, ALU.min)
                after(last)
                after(v.tensor_scalar(qb[:, gt(g), :], qb[:, gt(g), :], -128.0, MAGIC, ALU.max, ALU.add))
                v.tensor_scalar(q_int[:, gt(g), :], qb[:, gt(g), :], MAGIC, None, ALU.subtract).then_inc(S["quantised"], 1)

            for g in range(GROUPS):
                statistics(LN_H2, g, h[2][:, gt(g), :])
            for g in range(GROUPS):
                second_moment(RMS_TERN, LN_H2, g)
                after(normalise(LN_H2, g, x3[:, gt(g), :], h[2][:, gt(g), :]))
            for g in range(GROUPS):
                after(normalise(RMS_TERN, g, x3[:, gt(g), :], x3[:, gt(g), :], centre=False))
                quantise(g, g, x3[:, gt(g), :], 0)
                for t in group_tiles(g):
                    if t >= 2:
                        dve.wait_ge(S["dq_done"], t - 1)
                    v.tensor_scalar(diag[:, t % 2, :], ident[0:ROWS, 0:ROWS], amax[:, t, 3:4], None,
                                    ALU.mult).then_inc(S["diag_ready"], 1)
            v.memset(v3[:, :, :, HD1:HD1 + 1], 1.0)
            for g in range(GROUPS):
                dve.wait_ge(S["dq_ready"], g + 1)
                for m in range(3):
                    dve.wait_ge(S["qk3_done"], 3 * g + m + 1)
                    v.tensor_tensor(qk3[:, :, m, gcols(g)], slot_of[("qk3", g, m)][:, :, 0:COLS],
                                    dq[:, gcols(g)].unsqueeze(1).to_broadcast([128, 2, COLS]),
                                    ALU.mult).then_inc(S["qk3_scaled"], 1)
                dve.wait_ge(S["v3_done"], g + 1)
                src = by_tile(slot_of[("v3", g)])
                for i, t in enumerate(group_tiles(g)):
                    last = v.tensor_scalar(v3[:, t, :, 0:HD1], src[:, i, :].rearrange("p (k d) -> p k d", k=HEADS),
                                           amax[:, t, 3:4], None, ALU.mult)
                last.then_inc(S["v3_scaled"], 1)

            def scaled3(t):
                dve.wait_ge(S["attended"], TILES + t + 1)
                src = slot_of[("attend3", t)][0:ROWS, 0, 0:HEADS * 17].rearrange("p (i d) -> p i d", d=17)
                after(v.reciprocal(rsum[:, t, :], src[:, :, HD1]))
                v.tensor_tensor(o3[:, t, :].rearrange("p (i d) -> p i d", d=HD1), src[:, :, 0:HD1],
                                along(rsum[:, t, :], HD1), ALU.mult).then_inc(S["o3_scaled"], 1)

            for t in range(TILES):
                for jp in range(2):
                    src = slot_of[("score3", t, jp)][0:ROWS, :, 0:COLS].rearrange("p b (i x) -> p b i x", x=ROWS)
                    negative_max(TILES + t, jp, (src, 2, 3), 0.25)
                if t >= 1:
                    turned_probs(TILES + t - 1)
                if t >= 2:
                    scaled3(t - 2)
            turned_probs(2 * TILES - 1)
            scaled3(TILES - 2)
            scaled3(TILES - 1)
            for g in range(GROUPS):
                dve.wait_ge(S["o3_scaled"], 3 * g + 3)
                statistics(RMS_PROJ, g, o3[:, gt(g), :], square=True)
            for g in range(GROUPS):
                after(normalise(RMS_PROJ, g, o3[:, gt(g), :], o3[:, gt(g), :], centre=False))
                quantise(g, 2 + g, o3[:, gt(g), :], 1)
            for g in range(GROUPS):
                dve.wait_ge(S["attn3_done"], g + 1)
                src = by_tile(slot_of[("attn3", g)])
                for i, t in enumerate(group_tiles(g)):
                    last = v.scalar_tensor_tensor(h[3][:, t, :], src[:, i, :], amax[:, t, 3:4], h[2][:, t, :],
                                                  ALU.mult, ALU.add)
                last.then_inc(S["h3_ready"], 1)
                dve.wait_ge(S["h3_ready"], g + 1)
                statistics(LN_H3, g, h[3][:, gt(g), :])
            for g in range(GROUPS):
                normalise(LN_H3, g, xn[:, gt(g), :], h[3][:, gt(g), :]).then_inc(S["x_normed"], 1)

            dve.wait_ge(S["w_ff1_loaded"], 80)
            dve.wait_ge(S["logits1_sigmoid"], 2)
            score = lg[:, :, 0:EXPERTS1]
            after(v.tensor_tensor(rt[0][:, :, 0:8], score, on_tiles(gb_sb[:], TILES), ALU.add))
            pairs = rt[0][:, :, 0:8].rearrange("p t (g e) -> p t g e", e=2)
            after(v.memset(rt[1][:], MASKED))
            after(v.tensor_tensor(rt[1][:, :, 0:4], pairs[:, :, :, 0], pairs[:, :, :, 1], ALU.add))

            def two_largest(values, width, hot):
                for t in range(TILES):
                    last = v.max(top[:, t, :], values[:, t, 0:8])
                after(last)
                for t in range(TILES):
                    last = v.max_index(top_i[:, t, :], top[:, t, :], values[:, t, 0:8])
                after(last)
                after(v.tensor_copy(top_f[:], top_i[:, :, 0:2]))
                numbers = on_tiles(const("iota", ROWS)[:, 0:width], TILES)
                v.tensor_tensor(hot, numbers, along(top_f[:, :, 0], width), ALU.is_equal)
                after(v.tensor_tensor(rt[3][:, :, 0:width], numbers, along(top_f[:, :, 1], width), ALU.is_equal))
                after(v.tensor_tensor(hot, hot, rt[3][:, :, 0:width], ALU.add))

            two_largest(rt[1][:], 4, rt[2][:, :, 0:4])
            in_group = along2 = rt[4][:, :, 0:8].rearrange("p t (g e) -> p t g e", e=2)
            v.tensor_copy(in_group[:, :, :, 0], rt[2][:, :, 0:4])
            after(v.tensor_copy(in_group[:, :, :, 1], rt[2][:, :, 0:4]))
            v.tensor_tensor(rt[1][:, :, 0:8], rt[0][:, :, 0:8], rt[4][:, :, 0:8], ALU.mult)
            after(v.tensor_scalar(rt[5][:, :, 0:8], rt[4][:, :, 0:8], -MASKED, MASKED, ALU.mult, ALU.add))
            after(v.tensor_tensor(rt[1][:, :, 0:8], rt[1][:, :, 0:8], rt[5][:, :, 0:8], ALU.add))
            two_largest(rt[1][:], 8, rt[2][:, :, 0:8])
            after(v.tensor_tensor(rt[4][:, :, 0:8], rt[2][:, :, 0:8], score, ALU.mult))
            after(v.tensor_reduce(rden[:, :, 0:1], rt[4][:, :, 0:8], AX.X, ALU.add))
            after(v.tensor_scalar(rden[:, :, 0:1], rden[:, :, 0:1], 1e-6, None, ALU.add))
            after(v.reciprocal(rden[:, :, 1:2], rden[:, :, 0:1]))
            after(v.tensor_tensor(comb1[:], rt[4][:, :, 0:8], along(rden[:, :, 1], 8), ALU.mult))
            for n in range(EXPERTS1 + 2):
                k = n
                if n <= EXPERTS1:
                    hidden(n, n % 2, 0)
                if n >= 1:
                    if n >= 2:
                        dve.wait_ge(S["ff_added"], GROUPS * (n - 1))
                    if n == 1:
                        add_expert(k - 1, h[3], lambda t, rows: 1.0)
                    else:
                        add_expert(k - 1, h[3], lambda t, rows: comb1[0:rows, t, n - 2:n - 1])


def constants():
    c = np.zeros((128, CONST_WIDTH), np.float32)

    def put(name, value):
        at, width = CONST_AT[name]
        c[:value.shape[0], at:at + width] = value.reshape(value.shape[0], width)

    put("ident", np.eye(128))
    n = np.arange(128)
    put("swap", np.eye(128)[n ^ 1])
    r = np.arange(ROWS)
    same = r[:, None] // SEQ == r[None, :] // SEQ
    back = r[:, None] - r[None, :]
    put("causal", np.where(same & (back >= 0), 0.0, MASKED))
    put("block", np.where(same, 0.0, MASKED))
    put("ahead", np.where(same & (back <= 0), -back, 0))
    put("keep", (same & (back <= 0)).astype(np.float32))
    put("is_patch", (r % SEQ > 0).astype(np.float32)[:, None])
    put("before", np.triu(np.ones((128, 128)), 1))
    e = np.arange(EXPERTS0)
    put("is_one", np.ones((128, EXPERTS0)))
    put("own_slot", np.broadcast_to(BLOCK * e, (128, EXPERTS0)))
    put("over_slot", np.broadcast_to(BLOCK * (EXPERTS0 - 1 - e), (128, EXPERTS0)))
    put("steps", np.broadcast_to(BLOCK * (1 + np.arange(MORE)), (128, MORE)))
    put("block_no", np.broadcast_to(np.arange(OVERFLOW), (128, OVERFLOW)))
    put("iota", np.broadcast_to(np.arange(EXPERTS0, dtype=np.float32), (128, EXPERTS0)))
    inverse = (1.0 / np.float32(10000.0) ** (np.arange(0, HD2, 2, dtype=np.float32) / np.float32(HD2))).astype(np.float32)
    angle = np.arange(SEQ, dtype=np.float32)[None, :] * inverse[(n % HD2) // 2][:, None]
    sign = np.where(n % 2 == 0, -1.0, 1.0)[:, None]
    share = np.array([HD2 ** -0.5, 1.0])[None, :, None]
    put("cos", np.cos(angle)[:, None, :] * share)
    put("sin", (sign * np.sin(angle))[:, None, :] * share)
    return c


_OUT = (IMAGES, SEQ, E)


def kernel(**inputs):
    import concourse.bacc as _bacc
    from concourse.bass_utils import run_bass_kernel_spmd as _run

    a = {k: np.asarray(x) for k, x in inputs.items()}
    x = a["x"].reshape(IMAGES, 3, 6, 16, 6, 16).transpose(0, 2, 4, 1, 3, 5).reshape(IMAGES, PATCHES, PD)
    patches = np.zeros((TILES * PER_TILE, SEQ, PD), np.float32)
    patches[:IMAGES, 1:] = x

    def channels_first(w):
        return w.reshape(16, 16, 3, -1).transpose(2, 0, 1, 3).reshape(PD, -1)

    ln1 = np.stack([channels_first(a["L0_tok_ln1_g"])[:, 0], channels_first(a["L0_tok_ln1_b"])[:, 0]])
    pos = a["L0_tok_pos_embed"][0]
    cls_rows = np.zeros((PER_TILE, SEQ, E), np.float32)
    cls_rows[:, 0] = a["L0_tok_cls_token"]

    def padded_heads(w):
        p = np.zeros((w.shape[0], HEADS, 32), np.float32)
        p[:, :, :HD1] = w.reshape(w.shape[0], HEADS, HD1)
        return p.reshape(w.shape[0], 3, 128)

    qkv2 = a["L0_ffn_w_qkv"].reshape(E, HEADS + 2 * KV, HD2)
    pair_heads = [(0, 4), (1, 5), (2, 6), (3, 7), (8, 9), (10, 11), (12, 13), (14, 14)]
    wqk2 = np.stack([np.concatenate([qkv2[:, p], qkv2[:, q]], axis=1) for p, q in pair_heads], axis=1)
    row_heads = [0, 1, 2, 3, 4, 5, 6, 7, 8, 10, 9, 11]
    qkv3 = a["L1_attn_w_qkv"].T
    arrays = {
        "consts": constants(),
        "patches": patches.reshape(TILES, ROWS, PD),
        "w_patch": channels_first(a["L0_tok_W"]),
        "ln1_gb": ln1.reshape(2, PCH, 128).transpose(2, 0, 1),
        "rows_e": np.stack([a["L0_tok_b"], a["L0_tok_ln2_g"], a["L0_tok_ln2_b"], a["L0_attn_ln_w"], a["L0_attn_ln_b"]]),
        "pos_rows": np.concatenate([pos] * PER_TILE),
        "cls_rows": cls_rows.reshape(ROWS, E),
        "slopes": a["L0_attn_log_slope"],
        "wqk1": np.stack([padded_heads(a["L0_attn_Wq"]), padded_heads(a["L0_attn_Wk"])], axis=1),
        "wvo1": np.stack([a["L0_attn_Wv"], a["L0_attn_Wo"]], axis=1),
        "wg1": a["L0_attn_Wg1"],
        "wg2": a["L0_attn_Wg2"],
        "norm_cols": np.stack([a["L0_ffn_norm1_w"], a["L0_ffn_norm2_w"]]).reshape(2, 2, KH).transpose(2, 1, 0),
        "wqk2": wqk2,
        "wv2": qkv2[:, HEADS + KV:].reshape(E, E),
        "wout2": a["L0_ffn_w_out"].reshape(HEADS, HD2, E)[row_heads].reshape(HEADS * HD2, E),
        "wrouter0": a["L0_ffn_w_router"],
        "w_gate_up": a["L0_ffn_w_gate_up"],
        "w_down": a["L0_ffn_w_down"],
        "w_tern": np.concatenate([padded_heads(qkv3[:, :E]).reshape(E, 384), padded_heads(qkv3[:, E:2 * E]).reshape(E, 384),
                                  qkv3[:, 2 * E:], a["L1_attn_w_proj"].T], axis=1),
        "g_tern": np.stack([a["L1_attn_g_qkv"], a["L1_attn_g_proj"]]),
        "w_gate1": a["L1_ffn_gate_weight"].T,
        "gate_bias": a["L1_ffn_gate_bias"],
        "w13": np.concatenate([np.concatenate([a["L1_ffn_w1"], a["L1_ffn_sw1"][None]]).transpose(0, 2, 1),
                               np.concatenate([a["L1_ffn_w3"], a["L1_ffn_sw3"][None]]).transpose(0, 2, 1)], axis=2),
        "w2": np.concatenate([a["L1_ffn_w2"], a["L1_ffn_sw2"][None]]).transpose(0, 2, 1),
    }
    nc = _bacc.Bacc("TRN2", target_bir_lowering=False, num_devices=1)
    args = []
    for name, value in arrays.items():
        arrays[name] = value = np.ascontiguousarray(value)
        args.append(nc.dram_tensor(name, value.shape, mybir.dt.from_np(value.dtype), kind="ExternalInput").ap())
    out = nc.dram_tensor("out", (TOKENS, E), F32, kind="ExternalOutput").ap()
    vit_tower(nc, *args, out)
    r = _run(nc, [arrays], core_ids=[0])
    return r.results[0]["out"].reshape(_OUT)
```

```python
from contextlib import ExitStack

import numpy as np

import concourse.bass as bass
from concourse import mybir

ALU = mybir.AluOpType
ACT = mybir.ActivationFunctionType
AX = mybir.AxisListType
F32 = mybir.dt.float32
BF16 = mybir.dt.bfloat16
U32 = mybir.dt.uint32

IMAGES = 16
PATCHES = 36
SEQ = PATCHES + 1
PER_TILE = 3
ROWS = PER_TILE * SEQ
TILES = -(-IMAGES // PER_TILE)
GROUP = 3
GROUPS = TILES // GROUP
COLS = GROUP * ROWS
TOKENS = IMAGES * SEQ
E = 192
KH = E // 2
PD = 768
PCH = PD // 128
HEADS = 12
HD1 = E // HEADS
HD2 = 64
KV = 3
REP = HEADS // KV
EXPERTS0, FF0 = 16, 384
EXPERTS1, FF1 = 8, 128
MASKED = -1e30
MAGIC = 1.5 * 2.0 ** 23
RING = 4

BLOCK = 128
ASSIGNED = 2 * TOKENS
BLOCKS = (ASSIGNED + EXPERTS0 * (BLOCK - 1)) // BLOCK
OVERFLOW = BLOCKS - EXPERTS0
MORE = -(-TOKENS // BLOCK) - 1
SLOTS = BLOCKS * BLOCK
STAGES = {"first": range(EXPERTS0 + 3), "late": range(EXPERTS0 + 3, BLOCKS)}

CONST_PARTS = (("ident", 128), ("swap", 128), ("causal", ROWS), ("block", ROWS), ("ahead", ROWS),
               ("keep", ROWS), ("is_patch", 1), ("iota", EXPERTS0), ("cos", 2 * SEQ), ("sin", 2 * SEQ),
               ("before", 128), ("is_one", EXPERTS0), ("own_slot", EXPERTS0), ("over_slot", EXPERTS0), ("steps", MORE),
               ("block_no", OVERFLOW), ("position", BLOCK), ("block_at", BLOCKS),
               ("id_high", 2 * TILES), ("id_low", 2 * TILES), ("spare", BLOCKS))
CONST_AT = {}
_at = 0
for _name, _width in CONST_PARTS:
    CONST_AT[_name] = (_at, _width)
    _at += _width
CONST_WIDTH = _at

LN_PATCH, LN_EMBED, LN_H0, LN_DECAY, LN_H1, RMS_GQA, RMS_MOE, LN_H2, RMS_TERN, RMS_PROJ, LN_H3 = range(11)
NORMS = 11
NORM_ORDER = ([(LN_PATCH, g) for g in range(GROUPS)]
              + [(n, g) for g in range(GROUPS) for n in (LN_EMBED, LN_H0)]
              + [(n, g) for g in range(GROUPS) for n in (LN_DECAY, RMS_GQA, LN_H1)]
              + [(RMS_MOE, g) for g in range(GROUPS)]
              + [(RMS_TERN, g) for g in range(GROUPS)]
              + [(n, g) for n in (RMS_PROJ, LN_H3) for g in range(GROUPS)])
EPS = {n: 1e-6 if n in (RMS_GQA, RMS_MOE) else 1e-5 for n in range(NORMS)}


def live_cols(g):
    return min(COLS, TOKENS - g * COLS)


class Semaphores(dict):

    def __init__(self, nc, ctx):
        super().__init__()
        self.nc, self.ctx = nc, ctx

    def __missing__(self, name):
        self[name] = self.ctx.enter_context(self.nc.semaphore(name))
        return self[name]


def vit_tower(nc, consts, patches, w_patch, ln1_gb, rows_e, pos_rows, cls_rows, slopes, wqk1, wv1, wo1, wg1, wg2,
              norm_cols, wqk2, wv2, wout2, wrouter0, w_gate_up, w_down, w_tern, g_tern, w_gate1, gate_bias,
              w13, w2, out):
    with ExitStack() as ctx:
        S = Semaphores(nc, ctx)

        def sb(name, shape, dt=F32):
            return ctx.enter_context(nc.sbuf_tensor(name, shape, dt))

        c_sb = sb("consts_sb", [128, CONST_WIDTH])
        xs_dram = nc.dram_tensor("xs_dram", (TOKENS, E), F32, kind="Internal").ap()
        ys_dram = nc.dram_tensor("ys_dram", (2 * TOKENS + SLOTS, E), F32, kind="Internal").ap()
        ln1_sb = sb("ln1_gb_sb", [128, 2, PCH])
        re_sb = sb("rows_e_sb", [ROWS, 5, E])
        slope_sb = sb("slope_sb", [ROWS, HEADS])
        wqk1_sb = sb("wqk1_sb", [KH, 2, 2, 3, 128])
        wv1_sb = sb("wv1_sb", [KH, 2, E])
        wo1_sb = sb("wo1_sb", [128, 3, E])
        wg1_sb = sb("wg1_sb", [KH, 2, KH])
        wg2_sb = sb("wg2_sb", [KH, 3, 128])
        ncol_sb = sb("norm_cols_sb", [KH, 2, 2])
        wqk2_sb = sb("wqk2_sb", [KH, 2, 8, 128])
        wv2_sb = sb("wv2_sb", [KH, 2, E])
        wout2_sb = sb("wout2_sb", [128, 6, E])
        wr0_sb = sb("wr0_sb", [KH, 2, EXPERTS0])
        wt_sb = sb("w_tern_sb", [KH, 2, 5 * E + E])
        gt_sb = sb("g_tern_sb", [ROWS, 2, E])
        wr1_sb = sb("wr1_sb", [KH, 2, EXPERTS1])
        gb_sb = sb("gate_bias_sb", [ROWS, EXPERTS1])
        UP_SLOTS, DOWN_SLOTS = 3, 4

        def const(name, rows=128):
            at, width = CONST_AT[name]
            return c_sb[0:rows, at:at + width]

        ident = const("ident")

        decay = sb("decay", [ROWS, 4, 3, ROWS])
        ident_bf = sb("ident_bf", [128, 128], BF16)
        causal_bf = sb("causal_bf", [ROWS, ROWS], BF16)
        block_bf = sb("block_bf", [ROWS, ROWS], BF16)
        ones = sb("ones", [128, 128])
        half_neg = sb("half_neg", [ROWS, TILES])
        tern = sb("tern", [KH, 2, 6 * E], BF16)
        tern_f = wt_sb
        tern_abs = sb("tern_abs", [KH, 2])
        tern_mean = sb("tern_mean", [128, 2])
        tern_scale = sb("tern_scale", [128, 2])

        area_a = sb("area_a", [128, TILES * PD])
        area_b = sb("area_b", [128, PCH * TILES * ROWS])
        area_c = sb("area_c", [128, 8 * TILES * ROWS])
        area_d = sb("area_d", [128, 12 * COLS])

        def part(area, at, rows, pattern, **sizes):
            n = 1
            for size in sizes.values():
                n *= size
            return area[0:rows, at:at + n].rearrange(f"rows ({pattern}) -> rows {pattern}", **sizes)

        patch_x = part(area_a, 0, ROWS, "t n", t=TILES, n=PD)
        w13_sb = part(area_a, 0, KH, "c e n", c=2, e=EXPERTS1 + 1, n=2 * FF1)
        patch_t = part(area_b, 0, 128, "c n", c=PCH, n=TILES * ROWS)
        w2_sb = part(area_b, 0, FF1, "e n", e=EXPERTS1 + 1, n=E)
        stats = sb("stats", [ROWS, TILES, 2, 6])
        mv = sb("mean_var", [ROWS, NORMS, TILES, 2])
        ve = sb("var_eps", [ROWS, NORMS, TILES])
        vt = sb("var_tmp", [ROWS, NORMS, TILES])
        rstd = sb("rstd", [ROWS, NORMS, TILES])
        y0 = sb("y0", [ROWS, TILES, E])
        z0 = sb("z0", [ROWS, TILES, E])
        h = [sb(f"h{n}", [ROWS, TILES, E]) for n in range(3)]
        h.append(h[0])
        xn = sb("xn", [ROWS, TILES, E])
        x_t = sb("x_t", [KH, 2, TILES * ROWS])
        qk1 = part(area_c, 0, 128, "a m n", a=2, m=3, n=TILES * ROWS)
        v1 = part(area_d, 0, ROWS, "t n", t=TILES, n=E)
        v1_wide = area_d[0:ROWS, 0:TILES * E + HD1]
        g1_t = part(area_d, TILES * E + HD1, KH, "n", n=TILES * ROWS)
        gate1, o1_c = (part(area_a, n * 3 * TILES * ROWS, 128, "m n", m=3, n=TILES * ROWS) for n in range(2))
        o_rows = sb("o_rows", [ROWS, TILES, E])
        PB = 3
        area_e = sb("area_e", [128, 2 * PB * HEADS * ROWS])
        p_buf = part(area_e, 0, ROWS, "s p n", s=PB, p=HEADS, n=ROWS)
        pt_buf = part(area_e, PB * HEADS * ROWS, ROWS, "s p n", s=PB, p=HEADS, n=ROWS)
        wp_sb = part(area_e, 0, 128, "c n", c=PCH, n=E)
        pos_sb, cls_sb, gm_rows, add_rows = (area_e[0:ROWS, (PCH + n) * E:(PCH + n + 1) * E] for n in range(4))
        wgu_sb = part(area_e, 0, KH, "s c n", s=UP_SLOTS, c=2, n=2 * FF0)
        wdn_sb = part(area_e, UP_SLOTS * 4 * FF0, 128, "s c n", s=DOWN_SLOTS, c=3, n=E)
        x2 = y0
        raw, rsin, rcos = (part(area_d, 4 * n * COLS, 128, "s b n", s=2, b=2, n=COLS) for n in range(3))
        qk2 = part(area_c, 0, 128, "m n", m=8, n=TILES * ROWS)
        v2 = sb("v2", [ROWS, TILES, KV, HD2])
        nmax = sb("nmax", [ROWS, TILES, HEADS])
        rsum = sb("rsum", [ROWS, TILES, HEADS])
        o2_t = patch_t
        hh = z0
        m_t = x_t
        lg = sb("lg", [ROWS, TILES, EXPERTS0])
        top = sb("top", [ROWS, TILES, 8])
        top_i = sb("top_i", [ROWS, TILES, 8], U32)
        top_f = sb("top_f", [ROWS, TILES, 2])
        slot_id, slot_tmp, slot_blank, source_u, dest_u = (
            part(area_d, TILES * BLOCK + 4 * TILES * BLOCKS + n * BLOCKS, 128, "n", n=BLOCKS) for n in range(5))
        source_u, dest_u = source_u.bitcast(U32), dest_u.bitcast(U32)
        before_bf = sb("before_bf", [128, 128], BF16)
        ones_bf = sb("ones_bf", [128, 128], BF16)
        hot = sb("hot", [ROWS, 2, TILES, EXPERTS0])
        hot_bf = sb("hot_bf", [ROWS, TILES + 1, EXPERTS0], BF16)
        over = sb("over", [ROWS, EXPERTS0, MORE])
        share = sb("share", [ROWS, 4, EXPERTS0])
        slot_f = sb("slot_f", [ROWS, 2, TILES, 1])
        slot_tile = sb("slot_tile", [ROWS, 3, 2 * TILES])
        over_f = sb("over_f", [1, OVERFLOW, EXPERTS0])
        over_n = sb("over_n", [1, OVERFLOW])
        over_u = sb("over_u", [1, OVERFLOW], U32)
        used_u = sb("used_u", [1, 1], U32)
        pair_w = sb("pair_w", [ROWS, 2, TILES])
        rt = [sb(f"rt{n}", [ROWS, TILES, EXPERTS0]) for n in range(6)]
        rden = sb("rden", [ROWS, TILES, 2])
        XB, YB = 4, 3
        xb = part(area_c, 0, 128, "s n", s=XB, n=E)
        xb_t = part(area_c, XB * E, KH, "s c n", s=2, c=2, n=BLOCK)
        sb_silu = part(area_c, XB * E + 512, 128, "s n", s=2, n=FF0)
        hid_t = part(area_c, XB * E + 512 + 2 * FF0, 128, "s c n", s=2, c=3, n=BLOCK)
        yb = part(area_c, XB * E + 512 + 4 * FF0, 128, "s n", s=YB, n=E)
        yg = part(area_c, 8 * TILES * ROWS - 2 * TILES * E, ROWS, "k t n", k=2, t=TILES, n=E)
        xr = part(area_d, 2 * TILES * E, ROWS, "t n", t=TILES, n=E)
        at_position = area_d[0:ROWS, 0:TILES * BLOCK].bitcast(BF16).rearrange("p (k n) -> p k n", k=2 * TILES)
        in_block = part(area_d, TILES * BLOCK, ROWS, "k n", k=2 * TILES, n=BLOCKS)
        block_id = area_d[0:ROWS, TILES * BLOCK + 2 * TILES * BLOCKS:TILES * BLOCK + 4 * TILES * BLOCKS].bitcast(
            BF16).rearrange("p (k a n) -> p k a n", k=2 * TILES, a=2)
        silu_buf = part(area_c, 0, 128, "s n", s=2, n=TOKENS)
        hid = part(area_c, 2 * TOKENS, 128, "s c n", s=2, c=3, n=TOKENS)

        q_scale = sb("q_scale", [ROWS, TILES])
        amax = sb("amax", [ROWS, TILES, 4])
        q_int = xn[:, TILES // 2:, :].bitcast(BF16).rearrange("p a (b n) -> p (a b) n", n=E)
        q_int_t = area_d[0:KH, 4 * COLS:6 * COLS].bitcast(BF16).rearrange("p (c n) -> p c n", c=2)
        qa = y0
        qb = z0
        diag = part(area_d, 6 * COLS + TILES * HEADS * (HD1 + 1) + 32, ROWS, "s n", s=2, n=ROWS)
        dq = area_d[:, 0:TILES * ROWS]
        qk3 = qk1
        v3 = part(area_d, 6 * COLS, ROWS, "t h n", t=TILES, h=HEADS, n=HD1 + 1)
        v3_wide = part(area_d, 6 * COLS, ROWS, "n", n=TILES * HEADS * (HD1 + 1) + 32)
        o3_c = part(area_b, (EXPERTS1 + 1) * E, 128, "s n", s=2, n=COLS)
        o3 = o_rows
        comb1 = rt[5][:, :, 0:EXPERTS1]

        psum = [ctx.enter_context(nc.psum_tensor(f"slot{n}", [128, 2, 512], F32)) for n in range(RING)]

        def by_tile(slot, width=E, rows=ROWS):
            return slot[:].rearrange("p b (s x) -> p (b s) x", s=2)[0:rows, 0:GROUP, 0:width]

        def tile_cols(t):
            return slice(t * ROWS, (t + 1) * ROWS)

        def group_tiles(g):
            return range(g * GROUP, (g + 1) * GROUP)

        def gt(g):
            return slice(g * GROUP, (g + 1) * GROUP)

        def gcols(g, n=COLS):
            return slice(g * COLS, g * COLS + n)

        def on_tiles(ap, n=GROUP):
            return ap.unsqueeze(1).to_broadcast([ap.shape[0], n, ap.shape[1]])

        def along(ap, n):
            return ap.unsqueeze(2).to_broadcast([ap.shape[0], ap.shape[1], n])

        slot_of = {}
        ring = {"uses": 0, "freed": [[] for _ in range(RING)]}

        def take(pe, key, *freed_by):
            n = ring["uses"] % RING
            for s, value in ring["freed"][n]:
                pe.wait_ge(S[s], value)
            ring["freed"][n] = list(freed_by)
            ring["uses"] += 1
            slot_of[key] = psum[n]
            return psum[n]

        def nth(norm, g):
            return NORM_ORDER.index((norm, g)) + 1

        def late_needed(engine):
            used = engine.value_load(used_u[0:1, 0:1], min_val=0, max_val=OVERFLOW)
            return used > len(STAGES["first"]) - EXPERTS0

        block = ctx.enter_context(nc.Block())

        @block.tensor
        def _(pe):
            mm, tr = nc.tensor.matmul, nc.tensor.transpose

            def rows_to_columns(src, g, key, ready, *freed_by):
                slot = take(pe, key, *freed_by)
                for c in range(2):
                    for i, t in enumerate(group_tiles(g)):
                        last = tr(slot[0:KH, c, i * ROWS:(i + 1) * ROWS], src[:, t, c * KH:(c + 1) * KH],
                                  ident[0:ROWS, 0:ROWS])
                last.then_inc(S[ready], 1)

            def project_rows(lhs, w, g, key, ready, *freed_by):
                slot = take(pe, key, *freed_by)
                for i, t in enumerate(group_tiles(g)):
                    for c in range(2):
                        last = mm(by_tile(slot, w.shape[2])[:, i, :], lhs[:, c, tile_cols(t)], w[:, c, :],
                                  start=(c == 0), stop=(c == 1))
                last.then_inc(S[ready], 1)

            pe.wait_ge(S["consts_loaded"], 16)
            for g in range(GROUPS):
                pe.wait_ge(S["patch_normed"], g + 1)
                for u in range(PCH // 2):
                    freed = ([("patch_t_dve", u + 1), ("patch_t_act", u + 1)] if g == 0
                             else [("patch_t_act", PCH // 2 + 2 * (u + 1))])
                    slot = take(pe, ("patch_t", g, u), *freed)
                    for b in range(2):
                        c = 2 * u + b
                        for i, t in enumerate(group_tiles(g)):
                            last = tr(slot[:, b, i * ROWS:(i + 1) * ROWS], patch_x[:, t, c * 128:(c + 1) * 128],
                                      ident[0:ROWS, 0:ROWS])
                    last.then_inc(S["patch_turned"], 1)
                pe.wait_ge(S["w_patch_loaded"], 16)
                pe.wait_ge(S["patch_t_dve"], PCH // 2)
                pe.wait_ge(S["patch_t_act"], PCH // 2 + g * PCH)
                slot = take(pe, ("embed", g), ("embed_biased", g + 1))
                for i, t in enumerate(group_tiles(g)):
                    for c in range(PCH):
                        last = mm(by_tile(slot)[:, i, :], patch_t[:, c, tile_cols(t)], wp_sb[:, c, :],
                                  start=(c == 0), stop=(c == PCH - 1))
                last.then_inc(S["embed_done"], 1)

            pe.wait_ge(S["w_attn1_loaded"], 80)
            for g in range(GROUPS):
                pe.wait_ge(S["x_normed"], g + 1)
                rows_to_columns(xn, g, ("x0_t", g), "x_turned", ("x_t_ready", g + 1))
                pe.wait_ge(S["x_t_ready"], g + 1)
                for m in range(3):
                    slot = take(pe, ("qk1", g, m), ("qk1_silu", 3 * g + m + 1))
                    for b in range(2):
                        for c in range(2):
                            last = mm(slot[:, b, 0:COLS], wqk1_sb[:, c, b, m, :], x_t[:, c, gcols(g)],
                                      start=(c == 0), stop=(c == 1))
                    last.then_inc(S["qk1_done"], 1)
                project_rows(x_t, wv1_sb, g, ("v1", g), "v1_done", ("v1_silu", g + 1))
                slot = take(pe, ("g1", g), ("g1_copied", g + 1))
                for c in range(2):
                    last = mm(slot[0:KH, 0, 0:COLS], wg1_sb[:, c, :], x_t[:, c, gcols(g)], start=(c == 0), stop=(c == 1))
                last.then_inc(S["g1_done"], 1)
                pe.wait_ge(S["g1_copied"], g + 1)
                for u, parts in enumerate(((0, 1), (2,))):
                    slot = take(pe, ("gate1", g, u), ("gate1_tanh", 2 * g + u + 1))
                    for b, m in enumerate(parts):
                        last = mm(slot[:, b, 0:COLS], wg2_sb[:, m, :], g1_t[:, gcols(g)], start=True, stop=True)
                    last.then_inc(S["gate1_done"], 1)

            def energies(t):
                for jp in range(2):
                    slot = take(pe, ("energy", t, jp), ("energy_decayed", 2 * t + jp + 1))
                    for m in range(3):
                        for b in range(2):
                            r = 32 * (2 * jp + b)
                            last = mm(slot[0:ROWS, b, m * ROWS:(m + 1) * ROWS], qk1[r:r + 32, 1, m, tile_cols(t)],
                                      qk1[r:r + 32, 0, m, tile_cols(t)], start=True, stop=True)
                    last.then_inc(S["energy_done"], 1)

            def decay_values(t):
                slot = take(pe, ("decay_out", t), ("o1_gated", t + 1))
                pe.wait_ge(S["energy_decayed"], 2 * t + 2)
                for m in range(3):
                    for j in range(4):
                        at = t * E + (4 * m + j) * HD1
                        last = mm(slot[32 * j:32 * j + 32, 0, m * ROWS:(m + 1) * ROWS], v1_wide[:, at:at + 32],
                                  p_buf[:, t % PB, j * 3 + m, :], start=True, stop=True)
                last.then_inc(S["decay_out_done"], 1)

            pe.wait_ge(S["v1_silu"], GROUPS)
            pe.wait_ge(S["v1_edge"], 1)
            def project_out1(g):
                pe.wait_ge(S["o1_gated"], 3 * g + 3)
                slot = take(pe, ("attn1", g), ("attn1_normed", g + 1))
                for i, t in enumerate(group_tiles(g)):
                    for m in range(3):
                        last = mm(by_tile(slot)[:, i, :], o1_c[:, m, tile_cols(t)], wo1_sb[:, m, :],
                                  start=(m == 0), stop=(m == 2))
                last.then_inc(S["attn1_done"], 1)

            for t in range(TILES):
                pe.wait_ge(S["qk1_silu"], 3 * (t // GROUP) + 3)
                if t == GROUP + 1:
                    project_out1(0)
                energies(t)
                if t:
                    decay_values(t - 1)
            decay_values(TILES - 1)

            pe.wait_ge(S["w_attn2_loaded"], 64)
            def project_qk2(g, u):
                n = 4 * g + u
                slot = take(pe, ("qk2", g, u), ("qk2_raw", n + 1))
                for b in range(2):
                    for c in range(2):
                        last = mm(slot[:, b, 0:COLS], wqk2_sb[:, c, 2 * u + b, :], x_t[:, c, gcols(g)],
                                  start=(c == 0), stop=(c == 1))
                last.then_inc(S["qk2_done"], 1)

            def swap_qk2(g, u):
                n = 4 * g + u
                pe.wait_ge(S["qk2_raw"], n + 1)
                slot = take(pe, ("swap", g, u), ("qk2_sin", n + 1))
                for b in range(2):
                    last = mm(slot[:, b, 0:COLS], const("swap"), raw[:, n % 2, b, :], start=True, stop=True)
                last.then_inc(S["qk2_swapped"], 1)

            for g in range(GROUPS):
                pe.wait_ge(S["x_normed"], 2 + g + 1)
                rows_to_columns(xn, g, ("x1_t", g), "x_turned", ("x_t_ready", 2 + g + 1))
                if g == 0:
                    project_out1(1)
                pe.wait_ge(S["x_t_ready"], 2 + g + 1)
                for u in range(4):
                    project_qk2(g, u)
                    if u:
                        swap_qk2(g, u - 1)
                project_rows(x_t, wv2_sb, g, ("v2", g), "v2_done", ("v2_copied", g + 1))
                swap_qk2(g, 3)

            pe.wait_ge(S["masks_made"], 1)

            def masked_scores2(t):
                for u, heads in enumerate((REP, 2)):
                    slot = take(pe, ("score2", t, u), ("probs", 2 * t + u + 1))
                    for b in range(2):
                        mm(slot[0:ROWS, b, 0:heads * ROWS], ident_bf[0:ROWS, 0:ROWS],
                           on_tiles(causal_bf[:], heads), start=True, stop=False, skip_group_check=True)
                    for i in range(heads):
                        for b in range(2):
                            q, k = (i, 6) if u == 0 else (4 + i, 7)
                            r = 64 * b
                            last = mm(slot[0:ROWS, b, i * ROWS:(i + 1) * ROWS], qk2[r:r + 64, q, tile_cols(t)],
                                      qk2[r:r + 64, k, tile_cols(t)], start=False, stop=True, skip_group_check=True)
                    last.then_inc(S["score_done"], 1)

            def turn_probs(base, t):
                for u, heads in enumerate((8, 4)):
                    n = base + t
                    slot = take(pe, ("probs_t", n, u), ("probs_t_dve" if u == 0 else "probs_t_act", n + 1))
                    if base == 0:
                        pe.wait_ge(S["probs_scaled"], 2 * n + u + 1)
                    else:
                        pe.wait_ge(S["probs"], 2 * n + 2)
                    for i in range(heads):
                        last = tr(slot[0:ROWS, i // 4, (i % 4) * ROWS:(i % 4 + 1) * ROWS],
                                  p_buf[:, (TILES + n) % PB, 8 * u + i, :], ident[0:ROWS, 0:ROWS])
                    last.then_inc(S["probs_turned"], 1)

            def attend2(t):
                pe.wait_ge(S["probs_t_dve"], t + 1)
                pe.wait_ge(S["probs_t_act"], t + 1)
                slot = take(pe, ("attend2", t), ("o2_t_ready", t + 1))
                for b, at, heads, kvs in ((0, 0, 4, (0, 1)), (1, 8, 2, (2, 2))):
                    for half, kv in enumerate(kvs):
                        first = at + half * heads
                        last = mm(slot[64 * half:64 * half + 64, b, 0:heads * ROWS], v2[:, t, kv, :],
                                  pt_buf[:, t % PB, first:first + heads, :], start=True, stop=True)
                last.then_inc(S["attended"], 1)

            def project_out2(g):
                pe.wait_ge(S["o2_t_ready"], 3 * g + 3)
                slot = take(pe, ("attn2", g), ("hh_ready", g + 1))
                for i, t in enumerate(group_tiles(g)):
                    for c in range(6):
                        last = mm(by_tile(slot)[:, i, :], o2_t[:, c, tile_cols(t)], wout2_sb[:, c, :],
                                  start=(c == 0), stop=(c == 5))
                last.then_inc(S["attn2_done"], 1)

            for t in range(TILES):
                pe.wait_ge(S["qk2_rotated"], 4 * (t // GROUP) + 4)
                pe.wait_ge(S["v2_copied"], t // GROUP + 1)
                masked_scores2(t)
                if t >= 1:
                    turn_probs(0, t - 1)
                if t >= 2:
                    attend2(t - 2)
            project_out2(0)
            turn_probs(0, TILES - 1)
            attend2(TILES - 2)
            attend2(TILES - 1)
            project_out2(1)

            for g in range(GROUPS):
                pe.wait_ge(S["x_normed"], 4 + g + 1)
                rows_to_columns(xr, g, ("m_t", g), "x_turned", ("m_t_ready", g + 1))
                pe.wait_ge(S["m_t_ready"], g + 1)
                project_rows(m_t, wr0_sb, g, ("logits0", g), "logits0_done", ("logits0_copied", g + 1))

            def feed_up(n, w, columns):
                for part in range(2):
                    slot = take(pe, ("ff", n, part), ("ff_silu" if part == 0 else "ff_hidden", n + 1))
                    for c in range(2):
                        for g in range(GROUPS):
                            last = mm(slot[:, g, 0:live_cols(g)], w(c, part), columns[:, c, gcols(g, live_cols(g))],
                                      start=(c == 0), stop=(c == 1))
                    last.then_inc(S["ff_up"], 1)

            def feed_down(n, down, pieces, hidden_after):
                for g in range(GROUPS):
                    slot = take(pe, ("down", n, g), ("ff_added", GROUPS * n + g + 1))
                    pe.wait_ge(S["ff_hidden"], hidden_after)
                    for i, t in enumerate(group_tiles(g)):
                        rows = min(ROWS, TOKENS - t * ROWS)
                        for c in range(pieces):
                            last = mm(by_tile(slot, rows=rows)[:, i, :], hid[:, n % 2, c, t * ROWS:t * ROWS + rows],
                                      down[:, c, :], start=(c == 0), stop=(c == pieces - 1))
                    last.then_inc(S["ff_down"], 1)

            pe.wait_ge(S["hot_ready"], 1)
            slot = take(pe, "ranks", ("ranks_used", 1))
            mm(slot[0:ROWS, 0, 0:(TILES + 1) * EXPERTS0], before_bf[0:ROWS, 0:ROWS], hot_bf[:], start=True, stop=False)
            for t in range(TILES):
                rows = min(ROWS, TOKENS - t * ROWS)
                last = mm(slot[0:ROWS, 0, (t + 1) * EXPERTS0:(TILES + 1) * EXPERTS0], ones_bf[0:rows, 0:ROWS],
                          on_tiles(hot_bf[0:rows, t, :], TILES - t), start=False, stop=(t == TILES - 1))
            last.then_inc(S["ranks_done"], 1)

            pe.wait_ge(S["slots_found"], 1)
            slot = take(pe, "slot_ids", ("slots_ready", 1))
            for k in range(2):
                for t in range(TILES):
                    rows = min(ROWS, TOKENS - t * ROWS)
                    n = k * TILES + t
                    last = mm(slot[:, 0, 0:2 * BLOCKS], at_position[0:rows, n, :],
                              block_id[0:rows, n].rearrange("p a n -> p (a n)"), start=(n == 0), stop=(n == 2 * TILES - 1))
            last.then_inc(S["slot_ids_done"], 1)

            pe.wait_ge(S["tern_summed"], 2)
            slot = take(pe, "tern_sum", ("tern_mean_ready", 1))
            mm(slot[:, 0, 0:2], ones[0:KH, :], tern_abs[:], start=True, stop=True).then_inc(S["tern_sum_done"], 1)

            def run_blocks(when):
                blocks = STAGES[when]

                def turn_block(n):
                    pe.wait_ge(S[f"{when}_in{n % XB}"], 16 * (n // XB + 1))
                    slot = take(pe, (when, "turned", n), (f"{when}_columns", n + 1))
                    for c in range(2):
                        last = tr(slot[0:KH, 0, c * BLOCK:(c + 1) * BLOCK], xb[:, n % XB, c * KH:(c + 1) * KH], ident)
                    last.then_inc(S[f"{when}_turned"], 1)

                def block_up(n):
                    pe.wait_ge(S[f"{when}_columns"], n + 1)
                    pe.wait_ge(S[f"{when}_up_loaded{n % UP_SLOTS}"], 16 * (n // UP_SLOTS + 1))
                    slot = take(pe, (when, "up", n), (f"{when}_hidden", n + 1))
                    for gate_or_up in range(2):
                        for m in range(FF0 // 128):
                            at = gate_or_up * FF0 + m * 128
                            for c in range(2):
                                last = mm(slot[:, gate_or_up, m * BLOCK:(m + 1) * BLOCK],
                                          wgu_sb[:, n % UP_SLOTS, c, at:at + 128], xb_t[:, n % 2, c, :],
                                          start=(c == 0), stop=(c == 1))
                        last.then_inc(S[f"{when}_up"], 1)

                def block_down(n):
                    pe.wait_ge(S[f"{when}_hidden"], n + 1)
                    pe.wait_ge(S[f"{when}_down_loaded{n % DOWN_SLOTS}"], 16 * (n // DOWN_SLOTS + 1))
                    slot = take(pe, (when, "down", n), (f"{when}_out", n + 1))
                    for c in range(3):
                        last = mm(slot[:, 0, 0:E], hid_t[:, n % 2, c, :], wdn_sb[:, n % DOWN_SLOTS, c, :],
                                  start=(c == 0), stop=(c == 2))
                    last.then_inc(S[f"{when}_down"], 1)

                turn_block(0)
                for n in range(len(blocks) + 1):
                    if n + 1 < len(blocks):
                        turn_block(n + 1)
                    if n < len(blocks):
                        block_up(n)
                    if n >= 1:
                        block_down(n - 1)
                pe.wait_ge(S[f"{when}_out"], len(blocks))
                ring["freed"] = [[] for _ in range(RING)]

            pe.wait_ge(S["slots_ready"], 1)
            late = late_needed(pe)
            run_blocks("first")
            with pe.If(late):
                run_blocks("late")


            def turn_ints(g, n):
                pe.wait_ge(S["quantised"], n + 1)
                slot = take(pe, ("ints_t", n), ("ints_t_ready", n + 1))
                view = slot[:].bitcast(BF16)
                for c in range(2):
                    for i, t in enumerate(group_tiles(g)):
                        last = tr(view[0:KH, c, i * 112:i * 112 + ROWS], q_int[:, t, c * KH:(c + 1) * KH],
                                  ident_bf[0:ROWS, 0:ROWS])
                last.then_inc(S["ints_turned"], 1)

            def project_ints(g):
                turn_ints(g, g)
                slot = take(pe, ("dq", g), ("dq_ready", g + 1))
                for i, t in enumerate(group_tiles(g)):
                    pe.wait_ge(S["diag_ready"], t + 1)
                    last = mm(slot[:, 0, i * ROWS:(i + 1) * ROWS], ones[0:ROWS, :], diag[:, t % 2, :],
                              start=True, stop=True)
                    last.then_inc(S["dq_done"], 1)
                pe.wait_ge(S["tern_ready"], 1)
                pe.wait_ge(S["ints_t_ready"], g + 1)
                for m in range(3):
                    slot = take(pe, ("qk3", g, m), ("k3_scaled", 3 * g + m + 1), ("q3_copied", 3 * g + m + 1))
                    for b in range(2):
                        for c in range(2):
                            at = b * 384 + m * 128
                            last = mm(slot[:, b, 0:COLS], tern[:, c, at:at + 128], q_int_t[:, c, gcols(g)],
                                      start=(c == 0), stop=(c == 1))
                    last.then_inc(S["qk3_done"], 1)
                project_rows(q_int_t, tern[:, :, 768:960], g, ("v3", g), "v3_done", ("v3_scaled", g + 1))

            def masked_scores3(t):
                n = TILES + t
                for jp in range(2):
                    slot = take(pe, ("score3", t, jp), ("below_max", 2 * t + jp + 1))
                    for b in range(2):
                        mm(slot[0:ROWS, b, 0:COLS], ident_bf[0:ROWS, 0:ROWS], on_tiles(block_bf[:], 3),
                           start=True, stop=False, skip_group_check=True)
                    for m in range(3):
                        for b in range(2):
                            r = 32 * (2 * jp + b)
                            last = mm(slot[0:ROWS, b, m * ROWS:(m + 1) * ROWS], qk3[r:r + 32, 0, m, tile_cols(t)],
                                      qk3[r:r + 32, 1, m, tile_cols(t)], start=False, stop=True, skip_group_check=True)
                    last.then_inc(S["score_done"], 1)

            def attend3(t):
                n = TILES + t
                pe.wait_ge(S["probs_t_dve"], n + 1)
                pe.wait_ge(S["probs_t_act"], n + 1)
                slot = take(pe, ("attend3", t), ("o3_columns", t + 1))
                for m in range(3):
                    for j in range(4):
                        p = 3 * j + m
                        at = (t * HEADS + 4 * m + j) * (HD1 + 1)
                        last = mm(slot[32 * j:32 * j + 32, 0, m * ROWS:(m + 1) * ROWS], v3_wide[:, at:at + 32],
                                  pt_buf[:, n % PB, p, :], start=True, stop=True)
                last.then_inc(S["attended"], 1)

            def turn_back3(t):
                pe.wait_ge(S["o3_columns"], t + 1)
                slot = take(pe, ("o3_rows", t), ("o3_scaled", t + 1))
                for m in range(3):
                    last = tr(slot[0:ROWS, 0, m * 128:(m + 1) * 128], o3_c[:, t % 2, m * ROWS:(m + 1) * ROWS], ident)
                last.then_inc(S["o3_turned"], 1)

            project_ints(0)
            for t in range(TILES):
                if t == 1:
                    project_ints(1)
                pe.wait_ge(S["k3_scaled"], 3 * (t // GROUP) + 3)
                pe.wait_ge(S["q3_copied"], 3 * (t // GROUP) + 3)
                pe.wait_ge(S["v3_scaled"], t // GROUP + 1)
                masked_scores3(t)
                if t >= 1:
                    turn_probs(TILES, t - 1)
                if t >= 2:
                    attend3(t - 2)
                if t >= 3:
                    turn_back3(t - 3)
            def project_out3(g):
                pe.wait_ge(S["ints_t_ready"], 2 + g + 1)
                project_rows(q_int_t, tern[:, :, 960:1152], g, ("attn3", g), "attn3_done", ("h3_ready", g + 1))

            turn_probs(TILES, TILES - 1)
            turn_back3(TILES - 3)
            attend3(TILES - 2)
            attend3(TILES - 1)
            turn_back3(TILES - 2)
            turn_back3(TILES - 1)
            turn_ints(0, 2)
            project_out3(0)
            turn_ints(1, 3)
            project_out3(1)

            pe.wait_ge(S["w_ff1_loaded"], 80)
            order = [EXPERTS1] + list(range(EXPERTS1))

            def w13(n):
                return lambda c, part: w13_sb[:, c, order[n], part * FF1:(part + 1) * FF1]

            shared = []
            for g in range(GROUPS):
                pe.wait_ge(S["x_normed"], 6 + g + 1)
                rows_to_columns(xn, g, ("x4_t", g), "x_turned", ("x_t_ready", 4 + g + 1))
                if not shared:
                    shared = [take(pe, ("ff", 0, part), ("ff_silu" if part == 0 else "ff_hidden", 1)) for part in range(2)]
                pe.wait_ge(S["x_t_ready"], 4 + g + 1)
                for part in range(2):
                    for c in range(2):
                        last = mm(shared[part][:, g, 0:live_cols(g)], w13(0)(c, part), x_t[:, c, gcols(g, live_cols(g))],
                                  start=(c == 0), stop=(c == 1))
                    if g == GROUPS - 1:
                        last.then_inc(S["ff_up"], 1)
            for g in range(GROUPS):
                project_rows(x_t, wr1_sb, g, ("logits1", g), "logits1_done", ("logits1_sigmoid", g + 1))
            for n in range(1, EXPERTS1 + 2):
                if n <= EXPERTS1:
                    feed_up(n, w13(n), x_t)
                feed_down(n - 1, w2_sb[:, order[n - 1]].unsqueeze(1), 1, n)

        @block.sync
        def _(sp):
            def load(dst, src, sem):
                sp.dma_start(dst, src).then_inc(S[sem], 16)

            for t in range(TILES):
                load(patch_x[:, t, :], patches[t], f"patch_loaded{t // GROUP}")
            load(c_sb[:], consts, "consts_loaded")
            load(ln1_sb[:], ln1_gb, "ln1_loaded")
            load(wp_sb[:], w_patch.rearrange("(c p) e -> p c e", p=128), "w_patch_loaded")
            load(re_sb[:], rows_e.unsqueeze(0).to_broadcast([ROWS, 5, E]), "rows_loaded")
            load(pos_sb[:], pos_rows, "rows_loaded")
            load(cls_sb[:], cls_rows, "rows_loaded")
            load(slope_sb[:], slopes.unsqueeze(0).to_broadcast([ROWS, HEADS]), "slopes_loaded")
            load(wqk1_sb[:], wqk1.rearrange("(c p) a m n -> p c a m n", p=KH), "w_attn1_loaded")
            load(wv1_sb[:], wv1.rearrange("(c p) n -> p c n", p=KH), "w_attn1_loaded")
            load(wo1_sb[:], wo1, "w_attn1_loaded")
            load(wg1_sb[:], wg1, "w_attn1_loaded")
            load(wg2_sb[:], wg2, "w_attn1_loaded")
            load(ncol_sb[:], norm_cols, "norm_cols_loaded")
            load(wqk2_sb[:], wqk2.rearrange("(c p) m n -> p c m n", p=KH), "w_attn2_loaded")
            load(wv2_sb[:], wv2.rearrange("(c p) n -> p c n", p=KH), "w_attn2_loaded")
            load(wout2_sb[:], wout2.rearrange("(c p) n -> p c n", p=128), "w_attn2_loaded")
            load(wr0_sb[:], wrouter0.rearrange("(c p) n -> p c n", p=KH), "w_attn2_loaded")
            load(wt_sb[:], w_tern.rearrange("(c p) n -> p c n", p=KH), "w_tern_loaded")
            load(gt_sb[:], g_tern.unsqueeze(0).to_broadcast([ROWS, 2, E]), "g_tern_loaded")
            load(wr1_sb[:], w_gate1.rearrange("(c p) n -> p c n", p=KH), "w_ff1_loaded")
            load(gb_sb[:], gate_bias.unsqueeze(0).to_broadcast([ROWS, EXPERTS1]), "w_ff1_loaded")
            def expert_of(b):
                return b if b < EXPERTS0 else overflow_expert[b - EXPERTS0]

            def load_up(when, n):
                if n < len(STAGES[when]):
                    if n >= UP_SLOTS:
                        sp.wait_ge(S[f"{when}_up"], 2 * (n - UP_SLOTS + 1))
                    load(wgu_sb[:, n % UP_SLOTS], w_gate_up[expert_of(STAGES[when][n])].rearrange("(c p) n -> p c n", p=KH),
                         f"{when}_up_loaded{n % UP_SLOTS}")

            def load_down(when, n):
                if n < len(STAGES[when]):
                    if n >= DOWN_SLOTS:
                        sp.wait_ge(S[f"{when}_down"], n - DOWN_SLOTS + 1)
                    load(wdn_sb[:, n % DOWN_SLOTS], w_down[expert_of(STAGES[when][n])].rearrange("(c p) n -> p c n", p=128),
                         f"{when}_down_loaded{n % DOWN_SLOTS}")

            def first_weights(when):
                for n in range(UP_SLOTS):
                    load_up(when, n)
                    load_down(when, n)

            def stream_blocks(when):
                for n in range(len(STAGES[when])):
                    load_up(when, n + UP_SLOTS)
                    load_down(when, n + UP_SLOTS)

            sp.wait_ge(S["attended"], TILES)
            first_weights("first")
            for t in range(TILES):
                rows = min(ROWS, TOKENS - t * ROWS)
                sp.wait_ge(S["x_normed"], 4 + t // GROUP + 1)
                sp.dma_start(xs_dram[t * ROWS:t * ROWS + rows, :], xr[0:rows, t, :]).then_inc(S["rows_out"], 16)
            sp.wait_ge(S["slots_ready"], 1)
            late = late_needed(sp)
            overflow_expert = [sp.value_load(over_u[0:1, n:n + 1], min_val=0, max_val=EXPERTS0 - 1) for n in range(OVERFLOW)]
            stream_blocks("first")
            for n in range(YB):
                sp.wait_ge(S[f"first_stored{n}"], 16 * len(STAGES["first"][n::YB]))
            with sp.If(late):
                first_weights("late")
                stream_blocks("late")
                for n in range(YB):
                    sp.wait_ge(S[f"late_stored{n}"], 16 * len(STAGES["late"][n::YB]))
            for g in range(GROUPS):
                whole = [t for t in group_tiles(g) if (t + 1) * ROWS <= TOKENS]
                for k in range(2):
                    at = k * TOKENS + whole[0] * ROWS
                    load(yg[:, k, whole[0]:whole[-1] + 1, :],
                         ys_dram[at:at + len(whole) * ROWS, :].rearrange("(t p) n -> p t n", p=ROWS), f"tokens_back{g}")
                    if len(whole) < GROUP:
                        rows = TOKENS - (whole[-1] + 1) * ROWS
                        load(yg[0:rows, k, whole[-1] + 1, :], ys_dram[(k + 1) * TOKENS - rows:(k + 1) * TOKENS, :],
                             f"tokens_back{g}")
            for c in range(2):
                load(w13_sb[:, c], w13.rearrange("e (c p) n -> c p e n", p=KH)[c], "w_ff1_loaded")
            load(w2_sb[:], w2.rearrange("e p n -> p e n"), "w_ff1_loaded")
            for t in range(TILES):
                rows = min(ROWS, TOKENS - t * ROWS)
                sp.wait_ge(S["ff_added"], GROUPS * (EXPERTS1 + 1) - (GROUPS - 1 - t // GROUP))
                sp.dma_start(out[t * ROWS:t * ROWS + rows, :], h[3][0:rows, t, :]).then_inc(S["stored"], 16)
            sp.wait_ge(S["stored"], 16 * TILES)

        @block.gpsimd
        def _(pool):
            def power(norm, g):
                pool.wait_ge(S["norm_var"], nth(norm, g))
                nc.gpsimd.tensor_tensor(rstd[:, norm, gt(g)], ve[:, norm, gt(g)], half_neg[:, gt(g)],
                                        ALU.pow).then_inc(S["norm_rstd"], 1)

            nc.gpsimd.memset(v1_wide[:, TILES * E:], 0.0).then_inc(S["v1_edge"], 1)
            nc.gpsimd.memset(ones_bf[:], 1.0)
            nc.gpsimd.memset(hot_bf[:, TILES, :], 0.0)
            nc.gpsimd.memset(half_neg[:], -0.5)
            nc.gpsimd.memset(ones[:], 1.0).then_inc(S["pool_consts"], 1)
            pool.wait_ge(S["pool_consts"], 1)
            power(LN_PATCH, 0)
            power(LN_PATCH, 1)
            pool.wait_ge(S["rows_loaded"], 48)
            pool.wait_ge(S["consts_loaded"], 16)
            patch_row = const("is_patch", ROWS)
            nc.gpsimd.tensor_tensor(gm_rows[:], re_sb[:, 1, :], patch_row.to_broadcast([ROWS, E]), ALU.mult)
            nc.gpsimd.tensor_tensor(add_rows[:], re_sb[:, 2, :], patch_row.to_broadcast([ROWS, E]),
                                    ALU.mult).then_inc(S["embed_rows"], 1)
            pool.wait_ge(S["embed_rows"], 1)
            nc.gpsimd.tensor_tensor(add_rows[:], add_rows[:], pos_sb[:], ALU.add).then_inc(S["embed_rows"], 1)
            pool.wait_ge(S["embed_rows"], 2)
            nc.gpsimd.tensor_tensor(add_rows[:], add_rows[:], cls_sb[:], ALU.add).then_inc(S["embed_rows"], 1)
            nc.gpsimd.tensor_copy(causal_bf[:], const("causal", ROWS))
            nc.gpsimd.tensor_copy(block_bf[:], const("block", ROWS))
            nc.gpsimd.tensor_copy(before_bf[:], const("before"))
            nc.gpsimd.tensor_copy(ident_bf[:], ident).then_inc(S["masks_made"], 1)
            for g in range(GROUPS):
                power(LN_EMBED, g)
                power(LN_H0, g)
            for g in range(GROUPS):
                pool.wait_ge(S["h0_ready"], g + 1)
                nc.gpsimd.tensor_tensor(h[1][:, gt(g), :], h[0][:, gt(g), :], on_tiles(re_sb[:, 4, :]),
                                        ALU.add).then_inc(S["h0_shifted"], 1)
            for norm in (LN_DECAY, RMS_GQA, LN_H1):
                power(norm, 0)
            cos = const("cos").rearrange("p (a s) -> p a s", a=2)
            for g in range(GROUPS):
                for u in range(4):
                    if g == 0 and u < 3:
                        power((LN_DECAY, RMS_GQA, LN_H1)[u], 1)
                    n = 4 * g + u
                    pool.wait_ge(S["qk2_raw"], n + 1)
                    if n >= 2:
                        pool.wait_ge(S["qk2_rotated"], n - 1)
                    for b in range(2):
                        last = nc.gpsimd.tensor_tensor(
                            rcos[:, n % 2, b, :].rearrange("p (i s) -> p i s", s=SEQ),
                            raw[:, n % 2, b, :].rearrange("p (i s) -> p i s", s=SEQ),
                            cos[:, u // 3, :].unsqueeze(1).to_broadcast([128, COLS // SEQ, SEQ]), ALU.mult)
                    last.then_inc(S["qk2_cos"], 1)
            for g in range(GROUPS):
                power(RMS_MOE, g)
            for g in range(GROUPS):
                nc.gpsimd.tensor_tensor(h[2][:, gt(g), :], h[1][:, gt(g), :], hh[:, gt(g), :],
                                        ALU.add).then_inc(S["h2_base"], 1)

            def route_blocks(when):
                blocks = STAGES[when]

                def gather(n):
                    if n < len(blocks):
                        if n >= XB:
                            pool.wait_ge(S[f"{when}_turned"], n - XB + 1)
                        nc.gpsimd.indirect_dma_start(
                            xb[:, n % XB, :], None, xs_dram,
                            bass.IndirectOffsetOnAxis(ap=source_u[:, blocks[n]:blocks[n] + 1], axis=0)).then_inc(
                                S[f"{when}_in{n % XB}"], 16)

                for n in range(XB):
                    gather(n)
                for n in range(len(blocks)):
                    gather(n + XB)
                    pool.wait_ge(S[f"{when}_out"], n + 1)
                    nc.gpsimd.indirect_dma_start(
                        ys_dram, bass.IndirectOffsetOnAxis(ap=dest_u[:, blocks[n]:blocks[n] + 1], axis=0),
                        yb[:, n % YB, :], None).then_inc(S[f"{when}_stored{n % YB}"], 16)

            pool.wait_ge(S["rows_out"], 16 * TILES)
            pool.wait_ge(S["slots_ready"], 1)
            late = late_needed(pool)
            route_blocks("first")
            with pool.If(late):
                route_blocks("late")
            for g in range(GROUPS):
                power(RMS_TERN, g)
            for norm in (RMS_PROJ, LN_H3):
                for g in range(GROUPS):
                    power(norm, g)

        @block.scalar
        def _(act):
            fn = nc.scalar.activation

            act.wait_ge(S["ln1_loaded"], 16)
            for g in range(GROUPS):
                for u in range(PCH // 2):
                    act.wait_ge(S["patch_turned"], 3 * g + u + 1)
                    for b in ((1,) if g == 0 else (0, 1)):
                        c = 2 * u + b
                        fn(patch_t[:, c, gcols(g)], slot_of[("patch_t", g, u)][:, b, 0:COLS], ACT.Identity,
                           scale=ln1_sb[:, 0, c:c + 1], bias=ln1_sb[:, 1, c:c + 1]).then_inc(S["patch_t_act"], 1)

            act.wait_ge(S["consts_loaded"], 16)
            act.wait_ge(S["slopes_loaded"], 16)
            for hd in range(HEADS):
                last = fn(decay[:, hd % 4, hd // 4, :], const("ahead", ROWS), ACT.Exp, scale=slope_sb[:, hd:hd + 1])
            last.then_inc(S["decay_exp"], 1)

            def columns(key, turned, n, g, dst, ready):
                act.wait_ge(S[turned], n)
                fn(dst[:, :, gcols(g)], slot_of[key][0:KH, :, 0:COLS], ACT.Copy).then_inc(S[ready], 1)

            for g in range(GROUPS):
                columns(("x0_t", g), "x_turned", g + 1, g, x_t, "x_t_ready")
                for m in range(3):
                    act.wait_ge(S["qk1_done"], 3 * g + m + 1)
                    fn(qk1[:, :, m, gcols(g)], slot_of[("qk1", g, m)][:, :, 0:COLS], ACT.Silu).then_inc(S["qk1_silu"], 1)
                act.wait_ge(S["v1_done"], g + 1)
                fn(v1[:, gt(g), :], by_tile(slot_of[("v1", g)]), ACT.Silu).then_inc(S["v1_silu"], 1)
                act.wait_ge(S["g1_done"], g + 1)
                fn(g1_t[:, gcols(g)], slot_of[("g1", g)][0:KH, 0, 0:COLS], ACT.Copy).then_inc(S["g1_copied"], 1)
                for u, parts in enumerate((slice(0, 2), slice(2, 3))):
                    act.wait_ge(S["gate1_done"], 2 * g + u + 1)
                    fn(gate1[:, parts, gcols(g)], slot_of[("gate1", g, u)][:, 0:2 - u, 0:COLS], ACT.Tanh,
                       scale=0.5).then_inc(S["gate1_tanh"], 1)

            act.wait_ge(S["norm_cols_loaded"], 16)
            for g in range(GROUPS):
                act.wait_ge(S["x_turned"], 2 + g + 1)
                for c in range(2):
                    last = fn(x_t[:, c, gcols(g)], slot_of[("x1_t", g)][0:KH, c, 0:COLS], ACT.Copy,
                              scale=ncol_sb[:, c, 0:1])
                last.then_inc(S["x_t_ready"], 1)
                for u in range(4):
                    n = 4 * g + u
                    act.wait_ge(S["qk2_done"], n + 1)
                    if n >= 2:
                        act.wait_ge(S["qk2_swapped"], n - 1)
                        act.wait_ge(S["qk2_cos"], n - 1)
                    fn(raw[:, n % 2], slot_of[("qk2", g, u)][:, :, 0:COLS], ACT.Copy).then_inc(S["qk2_raw"], 1)
                act.wait_ge(S["v2_done"], g + 1)
                src = by_tile(slot_of[("v2", g)])
                for i, t in enumerate(group_tiles(g)):
                    last = fn(v2[:, t, :, :], src[:, i, :].rearrange("p (k d) -> p k d", k=KV), ACT.Copy)
                last.then_inc(S["v2_copied"], 1)

            def exps(n, unit, heads, src):
                act.wait_ge(S["nmax_ready"], 2 * n + unit + 1)
                if n >= PB:
                    act.wait_ge(S["probs_turned"], 2 * (n - PB + 1))
                for i in range(heads):
                    at = 8 * unit + i
                    last = fn(p_buf[:, (TILES + n) % PB, at, :], src(i), ACT.Exp, bias=nmax[:, n, at:at + 1],
                              accum_out=rsum[:, n, at:at + 1])
                last.then_inc(S["probs"], 1)

            def turned_probs(n):
                act.wait_ge(S["probs_turned"], 2 * n + 2)
                if n >= PB:
                    act.wait_ge(S["attended"], n - PB + 1)
                fn(pt_buf[:, n % PB, 8:12, :], slot_of[("probs_t", n, 1)][0:ROWS, 0, 0:4 * ROWS].rearrange(
                    "p (i x) -> p i x", x=ROWS), ACT.Copy).then_inc(S["probs_t_act"], 1)

            def columns2(t):
                act.wait_ge(S["attended"], t + 1)
                for b, c in enumerate((slice(0, 4), slice(4, 6))):
                    heads = 4 - 2 * b
                    last = fn(o2_t[:, c, tile_cols(t)], slot_of[("attend2", t)][:, b, 0:heads * ROWS].rearrange(
                        "p (i n) -> p i n", n=ROWS), ACT.Copy)
                last.then_inc(S["o2_t_ready"], 1)

            for t in range(TILES):
                s0, s1 = slot_of[("score2", t, 0)], slot_of[("score2", t, 1)]
                exps(t, 0, 8, lambda i: s0[0:ROWS, i // 4, (i % 4) * ROWS:(i % 4 + 1) * ROWS])
                exps(t, 1, 4, lambda i: s1[0:ROWS, i // 2, (i % 2) * ROWS:(i % 2 + 1) * ROWS])
                if t >= 1:
                    turned_probs(t - 1)
                if t >= 2:
                    columns2(t - 2)
            turned_probs(TILES - 1)
            columns2(TILES - 2)
            columns2(TILES - 1)

            for g in range(GROUPS):
                act.wait_ge(S["x_turned"], 4 + g + 1)
                for c in range(2):
                    last = fn(m_t[:, c, gcols(g)], slot_of[("m_t", g)][0:KH, c, 0:COLS], ACT.Copy,
                              scale=ncol_sb[:, c, 1:2])
                last.then_inc(S["m_t_ready"], 1)
            act.wait_ge(S["top0_ready"], 1)
            fn(pair_w[:, 1, :], rt[0][:, :, 0], ACT.Exp).then_inc(S["router_exp"], 1)

            def run_blocks(when):
                blocks = STAGES[when]

                def block_columns(n):
                    act.wait_ge(S[f"{when}_turned"], n + 1)
                    if n >= 2:
                        act.wait_ge(S[f"{when}_up"], 2 * (n - 1))
                    for c in range(2):
                        last = fn(xb_t[:, n % 2, c, :], slot_of[(when, "turned", n)][0:KH, 0, c * BLOCK:(c + 1) * BLOCK],
                                  ACT.Copy, scale=ncol_sb[:, c, 1:2])
                    last.then_inc(S[f"{when}_columns"], 1)

                block_columns(0)
                for n in range(len(blocks)):
                    if n + 1 < len(blocks):
                        block_columns(n + 1)
                    act.wait_ge(S[f"{when}_up"], 2 * n + 1)
                    if n >= 2:
                        act.wait_ge(S[f"{when}_hidden"], n - 1)
                    fn(sb_silu[:, n % 2, :], slot_of[(when, "up", n)][:, 0, 0:3 * BLOCK],
                       ACT.Silu).then_inc(S[f"{when}_silu"], 1)

            act.wait_ge(S["slots_ready"], 1)
            late = late_needed(act)
            run_blocks("first")
            with act.If(late):
                run_blocks("late")

            def silu(n):
                act.wait_ge(S["ff_up"], 2 * n + 1)
                if n >= 2:
                    act.wait_ge(S["ff_hidden"], n - 1)
                for g in range(GROUPS):
                    last = fn(silu_buf[:, n % 2, gcols(g, live_cols(g))], slot_of[("ff", n, 0)][:, g, 0:live_cols(g)],
                              ACT.Silu)
                last.then_inc(S["ff_silu"], 1)

            def int_columns(n, g):
                act.wait_ge(S["ints_turned"], n + 1)
                view = slot_of[("ints_t", n)][:].bitcast(BF16)
                for c in range(2):
                    last = fn(q_int_t[:, c, gcols(g)].rearrange("p (i x) -> p i x", x=ROWS),
                              view[0:KH, c, 0:3 * 112].rearrange("p (i x) -> p i x", x=112)[:, :, 0:ROWS], ACT.Copy)
                last.then_inc(S["ints_t_ready"], 1)

            def scales_and_queries(g):
                int_columns(g, g)
                act.wait_ge(S["dq_done"], 3 * g + 3)
                fn(dq[:, gcols(g)], slot_of[("dq", g)][:, 0, 0:COLS], ACT.Copy).then_inc(S["dq_ready"], 1)
                for m in range(3):
                    act.wait_ge(S["qk3_done"], 3 * g + m + 1)
                    fn(qk3[:, 0, m, gcols(g)], slot_of[("qk3", g, m)][:, 0, 0:COLS], ACT.Copy).then_inc(S["q3_copied"], 1)

            def columns3(t):
                act.wait_ge(S["attended"], TILES + t + 1)
                if t >= 2:
                    act.wait_ge(S["o3_turned"], t - 1)
                fn(o3_c[:, t % 2, :], slot_of[("attend3", t)][:, 0, 0:COLS], ACT.Copy).then_inc(S["o3_columns"], 1)

            for g in range(GROUPS):
                scales_and_queries(g)
            for t in range(TILES):
                n = TILES + t
                for jp in range(2):
                    act.wait_ge(S["below_max"], 2 * t + jp + 1)
                    p = p_buf[:, (TILES + n) % PB, 6 * jp:6 * jp + 6, :]
                    fn(p, p, ACT.Exp, scale=q_scale[:, t:t + 1]).then_inc(S["probs"], 1)
                if t >= 1:
                    turned_probs(TILES + t - 1)
                if t >= 2:
                    columns3(t - 2)
            turned_probs(2 * TILES - 1)
            columns3(TILES - 2)
            columns3(TILES - 1)
            for g in range(GROUPS):
                int_columns(2 + g, g)
            for g in range(GROUPS):
                columns(("x4_t", g), "x_turned", 6 + g + 1, g, x_t, "x_t_ready")
            silu(0)
            for g in range(GROUPS):
                act.wait_ge(S["logits1_done"], g + 1)
                fn(lg[:, gt(g), 0:EXPERTS1], by_tile(slot_of[("logits1", g)], EXPERTS1),
                   ACT.Sigmoid).then_inc(S["logits1_sigmoid"], 1)
            for n in range(1, EXPERTS1 + 1):
                silu(n)

        @block.vector
        def _(dve):
            v = nc.vector
            link = {"n": 0}

            def after(ins):
                link["n"] += 1
                ins.then_inc(S["dve_step"], 1)
                dve.wait_ge(S["dve_step"], link["n"])

            def statistics(norm, g, src, square=False, pieces=1, rms=None, plain=True, begun=0):
                width = src.shape[2] // pieces
                for i, t in enumerate(group_tiles(g)):
                    if i < begun:
                        continue
                    for p in range(pieces):
                        last = v.bn_stats(stats[:, t, p, :], src[:, i, p * width:(p + 1) * width])
                after(last)
                for t in group_tiles(g):
                    last = v.bn_aggr(mv[:, norm, t, :], stats[:, t, 0:pieces, :].rearrange("p a b -> p (a b)"))
                after(last)
                if square:
                    after(v.tensor_tensor(vt[:, norm, gt(g)], mv[:, norm, gt(g), 0], mv[:, norm, gt(g), 0], ALU.mult))
                    v.scalar_tensor_tensor(ve[:, norm, gt(g)], vt[:, norm, gt(g)], EPS[norm], mv[:, norm, gt(g), 1],
                                           ALU.add, ALU.add).then_inc(S["norm_var"], 1)
                if rms is not None:
                    v.tensor_scalar(ve[:, rms, gt(g)], mv[:, norm, gt(g), 1], 1.0 + EPS[rms], EPS[norm] * EPS[rms],
                                    ALU.mult, ALU.add).then_inc(S["norm_var"], 1)
                if not square and plain:
                    v.tensor_scalar(ve[:, norm, gt(g)], mv[:, norm, gt(g), 1], EPS[norm], None,
                                    ALU.add).then_inc(S["norm_var"], 1)

            def normalise(norm, g, dst, src, centre=True, rms=None):
                scale = norm if rms is None else rms
                dve.wait_ge(S["norm_rstd"], nth(scale, g))
                for i, t in enumerate(group_tiles(g)):
                    r = rstd[:, scale, t:t + 1]
                    if centre:
                        last = v.tensor_scalar(dst[:, i, :], src[:, i, :], mv[:, norm, t, 0:1], r, ALU.subtract, ALU.mult)
                    else:
                        last = v.tensor_scalar(dst[:, i, :], src[:, i, :], r, None, ALU.mult)
                return last

            dve.wait_ge(S["patch_loaded0"], 16 * GROUP)
            statistics(LN_PATCH, 0, patch_x[:, gt(0), :], pieces=2)
            dve.wait_ge(S["patch_loaded1"], 16 * GROUP)
            for p in range(2):
                v.bn_stats(stats[:, GROUP, p, :], patch_x[:, GROUP, p * PD // 2:(p + 1) * PD // 2])
            normalise(LN_PATCH, 0, patch_x[:, gt(0), :], patch_x[:, gt(0), :]).then_inc(S["patch_normed"], 1)
            statistics(LN_PATCH, 1, patch_x[:, gt(1), :], pieces=2, begun=1)
            normalise(LN_PATCH, 1, patch_x[:, gt(1), :], patch_x[:, gt(1), :]).then_inc(S["patch_normed"], 1)
            dve.wait_ge(S["ln1_loaded"], 16)
            for u in range(PCH // 2):
                c = 2 * u
                dve.wait_ge(S["patch_turned"], u + 1)
                v.tensor_scalar(patch_t[:, c, gcols(0)], slot_of[("patch_t", 0, u)][:, 0, 0:COLS],
                                ln1_sb[:, 0, c:c + 1], ln1_sb[:, 1, c:c + 1], ALU.mult,
                                ALU.add).then_inc(S["patch_t_dve"], 1)
            dve.wait_ge(S["rows_loaded"], 48)
            for g in range(GROUPS):
                dve.wait_ge(S["embed_done"], g + 1)
                v.tensor_tensor(y0[:, gt(g), :], by_tile(slot_of[("embed", g)]), on_tiles(re_sb[:, 0, :]),
                                ALU.add).then_inc(S["embed_biased"], 1)
                dve.wait_ge(S["embed_biased"], g + 1)
                statistics(LN_EMBED, g, y0[:, gt(g), :])
                dve.wait_ge(S["embed_rows"], 3)
                after(normalise(LN_EMBED, g, z0[:, gt(g), :], y0[:, gt(g), :]))
                after(v.tensor_tensor(z0[:, gt(g), :], z0[:, gt(g), :], on_tiles(gm_rows[:]), ALU.mult))
                v.tensor_tensor(h[0][:, gt(g), :], z0[:, gt(g), :], on_tiles(add_rows[:]),
                                ALU.add).then_inc(S["h0_ready"], 1)
                dve.wait_ge(S["h0_ready"], g + 1)
                statistics(LN_H0, g, h[0][:, gt(g), :])
                normalise(LN_H0, g, xn[:, gt(g), :], h[0][:, gt(g), :]).then_inc(S["x_normed"], 1)
            dve.wait_ge(S["decay_exp"], 1)
            keep = const("keep", ROWS)
            flat = decay[:].rearrange("p j m n -> p (j m) n")
            v.tensor_tensor(flat, flat, on_tiles(keep, HEADS), ALU.mult).then_inc(S["decay_ready"], 1)

            dve.wait_ge(S["decay_ready"], 1)

            def gated(t):
                dve.wait_ge(S["decay_out_done"], t + 1)
                dve.wait_ge(S["gate1_tanh"], 2 * (t // GROUP) + 2)
                v.scalar_tensor_tensor(o1_c[:, :, tile_cols(t)], gate1[:, :, tile_cols(t)], 1.0,
                                       slot_of[("decay_out", t)][:, 0, 0:COLS].rearrange("p (m n) -> p m n", m=3),
                                       ALU.add, ALU.mult).then_inc(S["o1_gated"], 1)

            def decayed(t):
                for jp in range(2):
                    dve.wait_ge(S["energy_done"], 2 * t + jp + 1)
                    if t >= PB:
                        dve.wait_ge(S["decay_out_done"], t - PB + 1)
                    v.tensor_tensor(p_buf[:, t % PB, 6 * jp:6 * jp + 6, :].rearrange("p (b m) n -> p b (m n)", b=2),
                                    slot_of[("energy", t, jp)][0:ROWS, :, 0:COLS],
                                    decay[:, 2 * jp:2 * jp + 2].rearrange("p b m n -> p b (m n)"),
                                    ALU.mult).then_inc(S["energy_decayed"], 1)

            def decay_norm_statistics(g):
                dve.wait_ge(S["attn1_done"], g + 1)
                statistics(LN_DECAY, g, by_tile(slot_of[("attn1", g)]))

            def h1_and_statistics(g):
                last = normalise(LN_DECAY, g, z0[:, gt(g), :], by_tile(slot_of[("attn1", g)]))
                last.then_inc(S["attn1_normed"], 1)
                dve.wait_ge(S["attn1_normed"], g + 1)
                after(v.tensor_tensor(z0[:, gt(g), :], z0[:, gt(g), :], on_tiles(re_sb[:, 3, :]), ALU.mult))
                dve.wait_ge(S["h0_shifted"], g + 1)
                v.tensor_tensor(h[1][:, gt(g), :], h[1][:, gt(g), :], z0[:, gt(g), :], ALU.add).then_inc(S["h1_ready"], 1)
                dve.wait_ge(S["h1_ready"], g + 1)
                statistics(LN_H1, g, h[1][:, gt(g), :], rms=RMS_GQA)

            def gqa_rows(g):
                normalise(LN_H1, g, xn[:, gt(g), :], h[1][:, gt(g), :], rms=RMS_GQA).then_inc(S["x_normed"], 1)

            def x2_rows(g):
                normalise(LN_H1, g, x2[:, gt(g), :], h[1][:, gt(g), :]).then_inc(S["x2_ready"], 1)

            for t in range(TILES):
                if t == GROUP + 1:
                    decay_norm_statistics(0)
                decayed(t)
                if t == GROUP + 1:
                    h1_and_statistics(0)
                if t:
                    gated(t - 1)
                if t == GROUP + 1:
                    gqa_rows(0)
            gated(TILES - 1)
            x2_rows(0)

            sin = const("sin").rearrange("p (a s) -> p a s", a=2)

            def rotated(g, u):
                n = 4 * g + u
                dve.wait_ge(S["qk2_swapped"], n + 1)
                for b in range(2):
                    last = v.tensor_tensor(rsin[:, n % 2, b, :].rearrange("p (i s) -> p i s", s=SEQ),
                                           slot_of[("swap", g, u)][:, b, 0:COLS].rearrange("p (i s) -> p i s", s=SEQ),
                                           sin[:, u // 3, :].unsqueeze(1).to_broadcast([128, COLS // SEQ, SEQ]),
                                           ALU.mult)
                last.then_inc(S["qk2_sin"], 1)
                dve.wait_ge(S["qk2_sin"], n + 1)
                dve.wait_ge(S["qk2_cos"], n + 1)
                v.tensor_tensor(qk2[:, 2 * u:2 * u + 2, gcols(g)], rsin[:, n % 2], rcos[:, n % 2],
                                ALU.add).then_inc(S["qk2_rotated"], 1)

            decay_norm_statistics(1)
            rotated(0, 0)
            h1_and_statistics(1)
            rotated(0, 1)
            gqa_rows(1)
            rotated(0, 2)
            rotated(0, 3)
            x2_rows(1)
            for u in range(4):
                rotated(1, u)

            def negative_max(n, unit, src, per):
                dve.wait_ge(S["score_done"], 2 * n + unit + 1)
                at = (8 if n < TILES else 6) * unit
                dst = nmax[:, n % TILES, at:at + 2 * per].rearrange("p (b i) -> p b i", b=2)
                return v.tensor_reduce(dst, src, AX.X, ALU.max, negate=True)

            def turned_probs(n):
                dve.wait_ge(S["probs_turned"], 2 * n + 1)
                if n >= PB:
                    dve.wait_ge(S["attended"], n - PB + 1)
                v.tensor_copy(pt_buf[:, n % PB, 0:8, :].rearrange("p (b i) x -> p b (i x)", b=2),
                              slot_of[("probs_t", n, 0)][0:ROWS, :, 0:4 * ROWS]).then_inc(S["probs_t_dve"], 1)

            def scaled_probs(t, u):
                dve.wait_ge(S["probs"], 2 * t + u + 1)
                heads = slice(8 * u, 8 + 4 * u)
                after(v.reciprocal(rsum[:, t, heads], rsum[:, t, heads]))
                p = p_buf[:, t % PB, heads, :]
                v.tensor_tensor(p, p, along(rsum[:, t:t + 1, heads].rearrange("p t h -> p (t h)"), ROWS),
                                ALU.mult).then_inc(S["probs_scaled"], 1)

            for t in range(TILES):
                for u, per in enumerate((4, 2)):
                    src = slot_of[("score2", t, u)][0:ROWS, :, 0:per * ROWS].rearrange("p b (i x) -> p b i x", x=ROWS)
                    negative_max(t, u, src, per).then_inc(S["nmax_ready"], 1)
                scaled_probs(t, 0)
                if t >= 1:
                    turned_probs(t - 1)
                scaled_probs(t, 1)
            turned_probs(TILES - 1)
            for g in range(GROUPS):
                dve.wait_ge(S["attn2_done"], g + 1)
                v.tensor_tensor(hh[:, gt(g), :], by_tile(slot_of[("attn2", g)]), x2[:, gt(g), :],
                                ALU.add).then_inc(S["hh_ready"], 1)
                dve.wait_ge(S["hh_ready"], g + 1)
                statistics(RMS_MOE, g, hh[:, gt(g), :], square=True)
                normalise(RMS_MOE, g, xr[:, gt(g), 0:E], hh[:, gt(g), :], centre=False).then_inc(S["x_normed"], 1)

            for g in range(GROUPS):
                dve.wait_ge(S["logits0_done"], g + 1)
                v.tensor_copy(lg[:, gt(g), :], by_tile(slot_of[("logits0", g)], EXPERTS0)).then_inc(S["logits0_copied"], 1)
                dve.wait_ge(S["logits0_copied"], g + 1)
                for t in group_tiles(g):
                    last = v.max(top[:, t, :], lg[:, t, :])
                after(last)
                for t in group_tiles(g):
                    last = v.max_index(top_i[:, t, :], top[:, t, :], lg[:, t, :])
            after(last)
            after(v.tensor_copy(top_f[:], top_i[:, :, 0:2]))
            iota = on_tiles(const("iota", ROWS), TILES)
            dve.wait_ge(S["pool_consts"], 1)
            for k in range(2):
                last = v.tensor_tensor(hot[:, k], iota, along(top_f[:, :, k], EXPERTS0), ALU.is_equal)
            after(last)
            v.tensor_tensor(hot_bf[:, 0:TILES, :], hot[:, 0], hot[:, 1], ALU.add).then_inc(S["hot_ready"], 1)
            v.tensor_tensor(rt[0][:, :, 0:1], top[:, :, 1:2], top[:, :, 0:1], ALU.subtract).then_inc(S["top0_ready"], 1)

            dve.wait_ge(S["ranks_done"], 1)
            ranks = slot_of["ranks"]
            counts = ranks[0:ROWS, 0, TILES * EXPERTS0:(TILES + 1) * EXPERTS0]
            after(v.tensor_tensor(over[:], counts.unsqueeze(2).to_broadcast([ROWS, EXPERTS0, MORE]),
                                  const("steps", ROWS).unsqueeze(1).to_broadcast([ROWS, EXPERTS0, MORE]), ALU.is_gt))
            after(v.tensor_reduce(share[:, 0, :], over[:], AX.X, ALU.add))
            after(v.tensor_tensor_scan(share[:, 1, :], const("is_one", ROWS), share[:, 0, :], 0.0, ALU.mult, ALU.add))
            v.tensor_tensor(over_f[:], share[0:1, 1, :].unsqueeze(1).to_broadcast([1, OVERFLOW, EXPERTS0]),
                            const("block_no", 1).unsqueeze(2).to_broadcast([1, OVERFLOW, EXPERTS0]), ALU.is_le)
            after(v.tensor_tensor(share[:, 2, :], share[:, 1, :], share[:, 0, :], ALU.subtract))
            v.tensor_reduce(over_n[:], over_f[:], AX.X, ALU.add)
            after(v.scalar_tensor_tensor(share[:, 3, :], share[:, 2, :], float(BLOCK), const("over_slot", ROWS),
                                         ALU.mult, ALU.add))
            v.tensor_scalar(over_u[:], over_n[:], EXPERTS0 - 1.0, None, ALU.min)
            v.tensor_copy(used_u[:], share[0:1, 1, EXPERTS0 - 1:EXPERTS0])
            rank = ranks[0:ROWS, 0, 0:TILES * EXPERTS0].rearrange("p (t e) -> p t e", e=EXPERTS0)
            v.scalar_tensor_tensor(rt[2][:], rank, float(BLOCK), on_tiles(share[:, 3, :], TILES), ALU.is_ge, ALU.mult)
            last = v.tensor_tensor(rt[3][:], rank, on_tiles(const("own_slot", ROWS), TILES), ALU.add)
            last.then_inc(S["ranks_used"], 1)
            dve.wait_ge(S["ranks_used"], 1)
            after(v.tensor_tensor(rt[2][:], rt[2][:], rt[3][:], ALU.add))
            for k in range(2):
                last = v.tensor_tensor(hot[:, k], hot[:, k], rt[2][:], ALU.mult)
            after(last)
            after(v.tensor_reduce(slot_f[:].rearrange("p k t o -> p (k t) o"), hot[:].rearrange("p k t e -> p (k t) e"),
                                  AX.X, ALU.add))
            slot_12 = slot_f[:].rearrange("p k t o -> p (k t o)")
            after(v.tensor_scalar(slot_tile[:, 0, :], slot_12, (BLOCK - 1) / 2, 1.0 / BLOCK, ALU.subtract, ALU.mult))
            after(v.tensor_scalar(slot_tile[:, 0, :], slot_tile[:, 0, :], MAGIC, None, ALU.add))
            after(v.tensor_scalar(slot_tile[:, 1, :], slot_tile[:, 0, :], MAGIC, float(BLOCK), ALU.subtract, ALU.mult))
            v.tensor_tensor(slot_tile[:, 2, :], slot_12, slot_tile[:, 1, :], ALU.subtract)

            def spread(ap, n):
                return ap.unsqueeze(2).to_broadcast([ROWS, 2 * TILES, n])

            after(v.tensor_tensor(in_block[:], on_tiles(const("block_at", ROWS), 2 * TILES),
                                  spread(slot_tile[:, 1, :], BLOCKS), ALU.is_equal))
            v.tensor_tensor(at_position[:], on_tiles(const("position", ROWS), 2 * TILES),
                            spread(slot_tile[:, 2, :], BLOCK), ALU.is_equal)
            v.tensor_tensor(block_id[:, :, 0, :], in_block[:], spread(const("id_high", ROWS), BLOCKS), ALU.mult)
            v.tensor_tensor(block_id[:, :, 1, :], in_block[:], spread(const("id_low", ROWS), BLOCKS),
                            ALU.mult).then_inc(S["slots_found"], 1)
            dve.wait_ge(S["slot_ids_done"], 1)
            ids = slot_of["slot_ids"]
            after(v.tensor_copy(slot_tmp[:], ids[:, 0, BLOCKS:2 * BLOCKS]))
            after(v.tensor_tensor(slot_id[:], ids[:, 0, 0:BLOCKS], slot_tmp[:], ALU.add))
            v.tensor_scalar(slot_tmp[:], slot_id[:], TOKENS + 0.5, float(TOKENS), ALU.is_gt, ALU.mult)
            after(v.scalar_tensor_tensor(slot_blank[:], slot_id[:], 0.5, const("spare"), ALU.is_lt, ALU.mult))
            after(v.scalar_tensor_tensor(slot_tmp[:], slot_id[:], 1.0, slot_tmp[:], ALU.subtract, ALU.subtract))
            v.tensor_scalar(source_u[:], slot_tmp[:], 0.0, None, ALU.max)
            v.scalar_tensor_tensor(dest_u[:], slot_id[:], 1.0, slot_blank[:], ALU.subtract,
                                   ALU.add).then_inc(S["slots_ready"], 1)
            dve.wait_ge(S["router_exp"], 1)
            after(v.tensor_scalar(rden[:, :, 0], pair_w[:, 1, :], 1.0, None, ALU.add))
            after(v.reciprocal(pair_w[:, 0, :], rden[:, :, 0]))
            after(v.tensor_tensor(pair_w[:, 1, :], pair_w[:, 1, :], pair_w[:, 0, :], ALU.mult))

            dve.wait_ge(S["w_tern_loaded"], 16)
            dve.wait_ge(S["g_tern_loaded"], 16)
            for n, cols in enumerate((slice(0, 5 * E), slice(5 * E, 6 * E))):
                v.tensor_reduce(tern_abs[:, n:n + 1], wt_sb[:, :, cols], AX.XY, ALU.add,
                                apply_absolute_value=True).then_inc(S["tern_summed"], 1)
            dve.wait_ge(S["tern_sum_done"], 1)
            for n, count in enumerate((3 * E * E, E * E)):
                last = v.tensor_scalar(tern_mean[:, n:n + 1], slot_of["tern_sum"][:, 0, n:n + 1], 1.0 / count, 1e-5,
                                       ALU.mult, ALU.max)
            last.then_inc(S["tern_mean_ready"], 1)
            dve.wait_ge(S["tern_mean_ready"], 1)
            after(v.reciprocal(tern_scale[:], tern_mean[:]))
            for n, cols in enumerate((slice(0, 5 * E), slice(5 * E, 6 * E))):
                last = v.tensor_scalar(tern_f[:, :, cols], wt_sb[:, :, cols], tern_scale[0:KH, n:n + 1], MAGIC,
                                       ALU.mult, ALU.add)
            after(last)
            after(v.tensor_scalar(tern_f[:], tern_f[:], MAGIC, 1.0, ALU.subtract, ALU.min))
            v.tensor_scalar(tern[:], tern_f[:], -1.0, None, ALU.max).then_inc(S["tern_ready"], 1)

            def run_blocks(when):
                blocks = STAGES[when]

                for n in range(len(blocks) + 1):
                    if n < len(blocks):
                        dve.wait_ge(S[f"{when}_up"], 2 * n + 2)
                        dve.wait_ge(S[f"{when}_silu"], n + 1)
                        if n >= 2:
                            dve.wait_ge(S[f"{when}_down"], n - 1)
                        v.tensor_tensor(hid_t[:, n % 2].rearrange("p c n -> p (c n)"), sb_silu[:, n % 2, :],
                                        slot_of[(when, "up", n)][:, 1, 0:3 * BLOCK], ALU.mult).then_inc(S[f"{when}_hidden"], 1)
                    if n >= 1:
                        dve.wait_ge(S[f"{when}_down"], n)
                        if n > YB:
                            dve.wait_ge(S[f"{when}_stored{(n - 1) % YB}"], 16 * ((n - 1) // YB))
                        v.tensor_copy(yb[:, (n - 1) % YB, :], slot_of[(when, "down", n - 1)][:, 0, 0:E]).then_inc(
                            S[f"{when}_out"], 1)

            dve.wait_ge(S["slots_ready"], 1)
            late = late_needed(dve)
            run_blocks("first")
            with dve.If(late):
                for n in range(YB):
                    dve.wait_ge(S[f"first_stored{n}"], 16 * len(STAGES["first"][n::YB]))
                run_blocks("late")
            dve.wait_ge(S["h2_base"], 2)

            def hidden(n, buffer, piece):
                dve.wait_ge(S["ff_silu"], n + 1)
                dve.wait_ge(S["ff_up"], 2 * n + 2)
                for g in range(GROUPS):
                    cols = gcols(g, live_cols(g))
                    last = v.tensor_tensor(hid[:, buffer, piece, cols], silu_buf[:, n % 2, cols],
                                           slot_of[("ff", n, 1)][:, g, 0:live_cols(g)], ALU.mult)
                last.then_inc(S["ff_hidden"], 1)

            def add_expert(n, dst, weight):
                for g in range(GROUPS):
                    dve.wait_ge(S["ff_down"], GROUPS * n + g + 1)
                    for i, t in enumerate(group_tiles(g)):
                        rows = min(ROWS, TOKENS - t * ROWS)
                        last = v.scalar_tensor_tensor(dst[0:rows, t, :], by_tile(slot_of[("down", n, g)], rows=rows)[:, i, :],
                                                      weight(t, rows), dst[0:rows, t, :], ALU.mult, ALU.add)
                    last.then_inc(S["ff_added"], 1)

            def gained(g, norm, src, gain, centre):
                for i, t in enumerate(group_tiles(g)):
                    if centre:
                        last = v.scalar_tensor_tensor(qa[:, t, :], src[:, i, :], mv[:, norm, t, 0:1], gt_sb[:, gain, :],
                                                      ALU.subtract, ALU.mult)
                    else:
                        last = v.tensor_tensor(qa[:, t, :], src[:, i, :], gt_sb[:, gain, :], ALU.mult)
                after(last)
                return v.tensor_reduce(amax[:, gt(g), 0:1], qa[:, gt(g), :], AX.X, ALU.max, apply_absolute_value=True)

            def quantise(g, n, scale):
                k = n // 2
                after(v.tensor_tensor(amax[:, gt(g), 0], amax[:, gt(g), 0], scale, ALU.mult))
                after(v.tensor_scalar(amax[:, gt(g), 1:2], amax[:, gt(g), 0:1], 1e-5, 1.0 / 127.0, ALU.max, ALU.mult))
                after(v.reciprocal(amax[:, gt(g), 2:3], amax[:, gt(g), 1:2]))
                v.tensor_scalar(amax[:, gt(g), 3:4], amax[:, gt(g), 1:2], tern_mean[0:ROWS, k:k + 1], None, ALU.mult)
                after(v.tensor_tensor(amax[:, gt(g), 2], amax[:, gt(g), 2], scale, ALU.mult))
                for t in group_tiles(g):
                    last = v.tensor_scalar(qb[:, t, :], qa[:, t, :], amax[:, t, 2:3], 127.0, ALU.mult, ALU.min)
                after(last)
                after(v.tensor_scalar(qb[:, gt(g), :], qb[:, gt(g), :], -128.0, MAGIC, ALU.max, ALU.add))
                v.tensor_scalar(q_int[:, gt(g), :], qb[:, gt(g), :], MAGIC, None, ALU.subtract).then_inc(S["quantised"], 1)

            def h2_rows(g):
                dve.wait_ge(S[f"tokens_back{g}"], 32 if g == 0 else 64)
                for k in range(2):
                    for t in group_tiles(g):
                        rows = min(ROWS, TOKENS - t * ROWS)
                        last = v.scalar_tensor_tensor(h[2][0:rows, t, :], yg[0:rows, k, t, :], pair_w[0:rows, k, t:t + 1],
                                                      h[2][0:rows, t, :], ALU.mult, ALU.add)
                    after(last)
                statistics(LN_H2, g, h[2][:, gt(g), :], rms=RMS_TERN, plain=False)
                after(gained(g, LN_H2, h[2][:, gt(g), :], 0, centre=True))

            def quantised_rows(g):
                dve.wait_ge(S["norm_rstd"], nth(RMS_TERN, g))
                quantise(g, g, rstd[:, RMS_TERN, gt(g)])
                v.tensor_scalar(q_scale[:, gt(g)], amax[:, gt(g), 3], HD1 ** -0.5, None, ALU.mult)
                for t in group_tiles(g):
                    if t >= 2:
                        dve.wait_ge(S["dq_done"], t - 1)
                    v.tensor_scalar(diag[:, t % 2, :], ident[0:ROWS, 0:ROWS], amax[:, t, 3:4], None,
                                    ALU.mult).then_inc(S["diag_ready"], 1)

            def keys_and_values3(g):
                dve.wait_ge(S["dq_ready"], g + 1)
                for m in range(3):
                    dve.wait_ge(S["qk3_done"], 3 * g + m + 1)
                    v.tensor_tensor(qk3[:, 1, m, gcols(g)], slot_of[("qk3", g, m)][:, 1, 0:COLS], dq[:, gcols(g)],
                                    ALU.mult).then_inc(S["k3_scaled"], 1)
                dve.wait_ge(S["v3_done"], g + 1)
                src = by_tile(slot_of[("v3", g)])
                for i, t in enumerate(group_tiles(g)):
                    last = v.tensor_scalar(v3[:, t, :, 0:HD1], src[:, i, :].rearrange("p (k d) -> p k d", k=HEADS),
                                           amax[:, t, 3:4], None, ALU.mult)
                last.then_inc(S["v3_scaled"], 1)

            def below_max3(t):
                n = TILES + t
                if n >= PB:
                    dve.wait_ge(S["probs_turned"], 2 * (n - PB + 1))
                for jp in range(2):
                    src = slot_of[("score3", t, jp)][0:ROWS, :, 0:COLS].rearrange("p b (i x) -> p b i x", x=ROWS)
                    after(negative_max(n, jp, src, 3))
                    heads = slice(6 * jp, 6 * jp + 6)
                    v.tensor_tensor(p_buf[:, (TILES + n) % PB, heads, :].rearrange("p (b i) x -> p b i x", b=2), src,
                                    nmax[:, t, heads].rearrange("p (b i) -> p b i", b=2).unsqueeze(3).to_broadcast(
                                        [ROWS, 2, 3, ROWS]), ALU.add).then_inc(S["below_max"], 1)

            def scaled3(t):
                dve.wait_ge(S["o3_turned"], t + 1)
                src = slot_of[("o3_rows", t)][0:ROWS, 0, 0:384].rearrange("p (i d) -> p i d", d=32)
                after(v.reciprocal(rsum[:, t, :], src[:, :, HD1]))
                v.tensor_tensor(o3[:, t, :].rearrange("p (i d) -> p i d", d=HD1), src[:, :, 0:HD1],
                                along(rsum[:, t, :], HD1), ALU.mult).then_inc(S["o3_scaled"], 1)

            h2_rows(0)
            quantised_rows(0)
            v.memset(v3[:, :, :, HD1:HD1 + 1], 1.0)
            v.memset(v3_wide[:, TILES * HEADS * (HD1 + 1):], 0.0)
            h2_rows(1)
            keys_and_values3(0)
            quantised_rows(1)
            below_max3(0)
            keys_and_values3(1)
            for t in range(TILES):
                if t >= 1:
                    below_max3(t)
                if t >= 1:
                    turned_probs(TILES + t - 1)
                if t >= 3:
                    scaled3(t - 3)
            turned_probs(2 * TILES - 1)
            dve.wait_ge(S["o3_scaled"], 3)
            statistics(RMS_PROJ, 0, o3[:, gt(0), :], square=True)

            def quantised_projection(g):
                dve.wait_ge(S["norm_rstd"], nth(RMS_PROJ, g))
                quantise(g, 2 + g, rstd[:, RMS_PROJ, gt(g)])

            def h3_rows(g):
                dve.wait_ge(S["attn3_done"], g + 1)
                src = by_tile(slot_of[("attn3", g)])
                for i, t in enumerate(group_tiles(g)):
                    last = v.scalar_tensor_tensor(h[3][:, t, :], src[:, i, :], amax[:, t, 3:4], h[2][:, t, :],
                                                  ALU.mult, ALU.add)
                last.then_inc(S["h3_ready"], 1)
                dve.wait_ge(S["h3_ready"], g + 1)
                statistics(LN_H3, g, h[3][:, gt(g), :])

            scaled3(TILES - 3)
            after(gained(0, RMS_PROJ, o3[:, gt(0), :], 1, centre=False))
            scaled3(TILES - 2)
            scaled3(TILES - 1)
            quantised_projection(0)
            dve.wait_ge(S["o3_scaled"], TILES)
            statistics(RMS_PROJ, 1, o3[:, gt(1), :], square=True)
            after(gained(1, RMS_PROJ, o3[:, gt(1), :], 1, centre=False))
            quantised_projection(1)
            h3_rows(0)
            normalise(LN_H3, 0, xn[:, gt(0), :], h[3][:, gt(0), :]).then_inc(S["x_normed"], 1)
            h3_rows(1)
            normalise(LN_H3, 1, xn[:, gt(1), :], h[3][:, gt(1), :]).then_inc(S["x_normed"], 1)

            hidden(0, 0, 0)

            dve.wait_ge(S["w_ff1_loaded"], 80)
            dve.wait_ge(S["logits1_sigmoid"], 2)
            score = lg[:, :, 0:EXPERTS1]
            after(v.tensor_tensor(rt[0][:, :, 0:8], score, on_tiles(gb_sb[:], TILES), ALU.add))
            pairs = rt[0][:, :, 0:8].rearrange("p t (g e) -> p t g e", e=2)
            after(v.memset(rt[1][:], MASKED))
            after(v.tensor_tensor(rt[1][:, :, 0:4], pairs[:, :, :, 0], pairs[:, :, :, 1], ALU.add))

            def two_largest(values, width, hot):
                for t in range(TILES):
                    last = v.max(top[:, t, :], values[:, t, 0:8])
                after(last)
                for t in range(TILES):
                    last = v.max_index(top_i[:, t, :], top[:, t, :], values[:, t, 0:8])
                after(last)
                after(v.tensor_copy(top_f[:], top_i[:, :, 0:2]))
                numbers = on_tiles(const("iota", ROWS)[:, 0:width], TILES)
                v.tensor_tensor(hot, numbers, along(top_f[:, :, 0], width), ALU.is_equal)
                after(v.tensor_tensor(rt[3][:, :, 0:width], numbers, along(top_f[:, :, 1], width), ALU.is_equal))
                after(v.tensor_tensor(hot, hot, rt[3][:, :, 0:width], ALU.add))

            two_largest(rt[1][:], 4, rt[2][:, :, 0:4])
            in_group = rt[4][:, :, 0:8].rearrange("p t (g e) -> p t g e", e=2)
            v.tensor_copy(in_group[:, :, :, 0], rt[2][:, :, 0:4])
            after(v.tensor_copy(in_group[:, :, :, 1], rt[2][:, :, 0:4]))
            v.tensor_tensor(rt[1][:, :, 0:8], rt[0][:, :, 0:8], rt[4][:, :, 0:8], ALU.mult)
            after(v.tensor_scalar(rt[5][:, :, 0:8], rt[4][:, :, 0:8], -MASKED, MASKED, ALU.mult, ALU.add))
            after(v.tensor_tensor(rt[1][:, :, 0:8], rt[1][:, :, 0:8], rt[5][:, :, 0:8], ALU.add))
            two_largest(rt[1][:], 8, rt[2][:, :, 0:8])
            after(v.tensor_tensor(rt[4][:, :, 0:8], rt[2][:, :, 0:8], score, ALU.mult))
            after(v.tensor_reduce(rden[:, :, 0:1], rt[4][:, :, 0:8], AX.X, ALU.add))
            after(v.tensor_scalar(rden[:, :, 0:1], rden[:, :, 0:1], 1e-6, None, ALU.add))
            after(v.reciprocal(rden[:, :, 1:2], rden[:, :, 0:1]))
            after(v.tensor_tensor(comb1, rt[4][:, :, 0:8], along(rden[:, :, 1], 8), ALU.mult))
            for n in range(1, EXPERTS1 + 2):
                if n <= EXPERTS1:
                    hidden(n, n % 2, 0)
                if n == 1:
                    add_expert(0, h[3], lambda t, rows: 1.0)
                else:
                    dve.wait_ge(S["ff_added"], GROUPS * (n - 1))
                    add_expert(n - 1, h[3], lambda t, rows: comb1[0:rows, t, n - 2:n - 1])


def constants():
    c = np.zeros((128, CONST_WIDTH), np.float32)

    def put(name, value):
        at, width = CONST_AT[name]
        c[:value.shape[0], at:at + width] = value.reshape(value.shape[0], width)

    put("ident", np.eye(128))
    n = np.arange(128)
    put("swap", np.eye(128)[n ^ 1])
    r = np.arange(ROWS)
    same = r[:, None] // SEQ == r[None, :] // SEQ
    back = r[:, None] - r[None, :]
    put("causal", np.where(same & (back >= 0), 0.0, MASKED))
    put("block", np.where(same, 0.0, MASKED))
    put("ahead", np.where(same & (back <= 0), -back, 0))
    put("keep", 0.5 * (same & (back <= 0)))
    put("is_patch", (r % SEQ > 0).astype(np.float32)[:, None])
    put("before", np.triu(np.ones((128, 128)), 1))
    e = np.arange(EXPERTS0)
    put("is_one", np.ones((128, EXPERTS0)))
    put("own_slot", np.broadcast_to(BLOCK * e, (128, EXPERTS0)))
    put("over_slot", np.broadcast_to(BLOCK * (EXPERTS0 - 1 - e), (128, EXPERTS0)))
    put("steps", np.broadcast_to(BLOCK * (1 + np.arange(MORE)), (128, MORE)))
    put("block_no", np.broadcast_to(np.arange(OVERFLOW), (128, OVERFLOW)))
    put("position", np.broadcast_to(np.arange(BLOCK), (128, BLOCK)))
    put("block_at", np.broadcast_to(BLOCK * np.arange(BLOCKS), (128, BLOCKS)))
    ids = 1 + TOKENS * np.arange(2)[None, :, None] + ROWS * np.arange(TILES)[None, None, :] + n[:, None, None]
    ids = ids.reshape(128, 2 * TILES)
    put("id_high", ids // 8 * 8)
    put("id_low", ids % 8)
    put("spare", 1 + 2 * TOKENS + BLOCK * np.arange(BLOCKS)[None, :] + n[:, None])
    put("iota", np.broadcast_to(np.arange(EXPERTS0, dtype=np.float32), (128, EXPERTS0)))
    inverse = (1.0 / np.float32(10000.0) ** (np.arange(0, HD2, 2, dtype=np.float32) / np.float32(HD2))).astype(np.float32)
    angle = np.arange(SEQ, dtype=np.float32)[None, :] * inverse[(n % HD2) // 2][:, None]
    sign = np.where(n % 2 == 0, -1.0, 1.0)[:, None]
    share = np.array([HD2 ** -0.5, 1.0])[None, :, None]
    put("cos", np.cos(angle)[:, None, :] * share)
    put("sin", (sign * np.sin(angle))[:, None, :] * share)
    return c


_OUT = (IMAGES, SEQ, E)


def kernel(**inputs):
    import concourse.bacc as _bacc
    from concourse.bass_utils import run_bass_kernel_spmd as _run

    a = {k: np.asarray(x) for k, x in inputs.items()}
    x = a["x"].reshape(IMAGES, 3, 6, 16, 6, 16).transpose(0, 2, 4, 1, 3, 5).reshape(IMAGES, PATCHES, PD)
    patches = np.zeros((TILES * PER_TILE, SEQ, PD), np.float32)
    patches[:IMAGES, 1:] = x

    def channels_first(w):
        return w.reshape(16, 16, 3, -1).transpose(2, 0, 1, 3).reshape(PD, -1)

    ln1 = np.stack([channels_first(a["L0_tok_ln1_g"])[:, 0], channels_first(a["L0_tok_ln1_b"])[:, 0]])
    pos = a["L0_tok_pos_embed"][0]
    cls_rows = np.zeros((PER_TILE, SEQ, E), np.float32)
    cls_rows[:, 0] = a["L0_tok_cls_token"]

    def padded_heads(w):
        p = np.zeros((w.shape[0], HEADS, 32), np.float32)
        p[:, :, :HD1] = w.reshape(w.shape[0], HEADS, HD1)
        return p.reshape(w.shape[0], 3, 128)

    qkv2 = a["L0_ffn_w_qkv"].reshape(E, HEADS + 2 * KV, HD2)
    pair_heads = [(0, 4), (1, 5), (2, 6), (3, 7), (8, 9), (10, 11), (12, 13), (14, 14)]
    wqk2 = np.stack([np.concatenate([qkv2[:, p], qkv2[:, q]], axis=1) for p, q in pair_heads], axis=1)
    row_heads = [0, 4, 1, 5, 2, 6, 3, 7, 8, 9, 10, 11]
    qkv3 = a["L1_attn_w_qkv"].T
    arrays = {
        "consts": constants(),
        "patches": patches.reshape(TILES, ROWS, PD),
        "w_patch": channels_first(a["L0_tok_W"]),
        "ln1_gb": ln1.reshape(2, PCH, 128).transpose(2, 0, 1),
        "rows_e": np.stack([a["L0_tok_b"], a["L0_tok_ln2_g"], a["L0_tok_ln2_b"], a["L0_attn_ln_w"], a["L0_attn_ln_b"]]),
        "pos_rows": np.concatenate([pos] * PER_TILE),
        "cls_rows": cls_rows.reshape(ROWS, E),
        "slopes": a["L0_attn_log_slope"],
        "wqk1": np.stack([padded_heads(a["L0_attn_Wq"]), padded_heads(a["L0_attn_Wk"])], axis=1),
        "wv1": a["L0_attn_Wv"],
        "wo1": padded_heads(a["L0_attn_Wo"].T).transpose(2, 1, 0),
        "wg1": np.pad(a["L0_attn_Wg1"], ((0, 0), (0, KH - 16))).reshape(2, KH, KH).transpose(1, 0, 2),
        "wg2": np.pad(padded_heads(a["L0_attn_Wg2"]), ((0, KH - 16), (0, 0), (0, 0))),
        "norm_cols": np.stack([a["L0_ffn_norm1_w"], a["L0_ffn_norm2_w"]]).reshape(2, 2, KH).transpose(2, 1, 0),
        "wqk2": wqk2,
        "wv2": qkv2[:, HEADS + KV:].reshape(E, E),
        "wout2": a["L0_ffn_w_out"].reshape(HEADS, HD2, E)[row_heads].reshape(HEADS * HD2, E),
        "wrouter0": a["L0_ffn_w_router"],
        "w_gate_up": a["L0_ffn_w_gate_up"],
        "w_down": a["L0_ffn_w_down"],
        "w_tern": np.concatenate([padded_heads(qkv3[:, :E]).reshape(E, 384), padded_heads(qkv3[:, E:2 * E]).reshape(E, 384),
                                  qkv3[:, 2 * E:], a["L1_attn_w_proj"].T], axis=1),
        "g_tern": np.stack([a["L1_attn_g_qkv"], a["L1_attn_g_proj"]]),
        "w_gate1": a["L1_ffn_gate_weight"].T,
        "gate_bias": a["L1_ffn_gate_bias"],
        "w13": np.concatenate([np.concatenate([a["L1_ffn_w1"], a["L1_ffn_sw1"][None]]).transpose(0, 2, 1),
                               np.concatenate([a["L1_ffn_w3"], a["L1_ffn_sw3"][None]]).transpose(0, 2, 1)], axis=2),
        "w2": np.concatenate([a["L1_ffn_w2"], a["L1_ffn_sw2"][None]]).transpose(0, 2, 1),
    }
    nc = _bacc.Bacc("TRN2", target_bir_lowering=False, num_devices=1)
    args = []
    for name, value in arrays.items():
        arrays[name] = value = np.ascontiguousarray(value)
        args.append(nc.dram_tensor(name, value.shape, mybir.dt.from_np(value.dtype), kind="ExternalInput").ap())
    out = nc.dram_tensor("out", (TOKENS, E), F32, kind="ExternalOutput").ap()
    vit_tower(nc, *args, out)
    r = _run(nc, [arrays], core_ids=[0])
    return r.results[0]["out"].reshape(_OUT)
```
